# Optimizing a Trainium2 kernel written in Bass

```python
import numpy as np
import jax
import jax.numpy as jnp

def _softmax(x, axis=-1):
    return jax.nn.softmax(x, axis=axis)

def _gelu(x):
    return jax.nn.gelu(x, approximate=True)

def _silu(x):
    return jax.nn.silu(x)

def _sigmoid(x):
    return jax.nn.sigmoid(x)

def _layernorm(x, axis=-1, eps=1e-05):
    m = jnp.mean(x, axis=axis, keepdims=True)
    v = jnp.var(x, axis=axis, keepdims=True)
    return (x - m) / jnp.sqrt(v + eps)

def _scatter_add(tgt, idx, src, axis=0):
    return tgt.at[idx].add(src)

def _segment_sum(src, seg, n):
    return jax.ops.segment_sum(src, seg, n)
kernel_name = 'mk_decoder_preln_d2_seqx_r8_073938'

def setup_inputs(seed: int=0):
    np.random.seed(seed)
    _w = jnp.asarray

    def _rec_inputs():
        import jax
        import jax.numpy as jnp
        _rk = jax.random.key(seed)
        x = 7.22e-05 + 1 * jax.random.normal(jax.random.fold_in(_rk, 1), (16, 128, 256), jnp.float32)
        _lenS = 128 - jax.random.randint(jax.random.fold_in(_rk, 7), (16,), 0, max(1, 128 // 4) + 1, jnp.int32)
        _lenS2 = 128 - jax.random.randint(jax.random.fold_in(_rk, 8), (16,), 0, max(1, 128 // 4) + 1, jnp.int32)
        _ctx_2048P = jax.random.normal(jax.random.fold_in(_rk, 11), (16, 16, 256), jnp.float32)
        _ctx_2048c = jax.random.dirichlet(jax.random.fold_in(_rk, 511), 0.3 * jnp.ones((16,), jnp.float32), (16, 128))
        _ctx_2048t = jnp.einsum('bsk,bkd->bsd', _ctx_2048c, _ctx_2048P)
        _ctx_2048t = _ctx_2048t * jax.lax.rsqrt(jnp.mean(jnp.square(_ctx_2048t)) + 1e-12) * 0.953939
        ctx_2048 = 4.13588e-05 + 0.999923 * (_ctx_2048t + 0.3 * jax.random.normal(jax.random.fold_in(_rk, 611), (16, 128, 256), jnp.float32))
        return (x, ctx_2048)
    x, ctx_2048 = _rec_inputs()

    def _L0_attn_setup():
        import jax, jax.numpy as jnp
        import numpy as np
        H = 16
        SB_RATIO = 0.1
        RB_RATIO = 0.5
        ROPE_BASE = 10000.0

        def _rotate_half(x):
            hd = x.shape[-1]
            x1, x2 = (x[..., :hd // 2], x[..., hd // 2:])
            return jnp.concatenate([-x2, x1], axis=-1)
        key = jax.random.key(seed)
        ks = jax.random.split(key, 6)
        B, T, D = (1, 256, 256)
        s = 0.02
        return {'hidden_states': jax.random.normal(ks[0], (B, T, D), jnp.float32), 'wq': jax.random.normal(ks[1], (D, D), jnp.float32) * s, 'wk': jax.random.normal(ks[2], (D, D), jnp.float32) * s, 'wv': jax.random.normal(ks[3], (D, D), jnp.float32) * s, 'wo': jax.random.normal(ks[4], (D, D), jnp.float32) * s, 'bern_u': jax.random.uniform(ks[5], (B, H), jnp.float32)}
    _L0_attn_all = _L0_attn_setup()
    _L0_attn_in = {k: v for k, v in _L0_attn_all.items() if k in ('wq', 'wk', 'wv', 'wo', 'bern_u')}
    del _L0_attn_all

    def _L0_xattn_setup():
        import jax, jax.numpy as jnp
        import numpy as np
        N_HEAD = 8
        key = jax.random.key(seed)
        k1, k2, k3 = jax.random.split(key, 3)
        b, d, m = (4, 128, 256)
        c, n = (128, 256)
        q = jax.random.normal(k1, (b, d, m), dtype=jnp.float32)
        k = jax.random.normal(k2, (d // d * b, d, n), dtype=jnp.float32).reshape(b, d, n)
        v = jax.random.normal(k3, (b, c, n), dtype=jnp.float32)
        return {'q': q, 'k': k, 'v': v}
    _L0_xattn_all = _L0_xattn_setup()
    _L0_xattn_in = {k: v for k, v in _L0_xattn_all.items() if k in ()}
    del _L0_xattn_all

    def _L0_ffn_setup():
        import math
        import jax, jax.numpy as jnp
        import numpy as np
        from jax import lax
        D = 256
        I = 128
        E = 32
        K = 4
        NG = 8
        TKG = 3
        NSH = 2
        SCALE = 2.5
        CF = 1.25
        B, S = (2, 256)

        def _router(x, router_w, e_bias):
            scores = jax.nn.sigmoid(x @ router_w.T)
            sc = scores + e_bias[None, :]
            T = x.shape[0]
            gs = sc.reshape(T, NG, E // NG)
            group_scores = lax.top_k(gs, 2)[0].sum(-1)
            _, gidx = lax.top_k(group_scores, TKG)
            gmask = jnp.zeros((T, NG), sc.dtype).at[jnp.arange(T)[:, None], gidx].set(1.0)
            smask = jnp.repeat(gmask, E // NG, axis=1)
            masked = jnp.where(smask > 0, sc, 0.0)
            _, topk_idx = lax.top_k(masked, K)
            topk_w = jnp.take_along_axis(scores, topk_idx, axis=1)
            topk_w = topk_w / (topk_w.sum(-1, keepdims=True) + 1e-20)
            topk_w = topk_w * SCALE
            return (topk_idx.astype(jnp.int32), topk_w)

        def _moe_forward(hidden_states, router_w, e_bias, W_gate, W_up, W_down, shared_gate, shared_up, shared_down):
            b, s, d = hidden_states.shape
            T = b * s
            C = int(math.ceil(CF * T / E))
            EC = E * C
            x = hidden_states.reshape(T, d)
            topk_idx, topk_w = _router(x, router_w, e_bias)
            expert_flat = topk_idx.reshape(-1)
            w_flat = topk_w.reshape(-1)
            tok_flat = jnp.repeat(jnp.arange(T, dtype=jnp.int32), K)
            sort_ix = jnp.argsort(expert_flat)
            e_sorted = expert_flat[sort_ix]
            tok_s = tok_flat[sort_ix]
            w_s = w_flat[sort_ix]
            counts = jnp.zeros(E, jnp.int32).at[e_sorted].add(1)
            group_start = jnp.concatenate([jnp.zeros(1, jnp.int32), jnp.cumsum(counts)[:-1].astype(jnp.int32)])
            pos = jnp.arange(T * K, dtype=jnp.int32) - group_start[e_sorted]
            valid = pos < C
            dest = e_sorted * C + jnp.where(valid, pos, 0)
            slots_token = jnp.zeros(EC, jnp.int32).at[dest].add(jnp.where(valid, tok_s, 0))
            slots_w = jnp.zeros(EC, w_s.dtype).at[dest].add(jnp.where(valid, w_s, 0.0))
            Xp = x[slots_token].reshape(E, C, d)
            G = jnp.einsum('ecd,edi->eci', Xp, W_gate)
            U = jnp.einsum('ecd,edi->eci', Xp, W_up)
            Y = jnp.einsum('eci,eid->ecd', jax.nn.silu(G) * U, W_down)
            Yf = Y.reshape(EC, d) * slots_w[:, None]
            out = jnp.zeros((T, d), x.dtype).at[slots_token].add(Yf)
            shared = jax.nn.silu(x @ shared_gate.T) * (x @ shared_up.T) @ shared_down.T
            return (out + shared).reshape(b, s, d)
        key = jax.random.key(seed)
        ks = jax.random.split(key, 8)

        def rn(k, shape, scale=0.02):
            return jax.random.normal(k, shape, jnp.float32) * scale
        return {'hidden_states': jax.random.normal(ks[0], (B, S, D), jnp.float32), 'router_w': rn(ks[1], (E, D)), 'e_bias': jnp.zeros((E,), jnp.float32), 'W_gate': rn(ks[2], (E, D, I)), 'W_up': rn(ks[3], (E, D, I)), 'W_down': rn(ks[4], (E, I, D)), 'shared_gate': rn(ks[5], (I * NSH, D)), 'shared_up': rn(ks[6], (I * NSH, D)), 'shared_down': rn(ks[7], (D, I * NSH))}
    _L0_ffn_all = _L0_ffn_setup()
    _L0_ffn_in = {k: v for k, v in _L0_ffn_all.items() if k in ('router_w', 'e_bias', 'W_gate', 'W_up', 'W_down', 'shared_gate', 'shared_up', 'shared_down')}
    del _L0_ffn_all

    def _L1_attn_setup():
        import jax, jax.numpy as jnp
        import numpy as np
        D_ATTN = 256
        D_STATE = 64
        SHIFT_FRAC = 0.5
        LN_EPS = 1e-05

        def _reference_tuple_inner(x, W_key, W_value, W_output, W_shift, gate, time_decay, time_first, ln_gamma, ln_beta):
            B, T, D = x.shape
            shift_len = max(1, int(T * SHIFT_FRAC))
            x_cat = jnp.roll(x, -shift_len, axis=1)
            g = jax.nn.sigmoid(gate)
            x_shift = jnp.einsum('btd,ed->bte', x_cat, W_shift) * g + x * (1.0 - g)
            mu = jnp.mean(x_shift, axis=-1, keepdims=True)
            var = jnp.var(x_shift, axis=-1, keepdims=True)
            x_norm = (x_shift - mu) * jax.lax.rsqrt(var + LN_EPS) * ln_gamma + ln_beta
            k = jnp.einsum('btd,sd->bts', x_norm, W_key)
            v = jnp.einsum('btd,sd->bts', x_norm, W_value)
            w = jnp.exp(time_decay)
            u = jnp.exp(time_first)
            wkv = jnp.exp(-u * jax.nn.sigmoid(k)) * v

            def step(state, wkv_t):
                state = state * w + wkv_t
                return (state, state)
            init = jnp.zeros((B, k.shape[-1]), x.dtype)
            last_state, states = jax.lax.scan(step, init, jnp.swapaxes(wkv, 0, 1))
            states = jnp.swapaxes(states, 0, 1)
            output = jnp.einsum('bts,ds->btd', states, W_output)
            return (output, jax.lax.stop_gradient(last_state))
        key = jax.random.key(seed)
        ks = jax.random.split(key, 8)
        B, T = (8, 256)
        s_attn = 1.0 / np.sqrt(D_ATTN)
        s_state = 1.0 / np.sqrt(D_STATE)
        x = jax.random.normal(ks[0], (B, T, D_ATTN), jnp.float32)
        W_key = jax.random.normal(ks[1], (D_STATE, D_ATTN), jnp.float32) * s_attn
        W_value = jax.random.normal(ks[2], (D_STATE, D_ATTN), jnp.float32) * s_attn
        W_output = jax.random.normal(ks[3], (D_ATTN, D_STATE), jnp.float32) * s_state
        W_shift = jax.random.normal(ks[4], (D_ATTN, D_ATTN), jnp.float32) * s_attn
        gate = jnp.ones((D_ATTN,), jnp.float32)
        time_decay = -jax.random.uniform(ks[5], (D_STATE,), jnp.float32, 0.05, 1.0)
        time_first = jax.random.normal(ks[6], (D_STATE,), jnp.float32) * 0.1
        ln_gamma = jnp.ones((D_ATTN,), jnp.float32)
        ln_beta = jnp.zeros((D_ATTN,), jnp.float32)
        return dict(x=x, W_key=W_key, W_value=W_value, W_output=W_output, W_shift=W_shift, gate=gate, time_decay=time_decay, time_first=time_first, ln_gamma=ln_gamma, ln_beta=ln_beta)
    _L1_attn_all = _L1_attn_setup()
    _L1_attn_in = {k: v for k, v in _L1_attn_all.items() if k in ('W_key', 'W_value', 'W_output', 'W_shift', 'gate', 'time_decay', 'time_first', 'ln_gamma', 'ln_beta')}
    del _L1_attn_all

    def _L1_xattn_setup():
        import jax, jax.numpy as jnp
        import numpy as np
        N_HEAD = 8
        ALPHA = 5.0
        EPS = 1e-12

        def _l2norm(x, axis):
            n = jnp.sqrt(jnp.sum(x * x, axis=axis, keepdims=True))
            return x / jnp.maximum(n, EPS)
        key = jax.random.key(seed)
        kq, kk, kv = jax.random.split(key, 3)
        B, D, T = (4, 128, 256)
        q = jax.random.normal(kq, (B, D, T), dtype=jnp.float32)
        k = jax.random.normal(kk, (B, D, T), dtype=jnp.float32)
        v = jax.random.normal(kv, (B, D, T), dtype=jnp.float32)
        return {'q': q, 'k': k, 'v': v}
    _L1_xattn_all = _L1_xattn_setup()
    _L1_xattn_in = {k: v for k, v in _L1_xattn_all.items() if k in ()}
    del _L1_xattn_all

    def _L1_ffn_setup():
        import jax, jax.numpy as jnp
        import numpy as np
        B, S, D, I, E, K = (4, 128, 256, 128, 8, 2)
        key = jax.random.key(seed)
        ks = jax.random.split(key, 7)

        def w(k, shape, fan_in):
            return jax.random.normal(k, shape, dtype=jnp.float32) * fan_in ** (-0.5)
        return {'hidden_states': jax.random.normal(ks[0], (B, S, D), dtype=jnp.float32), 'router_w': w(ks[1], (D, E), D), 'gate_up_w': w(ks[2], (E, D, 2 * I), D), 'down_w': w(ks[3], (E, I, D), I), 'shared_gate_w': w(ks[4], (D, I), D), 'shared_up_w': w(ks[5], (D, I), D), 'shared_down_w': w(ks[6], (I, D), I)}
    _L1_ffn_all = _L1_ffn_setup()
    _L1_ffn_in = {k: v for k, v in _L1_ffn_all.items() if k in ('router_w', 'gate_up_w', 'down_w', 'shared_gate_w', 'shared_up_w', 'shared_down_w')}
    del _L1_ffn_all
    return {'x': x, 'ctx_2048': ctx_2048, 'L0_attn_wq': _L0_attn_in['wq'], 'L0_attn_wk': _L0_attn_in['wk'], 'L0_attn_wv': _L0_attn_in['wv'], 'L0_attn_wo': _L0_attn_in['wo'], 'L0_attn_bern_u': _L0_attn_in['bern_u'], 'L0_ffn_router_w': _L0_ffn_in['router_w'], 'L0_ffn_e_bias': _L0_ffn_in['e_bias'], 'L0_ffn_W_gate': _L0_ffn_in['W_gate'], 'L0_ffn_W_up': _L0_ffn_in['W_up'], 'L0_ffn_W_down': _L0_ffn_in['W_down'], 'L0_ffn_shared_gate': _L0_ffn_in['shared_gate'], 'L0_ffn_shared_up': _L0_ffn_in['shared_up'], 'L0_ffn_shared_down': _L0_ffn_in['shared_down'], 'L1_attn_W_key': _L1_attn_in['W_key'], 'L1_attn_W_value': _L1_attn_in['W_value'], 'L1_attn_W_output': _L1_attn_in['W_output'], 'L1_attn_W_shift': _L1_attn_in['W_shift'], 'L1_attn_gate': _L1_attn_in['gate'], 'L1_attn_time_decay': _L1_attn_in['time_decay'], 'L1_attn_time_first': _L1_attn_in['time_first'], 'L1_attn_ln_gamma': _L1_attn_in['ln_gamma'], 'L1_attn_ln_beta': _L1_attn_in['ln_beta'], 'L1_ffn_router_w': _L1_ffn_in['router_w'], 'L1_ffn_gate_up_w': _L1_ffn_in['gate_up_w'], 'L1_ffn_down_w': _L1_ffn_in['down_w'], 'L1_ffn_shared_gate_w': _L1_ffn_in['shared_gate_w'], 'L1_ffn_shared_up_w': _L1_ffn_in['shared_up_w'], 'L1_ffn_shared_down_w': _L1_ffn_in['shared_down_w']}

def reference(x, ctx_2048, L0_attn_wq, L0_attn_wk, L0_attn_wv, L0_attn_wo, L0_attn_bern_u, L0_ffn_router_w, L0_ffn_e_bias, L0_ffn_W_gate, L0_ffn_W_up, L0_ffn_W_down, L0_ffn_shared_gate, L0_ffn_shared_up, L0_ffn_shared_down, L1_attn_W_key, L1_attn_W_value, L1_attn_W_output, L1_attn_W_shift, L1_attn_gate, L1_attn_time_decay, L1_attn_time_first, L1_attn_ln_gamma, L1_attn_ln_beta, L1_ffn_router_w, L1_ffn_gate_up_w, L1_ffn_down_w, L1_ffn_shared_gate_w, L1_ffn_shared_up_w, L1_ffn_shared_down_w):
    import jax
    import jax.numpy as jnp

    def _L0_attn_ref(hidden_states, wq, wk, wv, wo, bern_u):
        import jax, jax.numpy as jnp
        import numpy as np
        H = 16
        SB_RATIO = 0.1
        RB_RATIO = 0.5
        ROPE_BASE = 10000.0

        def _rotate_half(x):
            hd = x.shape[-1]
            x1, x2 = (x[..., :hd // 2], x[..., hd // 2:])
            return jnp.concatenate([-x2, x1], axis=-1)
        B, T, D = hidden_states.shape
        hd = D // H
        h = jnp.nan_to_num(hidden_states, nan=0.0, posinf=10000.0, neginf=-10000.0)

        def proj(w):
            return (h @ w.T).reshape(B, T, H, hd).transpose(0, 2, 1, 3)
        Q, K, V = (proj(wq), proj(wk), proj(wv))
        inv_freq = 1.0 / ROPE_BASE ** (jnp.arange(0, hd, 2, dtype=jnp.float32) / hd)
        pos = jnp.arange(T, dtype=jnp.float32)
        freqs = pos[:, None] * inv_freq[None, :]
        emb = jnp.concatenate([freqs, freqs], axis=-1)
        cos, sin = (jnp.cos(emb)[None, None], jnp.sin(emb)[None, None])
        Q = Q * cos + _rotate_half(Q) * sin
        K = K * cos + _rotate_half(K) * sin
        sb = max(0, min(int(SB_RATIO * T), T))
        rb = max(0, min(int(RB_RATIO * T), T - sb))
        kidx = jnp.arange(T)
        cam = (kidx < sb) | (kidx >= T - rb)
        scores = jnp.einsum('bhqd,bhkd->bhqk', Q, K) / np.sqrt(hd).astype(np.float32)
        neg = jnp.finfo(scores.dtype).min
        scores = jnp.where(cam[None, None, None, :], scores, neg)
        scores = jnp.nan_to_num(scores, nan=neg)
        probs = jax.nn.softmax(scores, axis=-1)
        if 0 < rb < T:
            e = T - rb
            ws = e + 1
            if T - ws > 0:
                last = probs[..., -1, :]
                mean_attn = last[..., ws:].mean(axis=-1) + 1e-06
                p = jnp.clip(last[..., e] / mean_attn, 0.0, 1.0)
                p = jnp.nan_to_num(p, nan=0.0, posinf=1.0, neginf=0.0)
                mask = (bern_u < p).astype(V.dtype)
                v_e = V[..., e, :] * mask[..., None] / rb
                end = min(T, ws + rb)
                V = V.at[..., ws:end, :].add(v_e[..., None, :])
        out = jnp.einsum('bhqk,bhkd->bhqd', probs, V)
        out = out.transpose(0, 2, 1, 3).reshape(B, T, D) @ wo.T
        return jnp.nan_to_num(out, nan=0.0, posinf=10000.0, neginf=-10000.0)

    def _L0_xattn_ref(q, k, v):
        import jax, jax.numpy as jnp
        import numpy as np
        N_HEAD = 8
        b, d, m = q.shape
        c = v.shape[1]
        h = N_HEAD
        qh = q.reshape(b * h, d // h, m)
        kh = k.reshape(b * h, d // h, -1)
        vh = v.reshape(b * h, c // h, -1)
        scale = 1.0 / jnp.sqrt(jnp.asarray(d // h, dtype=q.dtype))
        qk = jnp.einsum('bdm,bdn->bmn', qh, kh) * scale
        sm = jax.nn.softmax(qk, axis=-1)
        ret = jnp.einsum('bmn,bcn->bcm', sm, vh)
        return ret.reshape(b, c, m)

    def _L0_ffn_ref(hidden_states, router_w, e_bias, W_gate, W_up, W_down, shared_gate, shared_up, shared_down):
        import math
        import jax, jax.numpy as jnp
        import numpy as np
        from jax import lax
        D = 256
        I = 128
        E = 32
        K = 4
        NG = 8
        TKG = 3
        NSH = 2
        SCALE = 2.5
        CF = 1.25
        B, S = (2, 256)

        def _router(x, router_w, e_bias):
            scores = jax.nn.sigmoid(x @ router_w.T)
            sc = scores + e_bias[None, :]
            T = x.shape[0]
            gs = sc.reshape(T, NG, E // NG)
            group_scores = lax.top_k(gs, 2)[0].sum(-1)
            _, gidx = lax.top_k(group_scores, TKG)
            gmask = jnp.zeros((T, NG), sc.dtype).at[jnp.arange(T)[:, None], gidx].set(1.0)
            smask = jnp.repeat(gmask, E // NG, axis=1)
            masked = jnp.where(smask > 0, sc, 0.0)
            _, topk_idx = lax.top_k(masked, K)
            topk_w = jnp.take_along_axis(scores, topk_idx, axis=1)
            topk_w = topk_w / (topk_w.sum(-1, keepdims=True) + 1e-20)
            topk_w = topk_w * SCALE
            return (topk_idx.astype(jnp.int32), topk_w)

        def _moe_forward(hidden_states, router_w, e_bias, W_gate, W_up, W_down, shared_gate, shared_up, shared_down):
            b, s, d = hidden_states.shape
            T = b * s
            C = int(math.ceil(CF * T / E))
            EC = E * C
            x = hidden_states.reshape(T, d)
            topk_idx, topk_w = _router(x, router_w, e_bias)
            expert_flat = topk_idx.reshape(-1)
            w_flat = topk_w.reshape(-1)
            tok_flat = jnp.repeat(jnp.arange(T, dtype=jnp.int32), K)
            sort_ix = jnp.argsort(expert_flat)
            e_sorted = expert_flat[sort_ix]
            tok_s = tok_flat[sort_ix]
            w_s = w_flat[sort_ix]
            counts = jnp.zeros(E, jnp.int32).at[e_sorted].add(1)
            group_start = jnp.concatenate([jnp.zeros(1, jnp.int32), jnp.cumsum(counts)[:-1].astype(jnp.int32)])
            pos = jnp.arange(T * K, dtype=jnp.int32) - group_start[e_sorted]
            valid = pos < C
            dest = e_sorted * C + jnp.where(valid, pos, 0)
            slots_token = jnp.zeros(EC, jnp.int32).at[dest].add(jnp.where(valid, tok_s, 0))
            slots_w = jnp.zeros(EC, w_s.dtype).at[dest].add(jnp.where(valid, w_s, 0.0))
            Xp = x[slots_token].reshape(E, C, d)
            G = jnp.einsum('ecd,edi->eci', Xp, W_gate)
            U = jnp.einsum('ecd,edi->eci', Xp, W_up)
            Y = jnp.einsum('eci,eid->ecd', jax.nn.silu(G) * U, W_down)
            Yf = Y.reshape(EC, d) * slots_w[:, None]
            out = jnp.zeros((T, d), x.dtype).at[slots_token].add(Yf)
            shared = jax.nn.silu(x @ shared_gate.T) * (x @ shared_up.T) @ shared_down.T
            return (out + shared).reshape(b, s, d)
        return _moe_forward(hidden_states, router_w, e_bias, W_gate, W_up, W_down, shared_gate, shared_up, shared_down)

    def _L1_attn_ref(x, W_key, W_value, W_output, W_shift, gate, time_decay, time_first, ln_gamma, ln_beta):
        import jax, jax.numpy as jnp
        import numpy as np
        D_ATTN = 256
        D_STATE = 64
        SHIFT_FRAC = 0.5
        LN_EPS = 1e-05

        def _reference_tuple_inner(x, W_key, W_value, W_output, W_shift, gate, time_decay, time_first, ln_gamma, ln_beta):
            B, T, D = x.shape
            shift_len = max(1, int(T * SHIFT_FRAC))
            x_cat = jnp.roll(x, -shift_len, axis=1)
            g = jax.nn.sigmoid(gate)
            x_shift = jnp.einsum('btd,ed->bte', x_cat, W_shift) * g + x * (1.0 - g)
            mu = jnp.mean(x_shift, axis=-1, keepdims=True)
            var = jnp.var(x_shift, axis=-1, keepdims=True)
            x_norm = (x_shift - mu) * jax.lax.rsqrt(var + LN_EPS) * ln_gamma + ln_beta
            k = jnp.einsum('btd,sd->bts', x_norm, W_key)
            v = jnp.einsum('btd,sd->bts', x_norm, W_value)
            w = jnp.exp(time_decay)
            u = jnp.exp(time_first)
            wkv = jnp.exp(-u * jax.nn.sigmoid(k)) * v

            def step(state, wkv_t):
                state = state * w + wkv_t
                return (state, state)
            init = jnp.zeros((B, k.shape[-1]), x.dtype)
            last_state, states = jax.lax.scan(step, init, jnp.swapaxes(wkv, 0, 1))
            states = jnp.swapaxes(states, 0, 1)
            output = jnp.einsum('bts,ds->btd', states, W_output)
            return (output, jax.lax.stop_gradient(last_state))
        return _reference_tuple_inner(x, W_key, W_value, W_output, W_shift, gate, time_decay, time_first, ln_gamma, ln_beta)[0]

    def _L1_xattn_ref(q, k, v):
        import jax, jax.numpy as jnp
        import numpy as np
        N_HEAD = 8
        ALPHA = 5.0
        EPS = 1e-12

        def _l2norm(x, axis):
            n = jnp.sqrt(jnp.sum(x * x, axis=axis, keepdims=True))
            return x / jnp.maximum(n, EPS)
        B, D, Tq = q.shape
        Tk = k.shape[-1]
        Dv = v.shape[-2]
        h = N_HEAD
        d = D // h
        dv = Dv // h
        qh = q.reshape(B, h, d, Tq)
        kh = k.reshape(B, h, d, Tk)
        vh = v.reshape(B, h, dv, Tk)
        qn = _l2norm(qh, axis=-2)
        kn = _l2norm(kh, axis=-2)
        qk = ALPHA * jnp.einsum('bhdq,bhdk->bhqk', qn, kn)
        sm = jax.nn.softmax(qk, axis=-1)
        out = jnp.einsum('bhqk,bhdk->bhdq', sm, vh)
        return out.reshape(B, Dv, Tq)

    def _L1_ffn_ref(hidden_states, router_w, gate_up_w, down_w, shared_gate_w, shared_up_w, shared_down_w):
        import jax, jax.numpy as jnp
        import numpy as np
        B, S, D, I, E, K = (4, 128, 256, 128, 8, 2)
        Bb, Ss, Dd = hidden_states.shape
        x = hidden_states.reshape(-1, Dd)
        T = x.shape[0]
        shared = jax.nn.silu(x @ shared_gate_w) * (x @ shared_up_w) @ shared_down_w
        logits = x @ router_w
        top_val, top_idx = jax.lax.top_k(logits, K)
        probs = jnp.zeros_like(logits).at[jnp.arange(T)[:, None], top_idx].set(jax.nn.sigmoid(top_val))
        xin = probs.T[:, :, None] * x[None]
        gu = jnp.einsum('etd,edf->etf', xin, gate_up_w)
        gate, up = jnp.split(gu, 2, axis=-1)
        h = jax.nn.silu(gate) * up
        expert_out = jnp.einsum('eti,eid->etd', h, down_w)
        combined = shared + expert_out.sum(axis=0)
        return combined.reshape(Bb, Ss, Dd)
    x = x + _L0_attn_ref(_layernorm(x, axis=-1), L0_attn_wq, L0_attn_wk, L0_attn_wv, L0_attn_wo, L0_attn_bern_u)
    x = x + _L0_xattn_ref(_layernorm(x, axis=-1), ctx_2048, ctx_2048)
    x = x + _L0_ffn_ref(_layernorm(x, axis=-1), L0_ffn_router_w, L0_ffn_e_bias, L0_ffn_W_gate, L0_ffn_W_up, L0_ffn_W_down, L0_ffn_shared_gate, L0_ffn_shared_up, L0_ffn_shared_down)
    x = x + _L1_attn_ref(_layernorm(x, axis=-1), L1_attn_W_key, L1_attn_W_value, L1_attn_W_output, L1_attn_W_shift, L1_attn_gate, L1_attn_time_decay, L1_attn_time_first, L1_attn_ln_gamma, L1_attn_ln_beta)
    x = x + _L1_xattn_ref(_layernorm(x, axis=-1), ctx_2048, ctx_2048)
    x = x + _L1_ffn_ref(_layernorm(x, axis=-1), L1_ffn_router_w, L1_ffn_gate_up_w, L1_ffn_down_w, L1_ffn_shared_gate_w, L1_ffn_shared_up_w, L1_ffn_shared_down_w)
    return x

_drawn_inputs = setup_inputs


def setup_inputs(seed=0):
    import zlib

    import numpy as np

    out = dict(_drawn_inputs(seed))
    spreads = {'L0_ffn_e_bias': (0.0, 0.628),
     'L1_attn_gate': (1.0, 0.2),
     'L1_attn_ln_gamma': (1.0, 0.2),
     'L1_attn_ln_beta': (0.0, 0.1)}
    factors = {'L0_attn_wq': 8.0,
     'L0_attn_wk': 8.0,
     'L0_attn_bern_u': 200.0,
     'L0_ffn_router_w': 7.279,
     'L0_ffn_W_gate': 6.702,
     'L0_ffn_W_up': 8.0,
     'L0_ffn_W_down': 6.219,
     'L0_ffn_shared_gate': 2.75,
     'L0_ffn_shared_up': 2.915,
     'L0_ffn_shared_down': 2.777}
    for name, (base, spread) in spreads.items():
        noise = np.random.default_rng([zlib.crc32(name.encode()), seed]).standard_normal(out[name].shape)
        drawn = base * np.exp(spread * noise) if base else spread * noise
        out[name] = jnp.asarray(drawn.astype(out[name].dtype))
    for name, factor in factors.items():
        out[name] = (out[name] * factor).astype(out[name].dtype)
    return out
```

```python
from contextlib import ExitStack

import concourse.bass as bass
from concourse import mybir

F32 = mybir.dt.float32
BF16 = mybir.dt.bfloat16
I32 = mybir.dt.int32
U32 = mybir.dt.uint32
ALU = mybir.AluOpType
ACT = mybir.ActivationFunctionType
AX = mybir.AxisListType

NB, T, D = 16, 128, 256
KT = D // 128
EPS = 1e-5

H0, HD0 = 16, 16
SINK = int(0.1 * T)
RECENT = int(0.5 * T)
REC0 = T - RECENT
NK0 = SINK + RECENT
HG = 128 // HD0

HX = 8
DX = T // HX
TERMS = 6
QPART = (0, 1, 2, 0, 1, 0)
KPART = (0, 0, 0, 1, 1, 2)
NSTACK = TERMS * DX


CONST_AT, CONST_COLS = {}, 0
for _name, _width in (("ident", 128), ("key_of_head", HG), ("spread", NK0), ("pick3", 3), ("ones", 128),
                      ("half_ones", 64), ("rope_cos", HD0), ("rope_sin", HD0), ("group_ones", 128),
                      ("before", 128), ("iota32", 32)):
    CONST_AT[_name] = (CONST_COLS, _width)
    CONST_COLS += _width


def constants():
    import numpy as np

    p = np.arange(128)
    t = {k: np.zeros((128, w), np.float32) for k, (_, w) in CONST_AT.items()}
    t["ident"][p, p] = 1
    t["key_of_head"][p, p // HD0] = 1
    t["spread"][SINK, SINK + 1:] = 1.0 / RECENT
    t["pick3"][SINK, 0] = 1
    t["pick3"][SINK + 1:NK0, 1] = 1
    t["pick3"][:NK0, 2] = 1
    t["ones"][:] = 1
    t["half_ones"][:, 0:16] = 1
    t["half_ones"][:, 48:64] = 1
    freq = 1.0 / np.float32(10000.0) ** (np.arange(0, HD0, 2, dtype=np.float32) / HD0)
    angle = (p.astype(np.float32)[:, None] * freq[None, :].astype(np.float32)).astype(np.float32)
    t["rope_cos"][:] = np.tile(np.cos(angle), 2)
    t["rope_sin"][:] = np.concatenate([-np.sin(angle), np.sin(angle)], axis=1)
    t["group_ones"][:] = p[:, None] // DX == p[None, :] // DX
    t["iota32"][:] = np.arange(32)
    t["before"][:] = p[:, None] < p[None, :]
    return np.concatenate([t[k] for k in CONST_AT], axis=1)


EX0, TOP0, GROUPS, TOPG = 32, 4, 8, 3
CAP = -(-5 * NB * T // (4 * EX0))
SLOTS = EX0 * CAP
I0 = 128
SH0 = 2 * I0
DROPPED = 8192.0
NS = 64
EX1, TOP1, I1 = 8, 2, 128
EXS = EX1 + 1


def await_count(eng, sem, count):
    if isinstance(count, int) and count <= 0:
        return
    eng.wait_ge(sem, count)


def hold(eng):
    eng.nop(nofuse=True)


def live(n, k, total=NB):
    return not isinstance(n, int) or 0 <= n - k < total


def seen(n, k=0):
    return min(n - k, NB - 1) + 1 if isinstance(n, int) else n - k + 1


class Count:

    def __init__(self, sem):
        self.sem, self.base, self.n = sem, 0, 0

    def did(self, ins):
        ins.then_inc(self.sem, 1)
        self.n += 1

    def sync(self, eng):
        await_count(eng, self.sem, self.base + self.n)


def pipeline(eng, step, head, unroll, last_phase, count=None, per_step=0, total=NB,
             past=0):
    def peeled(n):
        step(n, n, lambda k, m: (n - k + past) // m + 1)

    def looped(j, c):
        step(j * unroll + c, c, lambda k, m: j * (unroll // m) + ((c - k + past) // m + 1))

    for n in range(head):
        peeled(n)
    turns = (total - head) // unroll
    assert turns * unroll == total - head
    if count is not None:
        base, n0 = count.base + count.n, per_step * unroll
    with eng.Fori(0, turns) as j:
        if count is not None:
            count.base, count.n = j * n0 + base, 0
        for u in range(unroll):
            looped(j, head + u)
        if count is not None:
            assert count.n == n0, (count.n, n0)
    if count is not None:
        count.base, count.n = base + turns * n0, 0
    for n in range(total, total + last_phase):
        peeled(n)


def decoder_kernel(nc, A, out):
    with ExitStack() as ctx:
        def keep(name, shape, dt=F32):
            return ctx.enter_context(nc.sbuf_tensor(name, shape, dt))

        def sem(name):
            return ctx.enter_context(nc.semaphore(name))

        bank = ctx.enter_context(nc.psum_tensor("bank", [128, 8, 512], F32))
        x_sb = keep("x_sb", [128, NB, D])
        moments = keep("moments", [128, NB, 2])
        mean_var = keep("mean_var", [128, 2])
        zero_eps = keep("zero_eps", [128, 2])
        rstd = keep("rstd", [128, NB])
        minus_half = keep("minus_half", [128, 1])
        bn6 = keep("bn6", [128, 2, 6])
        const = keep("const", [128, CONST_COLS])

        def table(name, rows=128):
            at, width = CONST_AT[name]
            return const[0:rows, at:at + width]

        ident = table("ident")

        x_loaded = sem("x_loaded")
        const_loaded = sem("const_loaded")
        stats_ready = sem("stats_ready")
        rstd_ready = sem("rstd_ready")
        x_ready = sem("x_ready")
        out_stored = sem("out_stored")

        NBUF = 4
        ORDER = (0, 2, 4, 6, 1, 3, 5, 7)
        c_rows = keep("c_rows", [128, 4, 2 * D])
        c_raw = c_rows[:, 0:2]
        c_unit = c_rows[:, 2:4]
        c_rest = keep("c_rest", [128, 2, 2 * D])
        c_part = keep("c_part", [128, 2, 3, 2 * D], BF16)
        q_stack = keep("q_stack", [128, NBUF, HX, D], BF16)
        k_stack = keep("k_stack", [128, NBUF, HX, D], BF16)
        c_vT_in = keep("c_vT_in", [128, 2, 2, T])
        c_vT = keep("c_vT", [128, 2, 2, HX, 32])
        c_max = keep("c_max", [128, 2, HX, 2])
        c_neg = keep("c_neg", [2 * HX, 3, 128], BF16)
        c_nrest = keep("c_nrest", [2 * HX, 2, 128])
        c_e = keep("c_e", [128, HX, 2, D])
        c_inv = keep("c_inv", [128, D])
        c_att = keep("c_att", [128, D])
        c_sq = keep("c_sq", [128, 2 * D])
        c_ss = keep("c_ss", [128, 2 * D])
        part_dram = nc.dram_tensor("part_dram", (2, 128, 3, 2 * D), BF16).ap()
        neg_dram = nc.dram_tensor("neg_dram", (2, 2 * HX, 3, 128), BF16).ap()
        pad_ready = sem("pad_ready")

        cross = {k: [sem(f"c_{k}{i}") for i in range(m)] for k, m in (
            ("ctx_in", 2), ("vT_in", 2), ("neg_in", NBUF), ("stack_in", NBUF))}
        cross |= {k: sem(f"c_{k}") for k in (
            "dve", "act", "h_ready", "sq_ready", "ss_in_psum", "ss_ready", "inv_norm", "unit_ready",
            "hi", "rest1", "mid", "rest2", "lo", "part_stored", "s_in_psum", "max_ready",
            "maxT_in_psum", "neg_ready", "neg_stored", "sT_in_psum", "e_ready", "pv_done",
            "vT_ready", "inv_ready")}
        cross_count = {k: Count(cross[k]) for k in ("dve", "act")}

        scope = ExitStack()

        def sb(name, shape, dt=F32):
            return scope.enter_context(nc.sbuf_tensor(name, shape, dt))

        wqk = sb("wqk", [128, KT, 2 * D])
        wv = sb("wv", [128, KT, D])
        wo = sb("wo", [128, KT, D])
        rope_cos, rope_sin = table("rope_cos"), table("rope_sin")
        key_of_head = table("key_of_head")
        spread = table("spread", NK0)
        pick3 = table("pick3", NK0)
        ones = table("ones")
        half_ones = table("half_ones").rearrange("p (o c) -> p o c", o=2)
        bern = sb("bern", [NK0, 3, H0])
        a_h = sb("a_h", [128, 2, D])
        a_hT = sb("a_hT", [128, 2, KT, T])
        a_hTk = sb("a_hTk", [128, 2, KT, NK0])
        a_v = sb("a_v", [NK0, 2, D])
        a_rot = sb("a_rot", [128, 2 * D])
        a_cos = sb("a_cos", [128, 2 * D])
        a_qk = sb("a_qk", [128, 2, 2 * D])
        a_qT = sb("a_qT", [128, 2, KT, T])
        a_kb = sb("a_kb", [128, 2, KT, HG, NK0])
        a_max = sb("a_max", [128, H0])
        a_p = sb("a_p", [128, 2, H0, NK0])
        a_pT = sb("a_pT", [NK0, H0, T])
        a_e3 = sb("a_e3", [NK0, 3, H0])
        a_lim = sb("a_lim", [NK0, 3, H0])
        a_add = sb("a_add", [NK0, D])
        a_vp = sb("a_vp", [NK0, H0, 32])
        a_inv = sb("a_inv", [128, 2 * T])
        a_oT = sb("a_oT", [128, 2, KT, T])
        w_loaded = sem("w_loaded")
        const_ready = sem("const_ready")
        a_dve = sem("a_dve")
        a_act = sem("a_act")
        a_h_ready = sem("a_h_ready")
        a_hT_in_psum = sem("a_hT_in_psum")
        a_hT_ready = sem("a_hT_ready")
        a_qkv_in_psum = sem("a_qkv_in_psum")
        a_v_ready = sem("a_v_ready")
        a_qk_ready = sem("a_qk_ready")
        a_qkT_in_psum = sem("a_qkT_in_psum")
        a_qT_ready = sem("a_qT_ready")
        a_kb_ready = sem("a_kb_ready")
        a_s_in_psum = sem("a_s_in_psum")
        a_s_shifted = sem("a_s_shifted")
        a_p_ready = sem("a_p_ready")
        a_pT_in_psum = sem("a_pT_in_psum")
        a_pT_ready = sem("a_pT_ready")
        a_e3_ready = sem("a_e3_ready")
        a_spread_in_psum = sem("a_spread_in_psum")
        a_vp_ready = sem("a_vp_ready")
        a_o_in_psum = sem("a_o_in_psum")
        a_inv_ready = sem("a_inv_ready")
        a_oT_ready = sem("a_oT_ready")
        a_out_in_psum = sem("a_out_in_psum")

        scope.close()
        ctx.callback(scope.close)

        h_all = sb("h_all", [128, NB, D])
        m_hc = sb("m_hc", [128, 2, D])
        RING = 8
        wgu = sb("wgu", [128, EXS, KT, 2 * I0])
        wdn = sb("wdn", [128, EXS, D])
        m_wr = sb("m_wr", [128, KT, EX0])
        m_wgu = sb("m_wgu", [128, KT, 2 * SH0])
        m_wdn = sb("m_wdn", [128, KT, D])
        m_hT = sb("m_hT", [128, 2, KT, T])
        m_sig = sb("m_sig", [128, 2, SH0])
        m_hid = sb("m_hid", [128, 2, SH0])
        m_hidT = sb("m_hidT", [128, KT, T])
        m_bias = sb("m_bias", [128, EX0])
        m_s = sb("m_s", [128, NB, EX0])
        m_t = [c_e[:, i * HX // 2:(i + 1) * HX // 2].rearrange("p h o (b e) -> p (h o b) e", e=EX0)
               .rearrange("p (b k) e -> p b k e", k=TOP0) for i in range(2)]
        m_hot = c_rows[:, :, :].rearrange("p a (b k e) -> p (a b) k e", k=TOP0, e=EX0)
        m_g = [sb(f"m_g{i}", [128, NB, GROUPS]) for i in range(6)]
        m_top = sb("m_top", [128, NB, 8])
        m_topi = sb("m_topi", [128, NB, 8], U32)
        m_pick = sb("m_pick", [128, NB, TOP0])
        m_w = sb("m_w", [128, NB, TOP0])
        m_k = [sb(f"m_k{i}", [128, NB, TOP0]) for i in range(3)]
        m_sum = sb("m_sum", [128, NB])
        m_slot = sb("m_slot", [128, NB, TOP0], U32)
        d_x = sb("d_x", [CAP, 2, D])
        d_xT = sb("d_xT", [128, 2, KT, CAP])
        d_sig = sb("d_sig", [CAP, I0])
        d_hid = sb("d_hid", [CAP, 2, I0])
        d_hidT = sb("d_hidT", [128, 2, CAP])
        d_y = sb("d_y", [CAP, 2, D])
        GB = 2
        g_y = sb("g_y", [128, GB, TOP0, D])
        xp_dram = nc.dram_tensor("xp_dram", (SLOTS, D), F32).ap()
        y_dram = nc.dram_tensor("y_dram", (SLOTS, D), F32).ap()
        m_w_loaded = sem("m_w_loaded")
        ring_in = [sem(f"ring_in{i}") for i in range(RING)]
        slots_zero, y_zero, y_used = sem("slots_zero"), sem("y_zero"), sem("y_used")
        m_dve, e_dve, r_dve, f_dve, l_dve, l_act = (sem(x) for x in (
            "m_dve", "e_dve", "r_dve", "f_dve", "l_dve", "l_act"))
        (m_h_ready, m_hT_in_psum, m_hT_ready, m_gu_in_psum, m_sig_ready, m_hid_ready, m_hidT_in_psum,
         m_hidT_ready, m_out_in_psum, m_s_ready, m_hot_ready, m_rank_in_psum, m_slot_ready, rows_sent) = (
            sem(x) for x in (
                "m_h_ready", "m_hT_in_psum", "m_hT_ready", "m_gu_in_psum", "m_sig_ready", "m_hid_ready",
                "m_hidT_in_psum", "m_hidT_ready", "m_out_in_psum", "m_s_ready", "m_hot_ready",
                "m_rank_in_psum", "m_slot_ready", "rows_sent"))
        d_x_in = [sem(f"d_x_in{i}") for i in range(2)]
        (d_xT_in_psum, d_xT_ready, d_gu_in_psum, d_sig_ready, d_hid_ready, d_hidT_in_psum, d_hidT_ready,
         d_y_in_psum, d_y_ready) = (sem(x) for x in (
             "d_xT_in_psum", "d_xT_ready", "d_gu_in_psum", "d_sig_ready", "d_hid_ready", "d_hidT_in_psum",
             "d_hidT_ready", "d_y_in_psum", "d_y_ready"))
        y_stored = [sem(f"y_stored{i}") for i in range(2)]
        y_in = [sem(f"y_in{i}") for i in range(4)]

        f_wshift = sb("f_wshift", [128, KT, D])
        f_wkv = sb("f_wkv", [128, 2, KT, 2 * NS])
        f_wo = sb("f_wo", [NS, D])
        f_gate = sb("f_gate", [128, 2, D])
        f_affine = sb("f_affine", [128, 2, KT])
        f_time = sb("f_time", [NS, 4])
        f_decay = sb("f_decay", [NS, T])
        f_bias = sb("f_bias", [NS, 3])
        f_h = h_all[:, 10:12, :]
        f_hT = h_all[:, 12:14, :].rearrange("p b (t c) -> p b t c", t=KT)
        f_part = sb("f_part", [128, D])
        f_xs = h_all[:, 14:16, :]
        f_mom = sb("f_mom", [128, 2, 2])
        f_var = sb("f_var", [128, 2])
        f_rstd = sb("f_rstd", [128, 2])
        f_z = sb("f_z", [128, D])
        f_zT = sb("f_zT", [128, KT, T])
        f_k = sb("f_k", [NS, 2, T])
        f_wkvx = sb("f_wkvx", [NS, T])
        f_state = sb("f_state", [NS, 2, T])
        (f_loaded, f_act, f_pe, f_h_ready, f_hT_in_psum, f_hT_ready, f_shift_in_psum, f_xs_ready, f_var_ready,
         f_rstd_ready, f_z_ready, f_zT_in_psum, f_zT_ready, f_kv_in_psum, f_k_ready, f_wkvx_ready,
         f_state_ready, f_out_in_psum, f_gate_exp, f_setup) = (sem(x) for x in (
             "f_loaded", "f_act", "f_pe", "f_h_ready", "f_hT_in_psum", "f_hT_ready", "f_shift_in_psum",
             "f_xs_ready", "f_var_ready", "f_rstd_ready", "f_z_ready", "f_zT_in_psum", "f_zT_ready",
             "f_kv_in_psum", "f_k_ready", "f_wkvx_ready", "f_state_ready", "f_out_in_psum", "f_gate_exp",
             "f_setup"))
        PAIRS = -(-EXS // 2)
        l_wr = sb("l_wr", [128, KT, EX1])
        l_h = m_hc
        l_hT = m_hT
        l_logit = sb("l_logit", [128, EX1])
        l_top = sb("l_top", [128, 8])
        l_topi = sb("l_topi", [128, 8], U32)
        l_pick = sb("l_pick", [128, TOP1])
        l_mask = sb("l_mask", [128, TOP1, EX1])
        l_p = sb("l_p", [128, 2, EXS])
        l_prob = sb("l_prob", [128, EX1])
        l_sig = sb("l_sig", [128, 2, 2 * I1])
        l_hid = sb("l_hid", [128, 2, 2 * I1])
        l_hidT = h_all[:, 0:EXS, :].rearrange("p b (i c) -> p (b i) c", c=T).rearrange(
            "p (b e) c -> p b e c", b=2)
        (l_loaded, l_h_ready, l_hT_in_psum, l_hT_ready, l_logit_in_psum, l_logit_ready, l_prob_ready, l_p_ready,
         l_gu_in_psum, l_sig_ready, l_hid_ready, l_hidT_in_psum, l_hidT_ready, l_out_in_psum) = (
             sem(x) for x in (
                 "l_loaded", "l_h_ready", "l_hT_in_psum", "l_hT_ready", "l_logit_in_psum", "l_logit_ready",
                 "l_prob_ready", "l_p_ready", "l_gu_in_psum", "l_sig_ready", "l_hid_ready", "l_hidT_in_psum",
                 "l_hidT_ready", "l_out_in_psum"))

        block = ctx.enter_context(nc.Block())

        def stats(dve, count, b):
            hold(dve)
            count.did(nc.vector.bn_stats(bn6[:, 0, :], x_sb[:, b, :]))
            count.sync(dve)
            hold(dve)
            count.did(nc.vector.bn_aggr(mean_var[:, :], bn6[:, 0, :]))
            count.sync(dve)
            nc.vector.tensor_tensor(moments[:, b, :], mean_var[:, :], zero_eps[:, :],
                                    ALU.add).then_inc(stats_ready, 1)

        def pool_rstd(pool, b, done):
            await_count(pool, stats_ready, done + b + 1)
            nc.gpsimd.tensor_tensor(rstd[:, bass.ds(b, 1)], moments[:, b, 1:2], minus_half[:, 0:1],
                                    ALU.pow).then_inc(rstd_ready, 1)

        s_bank = bank[:, 4:8, 0:4 * NK0].rearrange("p b (h k) -> p b h k", h=4)

        def attn_tensor(pe):
            def step(n, u, uses):
                p0, p1, p2, p3 = u % 2, (u - 1) % 2, u % 2, (u - 1) % 2
                if live(n, 1):
                    pe.wait_ge(a_qk_ready, n)
                    await_count(pe, a_oT_ready, n - 2)
                    for t in range(2 * KT):
                        mm = nc.tensor.transpose(bank[:, 3, t * T:(t + 1) * T],
                                                 a_qk[:, p1, t * 128:(t + 1) * 128], ident)
                    mm.then_inc(a_qkT_in_psum, 1)
                if live(n, 2):
                    pe.wait_ge(a_p_ready, n - 1)
                    for h in range(H0):
                        mm = nc.tensor.transpose(
                            bank[0:NK0, 4 + h // 4, (h % 4) * T:(h % 4 + 1) * T], a_p[:, p2, h, :],
                            ident)
                        if h % 4 == 3:
                            mm.then_inc(a_pT_in_psum, 1)
                if live(n, 0):
                    pe.wait_ge(a_h_ready, n + 1)
                    await_count(pe, x_ready, n - 3)
                    for t in range(KT):
                        mm = nc.tensor.transpose(bank[:, 0, t * T:(t + 1) * T],
                                                 a_h[:, p0, t * 128:(t + 1) * 128], ident)
                    mm.then_inc(a_hT_in_psum, 1)
                if live(n, 3):
                    pe.wait_ge(a_oT_ready, n - 2)
                    await_count(pe, a_hT_ready, 3 * seen(n))
                    for t in range(KT):
                        mm = nc.tensor.matmul(bank[:, 0, 0:D], a_oT[:, p3, t, :], wo[:, t, :],
                                              start=(t == 0), stop=(t == KT - 1))
                    mm.then_inc(a_out_in_psum, 1)
                if live(n, 0):
                    pe.wait_ge(a_hT_ready, 3 * (n + 1))
                    await_count(pe, a_qk_ready, n)
                    for t in range(KT):
                        nc.tensor.matmul(bank[:, 1, :], a_hT[:, p0, t, :], wqk[:, t, :],
                                         start=(t == 0), stop=(t == KT - 1))
                    await_count(pe, a_v_ready, n)
                    for t in range(KT):
                        mm = nc.tensor.matmul(bank[0:NK0, 2, 0:D], a_hTk[:, p0, t, :], wv[:, t, :],
                                              start=(t == 0), stop=(t == KT - 1))
                    mm.then_inc(a_qkv_in_psum, 1)
                if live(n, 2):
                    pe.wait_ge(a_e3_ready, n - 1)
                    await_count(pe, x_ready, seen(n, 3))
                    nc.tensor.matmul(bank[0:NK0, 0, 0:D], spread, a_v[:, p2, :],
                                     start=True, stop=True)
                    mm = nc.tensor.matmul(bank[0:NK0, 0, D:D + 3 * H0], ones[0:NK0, 0:NK0],
                                          a_e3[:, :, :].rearrange("p a h -> p (a h)"),
                                          start=True, stop=True)
                    mm.then_inc(a_spread_in_psum, 1)
                if live(n, 1):
                    pe.wait_ge(a_kb_ready, 2 * n)
                    pe.wait_ge(a_qT_ready, n)
                    await_count(pe, a_pT_ready, 4 * seen(n, 2))
                    for g in range(KT):
                        for half in range(2):
                            mm = nc.tensor.matmul(
                                s_bank[:, 2 * g + half, :, :], a_qT[:, p1, g, :],
                                a_kb[:, p1, g, 4 * half:4 * half + 4, :], start=True, stop=True)
                    mm.then_inc(a_s_in_psum, 1)
                if live(n, 2):
                    pe.wait_ge(a_vp_ready, 2 * (n - 1))
                    await_count(pe, a_qT_ready, seen(n, 1))
                    await_count(pe, a_kb_ready, 2 * seen(n, 1))
                    for g in range(KT):
                        for den in range(2):
                            col = (den * KT + g) * T
                            for odd in range(2):
                                for j in range(4):
                                    h = HG * g + 2 * j + odd
                                    w = half_ones[0:NK0, odd, :] if den else a_vp[:, h, :]
                                    mm = nc.tensor.matmul(
                                        bank[32 * j:32 * j + 32, 3, col:col + T], w, a_pT[:, h, :],
                                        start=(odd == 0), stop=(odd == 1))
                    mm.then_inc(a_o_in_psum, 1)

            pe.wait_ge(const_loaded, 16)
            pe.wait_ge(w_loaded, 16 * 5)
            pipeline(pe, step, 4, 2, 3)

        def attn_scalar(act):
            nc.scalar.preload_act_table_set("natural_log_exp_and_others")
            count = Count(a_act)

            def step(n, u, uses):
                p0, p1 = u % 2, (u - 1) % 2
                if live(n, 0):
                    act.wait_ge(a_hT_in_psum, n + 1)
                    await_count(act, a_qkv_in_psum, n - 1)
                    src = bank[:, 0, 0:D].rearrange("p (t c) -> p t c", t=KT)
                    nc.scalar.copy(a_hT[:, p0], src).then_inc(a_hT_ready, 1)
                    nc.scalar.copy(a_hTk[:, p0, :, 0:SINK], src[:, :, 0:SINK]).then_inc(a_hT_ready, 1)
                    nc.scalar.copy(a_hTk[:, p0, :, SINK:NK0], src[:, :, REC0:T]).then_inc(a_hT_ready, 1)
                if live(n, 1):
                    act.wait_ge(a_qkT_in_psum, n)
                    await_count(act, a_s_in_psum, n - 2)
                    nc.scalar.copy(a_qT[:, p1].rearrange("p t c -> p (t c)"),
                                   bank[:, 3, 0:KT * T]).then_inc(a_qT_ready, 1)
                if live(n, 2):
                    await_count(act, a_o_in_psum, n - 2)
                    for q in range(4):
                        act.wait_ge(a_pT_in_psum, 4 * (n - 2) + q + 1)
                        nc.scalar.copy(a_pT[:, 4 * q:4 * q + 4, :].rearrange("p h c -> p (h c)"),
                                       bank[0:NK0, 4 + q, :]).then_inc(a_pT_ready, 1)
                if live(n, 0):
                    act.wait_ge(a_qkv_in_psum, n + 1)
                    await_count(act, a_vp_ready, 2 * (n - 1))
                    nc.scalar.copy(a_v[:, p0, :], bank[0:NK0, 2, 0:D]).then_inc(a_v_ready, 1)
                if live(n, 1):
                    act.wait_ge(a_s_shifted, n)
                    nc.scalar.activation(a_p[:, p1], a_p[:, p1], ACT.Exp,
                                         scale=HD0 ** -0.5).then_inc(a_p_ready, 1)
                if live(n, 2):
                    act.wait_ge(a_o_in_psum, n - 1)
                    await_count(act, a_oT_ready, n - 2)
                    count.did(nc.scalar.activation(a_inv[:, :], bank[:, 3, KT * T:2 * KT * T], ACT.Ln))
                    count.sync(act)
                    nc.scalar.activation(a_inv[:, :], a_inv[:, :], ACT.Exp,
                                         scale=-1.0).then_inc(a_inv_ready, 1)

            pipeline(act, step, 4, 2, 3, count, 1)

        def attn_vector(dve):
            count = Count(a_dve)

            def step(n, u, uses):
                p0, p1, p2, p3 = u % 2, (u - 1) % 2, u % 2, (u - 1) % 2
                if live(n, 0):
                    dve.wait_ge(rstd_ready, n + 1)
                    await_count(dve, a_hT_in_psum, n - 1)
                    nc.vector.tensor_scalar(a_h[:, p0, :], x_sb[:, n, :], moments[:, n, 0:1],
                                            rstd[:, bass.ds(n, 1)], ALU.subtract, ALU.mult).then_inc(a_h_ready, 1)
                if live(n, 1):
                    dve.wait_ge(a_qT_ready, n)
                    await_count(dve, a_s_in_psum, n - 2)
                    kT = bank[:, 3, KT * T:2 * KT * T].rearrange("p (t c) -> p t c", t=KT)
                    for c0, c1, k0 in ((0, SINK, 0), (SINK, NK0, REC0)):
                        w = c1 - c0
                        nc.vector.tensor_tensor(
                            a_kb[:, p1, :, :, c0:c1],
                            kT[:, :, k0:k0 + w].unsqueeze(2).to_broadcast([128, KT, HG, w]),
                            key_of_head.unsqueeze(1).unsqueeze(3).to_broadcast([128, KT, HG, w]),
                            ALU.mult).then_inc(a_kb_ready, 1)
                if live(n, 3):
                    b = n - 3
                    dve.wait_ge(a_out_in_psum, n - 2)
                    nc.vector.tensor_tensor(x_sb[:, b, :], bank[:, 0, 0:D], x_sb[:, b, :],
                                            ALU.add).then_inc(x_ready, 1)
                if live(n, 2):
                    dve.wait_ge(a_pT_ready, 4 * (n - 1))
                    await_count(dve, a_spread_in_psum, n - 2)
                    nc.vector.tensor_tensor(
                        a_e3[:, :, :], a_pT[:, :, T - 1].unsqueeze(1).to_broadcast([NK0, 3, H0]),
                        pick3.unsqueeze(2).to_broadcast([NK0, 3, H0]),
                        ALU.mult).then_inc(a_e3_ready, 1)
                if live(n, 0):
                    dve.wait_ge(a_qkv_in_psum, n + 1)
                    await_count(dve, a_qkT_in_psum, n - 1)
                    heads = 2 * H0
                    raw = bank[:, 1, :].rearrange("p (h c) -> p h c", h=heads)
                    rot = a_rot[:, :].rearrange("p (h c) -> p h c", h=heads)
                    half = HD0 // 2
                    for c, s in ((0, half), (half, 0)):
                        count.did(nc.vector.tensor_tensor(
                            rot[:, :, c:c + half], raw[:, :, s:s + half],
                            rope_sin[:, c:c + half].unsqueeze(1).to_broadcast([128, heads, half]),
                            ALU.mult))
                    count.did(nc.vector.tensor_tensor(
                        a_cos[:, :].rearrange("p (h c) -> p h c", h=heads), raw,
                        rope_cos.unsqueeze(1).to_broadcast([128, heads, HD0]), ALU.mult))
                    count.sync(dve)
                    nc.vector.tensor_tensor(a_qk[:, p0, :], a_cos[:, :], a_rot[:, :],
                                            ALU.add).then_inc(a_qk_ready, 1)
                if live(n, 2):
                    dve.wait_ge(a_spread_in_psum, n - 1)
                    sums = bank[0:NK0, 0, D:D + 3 * H0].rearrange("p (a h) -> p a h", a=3)
                    count.did(nc.vector.tensor_scalar(a_lim[:, 0, :], sums[:, 1, :],
                                                      1.0 / (RECENT - 1), None, ALU.mult))
                    count.sync(dve)
                    count.did(nc.vector.scalar_tensor_tensor(
                        a_lim[:, 1, :], sums[:, 2, :], 1e-6, a_lim[:, 0, :], ALU.mult, ALU.add))
                    count.sync(dve)
                    count.did(nc.vector.tensor_tensor(a_lim[:, 2, :], a_lim[:, 1, :], bern[:, 2, :], ALU.mult))
                    count.sync(dve)
                    count.did(nc.vector.tensor_tensor(a_lim[:, 0, :], a_lim[:, 2, :], sums[:, 0, :],
                                                      ALU.is_lt))
                    count.sync(dve)
                    count.did(nc.vector.tensor_tensor(
                        a_add[:, :].rearrange("p (h c) -> p h c", h=H0),
                        bank[0:NK0, 0, 0:D].rearrange("p (h c) -> p h c", h=H0),
                        a_lim[:, 0, :].unsqueeze(2).to_broadcast([NK0, H0, HD0]), ALU.mult))
                    count.sync(dve)
                    await_count(dve, a_o_in_psum, n - 2)
                    for odd in range(2):
                        pick = [x.rearrange("p (j o c) -> p j o c", o=2, c=HD0)[:, :, odd, :]
                                for x in (a_add[:, :], a_v[:, p2, :])]
                        nc.vector.tensor_tensor(
                            a_vp[:, :, :].rearrange("p (j o) c -> p j o c", o=2)[
                                :, :, odd, HD0 * odd:HD0 * odd + HD0],
                            pick[0], pick[1], ALU.add).then_inc(a_vp_ready, 1)
                if live(n, 1):
                    dve.wait_ge(a_s_in_psum, n)
                    await_count(dve, a_pT_in_psum, 4 * (n - 2))
                    count.did(nc.vector.tensor_reduce(
                        a_max[:, :].rearrange("p (b h) -> p b h", b=4), s_bank, AX.X, ALU.max))
                    count.sync(dve)
                    nc.vector.tensor_tensor(
                        a_p[:, p1].rearrange("p (b h) k -> p b h k", b=4), s_bank,
                        a_max[:, :].rearrange("p (b h) -> p b h", b=4).unsqueeze(3)
                        .to_broadcast([128, 4, 4, NK0]), ALU.subtract).then_inc(a_s_shifted, 1)
                if live(n, 3):
                    dve.wait_ge(x_ready, n - 2)
                    stats(dve, count, n - 3)
                if live(n, 2):
                    dve.wait_ge(a_inv_ready, n - 1)
                    await_count(dve, a_out_in_psum, n - 3)
                    nc.vector.tensor_tensor(a_oT[:, p2].rearrange("p t c -> p (t c)"),
                                            bank[:, 3, 0:KT * T], a_inv[:, :],
                                            ALU.mult).then_inc(a_oT_ready, 1)

            dve.wait_ge(const_ready, 3)
            dve.wait_ge(w_loaded, 16 * 5)
            dve.wait_ge(const_loaded, 16)
            count.did(nc.vector.tensor_scalar(bern[:, 1, :], bern[:, 0, :], 1.0, 1e30, ALU.is_ge, ALU.mult))
            count.did(nc.vector.memset(a_vp[:, :, :], 0.0))
            nc.vector.memset(k_stack[NSTACK:NSTACK + 3, :, :, :], 1.0).then_inc(pad_ready, 1)
            count.sync(dve)
            count.did(nc.vector.tensor_tensor(bern[:, 2, :], bern[:, 0, :], bern[:, 1, :], ALU.add))
            for b in range(NB):
                dve.wait_ge(x_loaded, 16 * (b // 4 + 1))
                if b:
                    dve.wait_ge(stats_ready, b)
                stats(dve, count, b)
            pipeline(dve, step, 4, 2, 3, count, 3 + 5 + 1 + 2)

        def attn_gpsimd(pool):
            for b in range(NB):
                pool_rstd(pool, b, 0)

        def cross_tensor(pe, layer, done, rdone):
            S, past = cross, layer * NB
            rows = NSTACK + (3 if layer == 0 else 0)

            def weigh(n, u, odd):
                pe.wait_ge(S["e_ready"], HX * (n + past - 3) + 4 + 4 * odd)
                for half in range(2):
                    for den in range(2):
                        for j in range(4):
                            w = half_ones[:, odd, :] if den else c_vT[:, (u - 3) % 2, half, 2 * j + odd, :]
                            mm = nc.tensor.matmul(
                                bank[32 * j:32 * j + 32, 5 + den, 0:D], w, c_e[:, j + 4 * odd, half, :],
                                start=(odd == 0 and half == 0), stop=(odd == 1 and half == 1))
                mm.then_inc(S["pv_done"], 1)

            def step(n, u, uses):
                c = n + past
                if layer == 1 and live(n, 0):
                    pe.wait_ge(S["sq_ready"], n + 1)
                    await_count(pe, S["ss_ready"], n)
                    nc.tensor.matmul(bank[:, 7, :], table("group_ones"), c_sq[:, :],
                                     start=True, stop=True).then_inc(S["ss_in_psum"], 1)
                if live(n, 3):
                    pe.wait_ge(S["stack_in"][(u - 3) % NBUF], 16 * 2 * TERMS * uses(3, NBUF))
                    if layer == 0:
                        pe.wait_ge(S["neg_in"][(u - 3) % NBUF], 16 * uses(3, NBUF))
                for i in range(HX):
                    if live(n, 3):
                        await_count(pe, S["e_ready"], HX * (c - 3) + i - 1)
                        for half in range(2):
                            mm = nc.tensor.matmul(
                                bank[:, 2 + i % 2, half * D:half * D + D],
                                k_stack[0:rows, (u - 3) % NBUF, ORDER[i], half * 128:half * 128 + 128],
                                q_stack[0:rows, (u - 3) % NBUF, ORDER[i], :], start=True, stop=True)
                        mm.then_inc(S["sT_in_psum"], 1)
                    if layer == 0 and live(n, 1):
                        if i == 0:
                            pe.wait_ge(S["stack_in"][(u - 1) % NBUF], 16 * 2 * TERMS * uses(1, NBUF))
                        await_count(pe, S["max_ready"], HX * (c - 1) + i - 1)
                        for half in range(2):
                            mm = nc.tensor.matmul(
                                bank[:, i % 2, half * D:half * D + D],
                                q_stack[0:NSTACK, (u - 1) % NBUF, i, half * 128:half * 128 + 128],
                                k_stack[0:NSTACK, (u - 1) % NBUF, i, :], start=True, stop=True)
                        mm.then_inc(S["s_in_psum"], 1)
                    if i == 5 and live(n, 3):
                        pe.wait_ge(S["vT_ready"], 2 * (c - 2))
                        await_count(pe, x_ready, done + n - 3)
                        weigh(n, u, 0)
                if layer == 0 and live(n, 1):
                    pe.wait_ge(S["max_ready"], HX * c)
                    await_count(pe, S["neg_ready"], c - 1)
                    nc.tensor.transpose(bank[0:2 * HX, 4, 0:128],
                                        c_max[:, (u - 1) % 2].rearrange("p h a -> p (h a)"),
                                        ident).then_inc(S["maxT_in_psum"], 1)
                if live(n, 3):
                    weigh(n, u, 1)

            pe.wait_ge(x_ready, done)
            pe.wait_ge(pad_ready, 2)
            pipeline(pe, step, 4, 4, 3, past=past)

        def cross_scalar(act, layer, done, rdone):
            S, past = cross, layer * NB
            count = cross_count["act"]
            scale = DX ** -0.5 if layer == 0 else 5.0
            src = c_raw if layer == 0 else c_unit
            per_step = 1 if layer == 0 else 2

            def step(n, u, uses):
                c = n + past
                p0 = u % 2

                def part(k, waits):
                    if live(n, 0):
                        for s, m in waits:
                            act.wait_ge(s, m)
                        nc.scalar.copy(c_part[:, p0, k, :], (src if k == 0 else c_rest)[:, p0, :]
                                       ).then_inc(S[("hi", "mid", "lo")[k]], 1)

                if layer == 1 and live(n, 0):
                    act.wait_ge(S["ss_ready"], n + 1)
                    count.did(nc.scalar.activation(c_ss[:, :], c_ss[:, :], ACT.Ln))
                    count.sync(act)
                    nc.scalar.activation(c_ss[:, :], c_ss[:, :], ACT.Exp,
                                         scale=-0.5).then_inc(S["inv_norm"], 1)
                if live(n, 0):
                    await_count(act, S["part_stored"], 16 * (c - 1))
                part(0, [(S["h_ready"], c + 1), (S["ctx_in"][p0], 16 * uses(0, 2))] if layer == 0 else
                     [(S["unit_ready"], n + 1)])
                for i in range(HX):
                    if live(n, 3):
                        act.wait_ge(S["sT_in_psum"], HX * (c - 3) + i + 1)
                        await_count(act, S["pv_done"], 2 * (c - 4) + 1 + i // 4)
                        nc.scalar.activation(c_e[:, i].rearrange("p a m -> p (a m)"), bank[:, 2 + i % 2, :],
                                             ACT.Exp, scale=scale).then_inc(S["e_ready"], 1)
                    if i == 3:
                        part(1, [(S["rest1"], c + 1)])
                    if i == 6:
                        part(2, [(S["rest2"], c + 1)])
                if live(n, 3):
                    act.wait_ge(S["pv_done"], 2 * (c - 2))
                    await_count(act, x_ready, done + n - 3)
                    count.did(nc.scalar.activation(c_inv[:, :], bank[:, 6, 0:D], ACT.Ln))
                    count.sync(act)
                    nc.scalar.activation(c_inv[:, :], c_inv[:, :], ACT.Exp,
                                         scale=-1.0).then_inc(S["inv_ready"], 1)

            nc.scalar.preload_act_table_set("natural_log_exp_and_others")
            pipeline(act, step, 4, 4, 3, count, per_step, past=past)

        def cross_vector(dve, layer, done, rdone):
            S, past = cross, layer * NB
            count = cross_count["dve"]

            def step(n, u, uses):
                c = n + past
                p0, p1 = u % 2, (u - 1) % 2
                if live(n, 0):
                    dve.wait_ge(rstd_ready, rdone + n + 1)
                    await_count(dve, S["rest1"], c - 1)
                    nc.vector.tensor_scalar(
                        c_raw[:, p0, 0:D], x_sb[:, n, :], moments[:, n, 0:1],
                        rstd[:, bass.ds(n, 1)], ALU.subtract, ALU.mult).then_inc(S["h_ready"], 1)
                if layer == 1 and live(n, 0):
                    dve.wait_ge(S["ss_in_psum"], n + 1)
                    await_count(dve, S["unit_ready"], n)
                    nc.vector.tensor_scalar(c_ss[:, :], bank[:, 7, :], 1e-24, None,
                                            ALU.max).then_inc(S["ss_ready"], 1)
                    dve.wait_ge(S["inv_norm"], n + 1)
                    nc.vector.tensor_tensor(c_unit[:, p0, :], c_raw[:, p0, :], c_ss[:, :],
                                            ALU.mult).then_inc(S["unit_ready"], 1)
                if layer == 0 and live(n, 1):
                    await_count(dve, S["maxT_in_psum"], c - 2)
                    for i in range(HX):
                        dve.wait_ge(S["s_in_psum"], HX * (c - 1) + i + 1)
                        nc.vector.tensor_reduce(
                            c_max[:, p1, i, :], bank[:, i % 2, :].rearrange("p (a m) -> p a m", a=2),
                            AX.X, ALU.max).then_inc(S["max_ready"], 1)
                    dve.wait_ge(S["maxT_in_psum"], c)
                    await_count(dve, S["neg_stored"], 16 * (c - 1))
                    maxT = bank[0:2 * HX, 4, 0:128]
                    count.did(nc.vector.tensor_scalar(c_neg[:, 0, :], maxT, -1.0, None, ALU.mult))
                    count.sync(dve)
                    count.did(nc.vector.scalar_tensor_tensor(c_nrest[:, 0, :], maxT, -1.0, c_neg[:, 0, :],
                                                             ALU.mult, ALU.subtract))
                    count.sync(dve)
                    count.did(nc.vector.tensor_copy(c_neg[:, 1, :], c_nrest[:, 0, :]))
                    count.sync(dve)
                    nc.vector.tensor_tensor(c_neg[:, 2, :], c_nrest[:, 0, :], c_neg[:, 1, :],
                                            ALU.subtract).then_inc(S["neg_ready"], 1)
                if live(n, 3):
                    b = n - 3
                    dve.wait_ge(S["inv_ready"], c - 2)
                    count.did(nc.vector.tensor_tensor(c_att[:, :], bank[:, 5, 0:D], c_inv[:, :], ALU.mult))
                    count.sync(dve)
                    nc.vector.tensor_tensor(x_sb[:, b, :], c_att[:, :], x_sb[:, b, :],
                                            ALU.add).then_inc(x_ready, 1)
                    dve.wait_ge(x_ready, done + n - 2)
                    stats(dve, count, b)

            pipeline(dve, step, 4, 4, 3, count, 3 + (3 if layer == 0 else 0), past=past)

        def cross_gpsimd(pool, layer, done, rdone):
            S, past = cross, layer * NB
            src = c_raw if layer == 0 else c_unit

            def step(n, u, uses):
                c = n + past
                p0, p2 = u % 2, u % 2
                if layer == 1 and live(n, 0):
                    pool.wait_ge(S["h_ready"], c + 1)
                    pool.wait_ge(S["ctx_in"][p0], 16 * uses(0, 2))
                    await_count(pool, S["ss_in_psum"], n)
                    nc.gpsimd.tensor_tensor(c_sq[:, :], c_raw[:, p0, :], c_raw[:, p0, :],
                                            ALU.mult).then_inc(S["sq_ready"], 1)
                if live(n, 0):
                    pool.wait_ge(S["hi"], c + 1)
                    await_count(pool, S["lo"], c - 1)
                    nc.gpsimd.tensor_tensor(c_rest[:, p0, :], src[:, p0, :], c_part[:, p0, 0, :],
                                            ALU.subtract).then_inc(S["rest1"], 1)
                if live(n, 2):
                    pool.wait_ge(S["vT_in"][p2], 16 * uses(2, 2))
                    await_count(pool, S["pv_done"], 2 * (c - 3))
                    hold(pool)
                    for odd in range(2):
                        pick = c_vT_in[:, p2].rearrange("p a (j o c) -> p a j o c", o=2, c=DX)
                        nc.gpsimd.tensor_copy(
                            c_vT[:, p2].rearrange("p a (j o) c -> p a j o c", o=2)[
                                :, :, :, odd, DX * odd:DX * odd + DX],
                            pick[:, :, :, odd, :]).then_inc(S["vT_ready"], 1)
                if live(n, 0):
                    pool.wait_ge(S["mid"], c + 1)
                    nc.gpsimd.tensor_tensor(c_rest[:, p0, :], c_rest[:, p0, :], c_part[:, p0, 1, :],
                                            ALU.subtract).then_inc(S["rest2"], 1)
                if live(n, 3):
                    pool_rstd(pool, n - 3, rdone + NB)

            pipeline(pool, step, 4, 4, 3, past=past)

        def cross_sync(sp, layer, done, rdone):
            S, past = cross, layer * NB

            def step(n, u, uses):
                c = n + past
                p0, p1 = u % 2, (u - 1) % 2
                if live(n, 0):
                    await_count(sp, S["rest1"], c - 1)
                    sp.dma_start(c_raw[:, p0, D:2 * D],
                                 A["context"][bass.ds(n, 1)].rearrange("b t d -> (b t) d")
                                 ).then_inc(S["ctx_in"][p0], 16)
                if live(n, 2):
                    await_count(sp, S["vT_ready"], 2 * (c - 3))
                    sp.dma_start(c_vT_in[:, p0],
                                 A["contextT"][bass.ds(n - 2, 1)].rearrange("b (a p) t -> p (b a) t", p=128)
                                 ).then_inc(S["vT_in"][p0], 16)
                if live(n, 0):
                    sp.wait_ge(S["lo"], c + 1)
                    if live(n, 2):
                        sp.wait_ge(S["stack_in"][(u - 2) % NBUF], 16 * 2 * TERMS * uses(2, NBUF))
                    sp.dma_start(part_dram[p0], c_part[:, p0]).then_inc(S["part_stored"], 16)
                    sp.wait_ge(S["part_stored"], 16 * (c + 1))
                    hold(sp)
                    await_count(sp, S["sT_in_psum"], HX * (c - 3))
                    hold(sp)
                    for r in range(TERMS):
                        for stack, part, at in ((q_stack, QPART[r], 0), (k_stack, KPART[r], D)):
                            sp.dma_start(
                                stack[DX * r:DX * r + DX, u % NBUF, :, :],
                                part_dram[p0, :, part, at:at + D].rearrange("(h d) m -> d h m", d=DX)
                            ).then_inc(S["stack_in"][u % NBUF], 16)
                if layer == 0 and live(n, 1):
                    sp.wait_ge(S["neg_ready"], c)
                    hold(sp)
                    if live(n, 3):
                        sp.wait_ge(S["neg_in"][(u - 3) % NBUF], 16 * uses(3, NBUF))
                    sp.dma_start(neg_dram[p1], c_neg[:, :, :]).then_inc(S["neg_stored"], 16)
                    sp.wait_ge(S["neg_stored"], 16 * c)
                    sp.dma_start(
                        q_stack[NSTACK:NSTACK + 3, (u - 1) % NBUF, :, :].rearrange(
                            "c h (a m) -> c (h a) m", a=2),
                        neg_dram[p1].rearrange("a c m -> c a m")).then_inc(S["neg_in"][(u - 1) % NBUF], 16)

            pipeline(sp, step, 4, 4, 2, past=past)

        def shared_tensor(pe, done):
            def step(n, u, uses):
                p0 = u % 2
                if live(n, 1):
                    pe.wait_ge(m_hid_ready, n)
                    await_count(pe, m_hidT_ready, n - 1)
                    for t in range(KT):
                        mm = nc.tensor.transpose(bank[:, 3, t * T:(t + 1) * T],
                                                 m_hid[:, (u - 1) % 2, t * 128:(t + 1) * 128], ident)
                    mm.then_inc(m_hidT_in_psum, 1)
                if live(n, 0):
                    pe.wait_ge(m_h_ready, n + 1)
                    await_count(pe, m_hT_ready, n)
                    for t in range(KT):
                        mm = nc.tensor.transpose(bank[:, 0, t * T:(t + 1) * T],
                                                 m_hc[:, p0, t * 128:(t + 1) * 128], ident)
                    mm.then_inc(m_hT_in_psum, 1)
                if live(n, 1):
                    pe.wait_ge(m_hidT_ready, n)
                    await_count(pe, x_ready, done + n - 1)
                    for t in range(KT):
                        mm = nc.tensor.matmul(bank[:, 4, 0:D], m_hidT[:, t, :], m_wdn[:, t, :],
                                              start=(t == 0), stop=(t == KT - 1))
                    mm.then_inc(m_out_in_psum, 1)
                if live(n, 0):
                    pe.wait_ge(m_hT_ready, n + 1)
                    await_count(pe, m_hid_ready, n)
                    for t in range(KT):
                        nc.tensor.matmul(bank[:, 1, bass.ds(n * EX0, EX0)], m_hT[:, p0, t, :],
                                         m_wr[:, t, :], start=(t == 0), stop=(t == KT - 1))
                    for t in range(KT):
                        mm = nc.tensor.matmul(bank[:, 2, :], m_hT[:, p0, t, :], m_wgu[:, t, :],
                                              start=(t == 0), stop=(t == KT - 1))
                    mm.then_inc(m_gu_in_psum, 1)

            pe.wait_ge(x_ready, done)
            pe.wait_ge(m_w_loaded, 16 * 4)
            pipeline(pe, step, 4, 2, 1)
            pe.wait_ge(m_hot_ready, 1)
            pe.wait_ge(x_ready, done + NB)
            hot = m_s[:, :, :].rearrange("p b e -> p (b e)")
            nc.tensor.matmul(bank[:, 0, :], table("before"), hot, start=True, stop=True)
            nc.tensor.matmul(bank[:, 2, :], ones, hot, start=True, stop=True).then_inc(m_rank_in_psum, 1)

        def shared_scalar(act, done):
            def step(n, u, uses):
                p0 = u % 2
                if live(n, 0):
                    act.wait_ge(m_hT_in_psum, n + 1)
                    await_count(act, m_gu_in_psum, n - 1)
                    nc.scalar.copy(m_hT[:, p0].rearrange("p t c -> p (t c)"),
                                   bank[:, 0, 0:D]).then_inc(m_hT_ready, 1)
                if live(n, 1):
                    act.wait_ge(m_hidT_in_psum, n)
                    await_count(act, m_out_in_psum, n - 1)
                    nc.scalar.copy(m_hidT[:, :, :].rearrange("p t c -> p (t c)"),
                                   bank[:, 3, 0:D]).then_inc(m_hidT_ready, 1)
                if live(n, 0):
                    act.wait_ge(m_gu_in_psum, n + 1)
                    await_count(act, m_hid_ready, n - 1)
                    nc.scalar.activation(m_sig[:, p0, :], bank[:, 2, 0:SH0],
                                         ACT.Sigmoid).then_inc(m_sig_ready, 1)

            act.wait_ge(x_ready, done)
            nc.scalar.preload_act_table(ACT.Sigmoid)
            pipeline(act, step, 4, 2, 1)
            nc.scalar.activation(m_t[0][:, 0:NB // TOP0].rearrange("p b k e -> p (b k e)"), bank[:, 1, :],
                                 ACT.Sigmoid).then_inc(m_s_ready, 1)

        def shared_vector(dve, done):
            count = Count(m_dve)

            def step(n, u, uses):
                p0 = u % 2
                if live(n, 0):
                    dve.wait_ge(rstd_ready, done + n + 1)
                    await_count(dve, m_hT_in_psum, n - 1)
                    count.did(nc.vector.tensor_scalar(
                        m_hc[:, p0, :], x_sb[:, n, :], moments[:, n, 0:1],
                        rstd[:, bass.ds(n, 1)], ALU.subtract, ALU.mult))
                    count.sync(dve)
                    nc.vector.tensor_copy(h_all[:, n, :], m_hc[:, p0, :]).then_inc(m_h_ready, 1)
                    dve.wait_ge(m_sig_ready, n + 1)
                    await_count(dve, m_hidT_in_psum, n - 1)
                    count.did(nc.vector.tensor_tensor(m_sig[:, p0, :], bank[:, 2, 0:SH0], m_sig[:, p0, :],
                                                      ALU.mult))
                    count.sync(dve)
                    nc.vector.tensor_tensor(m_hid[:, p0, :], bank[:, 2, SH0:2 * SH0], m_sig[:, p0, :],
                                            ALU.mult).then_inc(m_hid_ready, 1)
                if live(n, 1):
                    dve.wait_ge(m_out_in_psum, n)
                    nc.vector.tensor_tensor(x_sb[:, n - 1, :], bank[:, 4, 0:D], x_sb[:, n - 1, :],
                                            ALU.add).then_inc(x_ready, 1)

            pipeline(dve, step, 4, 2, 1, count, 2)
            dve.wait_ge(x_ready, done + NB)
            dve.wait_ge(m_s_ready, 1)
            dve.wait_ge(m_w_loaded, 16 * 4)
            seq = lambda ins: (count.did(ins), count.sync(dve))
            tt, ts = nc.vector.tensor_tensor, nc.vector.tensor_scalar
            all_e = [128, NB, TOP0, EX0]
            score = m_t[0][:, 0:NB // TOP0].rearrange("p a k e -> p (a k) e")
            sc = m_t[1][:, 0:NB // TOP0].rearrange("p a k e -> p (a k) e")
            seq(tt(sc, score, m_bias[:, :].unsqueeze(1).to_broadcast([128, NB, EX0]), ALU.add))
            of = sc.rearrange("p b (g c) -> p b g c", c=EX0 // GROUPS)
            a, b_, c, d = (of[:, :, :, i] for i in range(4))
            g = [x[:, :, :] for x in m_g]
            for o, i0, i1, op in ((g[0], a, b_, ALU.max), (g[1], a, b_, ALU.min), (g[2], c, d, ALU.max),
                                  (g[3], c, d, ALU.min)):
                count.did(tt(o, i0, i1, op))
            count.sync(dve)
            count.did(tt(g[4], g[0], g[2], ALU.max))
            count.did(tt(g[5], g[0], g[2], ALU.min))
            seq(tt(g[1], g[1], g[3], ALU.max))
            seq(tt(g[5], g[5], g[1], ALU.max))
            seq(tt(g[4], g[4], g[5], ALU.add))
            for b in range(NB):
                count.did(nc.vector.max(m_top[:, b, :], g[4][:, b, :]))
            count.sync(dve)
            for b in range(NB):
                count.did(nc.vector.max_index(m_topi[:, b, :], m_top[:, b, :], g[4][:, b, :]))
            count.sync(dve)
            seq(nc.vector.tensor_copy(m_pick[:, :, 0:TOPG], m_topi[:, :, 0:TOPG]))
            iota = table("iota32")
            chosen = m_hot[:, :, 0:TOPG, 0:GROUPS]
            for k in range(TOPG):
                count.did(tt(m_hot[:, :, k, 0:GROUPS],
                             iota[:, 0:GROUPS].unsqueeze(1).to_broadcast([128, NB, GROUPS]),
                             m_pick[:, :, k:k + 1].to_broadcast([128, NB, GROUPS]), ALU.is_equal))
            count.sync(dve)
            seq(nc.vector.tensor_reduce(g[0], chosen.rearrange("p b k g -> p b g k"), AX.X, ALU.add))
            seq(tt(of, of, g[0].unsqueeze(3).to_broadcast([128, NB, GROUPS, EX0 // GROUPS]), ALU.mult))
            seq(ts(sc, sc, 0.0, None, ALU.add))
            for b in range(NB):
                count.did(nc.vector.max(m_top[:, b, :], sc[:, b, :]))
            count.sync(dve)
            for b in range(NB):
                count.did(nc.vector.max_index(m_topi[:, b, :], m_top[:, b, :], sc[:, b, :]))
            count.sync(dve)
            seq(nc.vector.tensor_copy(m_pick[:, :, :], m_topi[:, :, 0:TOP0]))
            for k in range(TOP0):
                count.did(tt(m_hot[:, :, k, :], iota.unsqueeze(1).to_broadcast([128, NB, EX0]),
                             m_pick[:, :, k:k + 1].to_broadcast([128, NB, EX0]), ALU.is_equal))
            count.sync(dve)
            nc.vector.tensor_reduce(m_s[:, :, :], m_hot[:, :, :, :].rearrange("p b k e -> p b e k"), AX.X,
                                    ALU.add).then_inc(m_hot_ready, 1)
            dve.wait_ge(m_hot_ready, 1)
            for k in range(TOP0):
                count.did(tt(m_t[1][:, :, k, :], m_hot[:, :, k, :], score, ALU.mult))
            count.sync(dve)
            seq(nc.vector.tensor_reduce(m_w[:, :, :], m_t[1][:, :, :, :], AX.X, ALU.add))
            seq(nc.vector.tensor_reduce(m_sum[:, :], m_w[:, :, :], AX.X, ALU.add))
            seq(ts(m_sum[:, :], m_sum[:, :], 1e-20, None, ALU.add))
            seq(nc.vector.reciprocal(m_sum[:, :], m_sum[:, :]))
            seq(ts(m_sum[:, :], m_sum[:, :], 2.5, None, ALU.mult))
            seq(tt(m_w[:, :, :], m_w[:, :, :], m_sum[:, :].unsqueeze(2).to_broadcast([128, NB, TOP0]),
                   ALU.mult))
            dve.wait_ge(m_rank_in_psum, 1)
            before = bank[:, 0, :].rearrange("p (b e) -> p b e", e=EX0)
            in_all = bank[:, 2, :].rearrange("p (b e) -> p b e", e=EX0)
            base = m_t[1][:, 0:NB // TOP0].rearrange("p a k e -> p (a k) e")
            seq(nc.vector.memset(base[:, 0, :], 0.0))
            for b in range(1, NB):
                seq(tt(base[:, b, :], in_all[:, b - 1, :], base[:, b - 1, :], ALU.add))
            seq(tt(m_s[:, :, :], before, base, ALU.add))
            for k in range(TOP0):
                count.did(tt(m_t[0][:, :, k, :], m_hot[:, :, k, :], m_s[:, :, :], ALU.mult))
            count.sync(dve)
            rank, slot, over = (x[:, :, :] for x in m_k)
            seq(nc.vector.tensor_reduce(rank, m_t[0][:, :, :, :], AX.X, ALU.add))
            count.did(ts(over, rank, float(CAP), DROPPED, ALU.is_ge, ALU.mult))
            seq(nc.vector.scalar_tensor_tensor(slot.rearrange("p b k -> p (b k)"),
                                               m_pick[:, :, :].rearrange("p b k -> p (b k)"), float(CAP),
                                               rank.rearrange("p b k -> p (b k)"), ALU.mult, ALU.add))
            seq(tt(slot, slot, over, ALU.add))
            nc.vector.tensor_copy(m_slot[:, :, :], slot).then_inc(m_slot_ready, 1)

        def dispatch_gpsimd(pool):
            pool.wait_ge(m_slot_ready, 1)
            pool.wait_ge(slots_zero, 16 * 5)
            for b in range(NB):
                for k in range(TOP0):
                    pool.indirect_dma_start(
                        out=xp_dram, out_offset=bass.IndirectOffsetOnAxis(ap=m_slot[:, b, k:k + 1], axis=0),
                        in_=h_all[:, b, :], in_offset=None, bounds_check=SLOTS - 1,
                        oob_is_err=False).then_inc(rows_sent, 16)

        def collect_gpsimd(pool, done):
            for n in range(NB):
                if n == 0:
                    for p in range(2):
                        pool.wait_ge(y_stored[p], 16 * (EX0 // 2))
                await_count(pool, y_zero, n - GB + 1 + 1)
                for k in range(TOP0):
                    pool.indirect_dma_start(
                        out=g_y[:, n % GB, k, :], out_offset=None, in_=y_dram,
                        in_offset=bass.IndirectOffsetOnAxis(ap=m_slot[:, n, k:k + 1], axis=0),
                        bounds_check=SLOTS - 1, oob_is_err=False).then_inc(y_in[n % GB], 16)
                if n >= 1:
                    pool_rstd(pool, n - 1, 3 * NB)
            pool_rstd(pool, NB - 1, 3 * NB)

        def collect_vector(dve, done):
            count = Count(r_dve)

            def step(n, u, uses):
                dve.wait_ge(y_in[u % GB], 16 * TOP0 * uses(0, GB))
                for k in range(TOP0):
                    ins = nc.vector.scalar_tensor_tensor(x_sb[:, n, :], g_y[:, u % GB, k, :],
                                                         m_w[:, n, k:k + 1], x_sb[:, n, :],
                                                         ALU.mult, ALU.add)
                    if k < TOP0 - 1:
                        count.did(ins)
                        count.sync(dve)
                    else:
                        ins.then_inc(x_ready, 1)
                dve.wait_ge(x_ready, done + n + 1)
                nc.vector.memset(g_y[:, u % GB], 0.0).then_inc(y_zero, 1)
                stats(dve, count, n)

            pipeline(dve, step, 4, 4, 0, count, TOP0 - 1 + 2)

        def expert_tensor(pe):
            def step(n, u, uses):
                p0, p1 = u % 2, (u - 1) % 2
                if live(n, 1, EX0):
                    pe.wait_ge(d_hid_ready, n)
                    await_count(pe, d_hidT_ready, n - 1)
                    nc.tensor.transpose(bank[:, 2, 0:CAP], d_hid[:, p1, :],
                                        ident[0:CAP, 0:CAP]).then_inc(d_hidT_in_psum, 1)
                if live(n, 0, EX0):
                    pe.wait_ge(d_x_in[p0], 16 * uses(0, 2))
                    await_count(pe, d_xT_ready, n)
                    for t in range(KT):
                        mm = nc.tensor.transpose(bank[:, 0, t * CAP:(t + 1) * CAP],
                                                 d_x[:, p0, t * 128:(t + 1) * 128], ident[0:CAP, 0:CAP])
                    mm.then_inc(d_xT_in_psum, 1)
                if live(n, 1, EX0):
                    pe.wait_ge(d_hidT_ready, n)
                    await_count(pe, d_y_ready, n - 1)
                    nc.tensor.matmul(bank[0:CAP, 3, 0:D], d_hidT[:, p1, :], wdn[:, (u - 1) % RING, :],
                                     start=True, stop=True).then_inc(d_y_in_psum, 1)
                if live(n, 0, EX0):
                    pe.wait_ge(d_xT_ready, n + 1)
                    pe.wait_ge(ring_in[u % RING], 32 * uses(0, RING))
                    await_count(pe, d_hid_ready, n)
                    for t in range(KT):
                        mm = nc.tensor.matmul(bank[0:CAP, 1, 0:2 * I0], d_xT[:, p0, t, :],
                                              wgu[:, u % RING, t, :], start=(t == 0), stop=(t == KT - 1))
                    mm.then_inc(d_gu_in_psum, 1)

            pe.wait_ge(m_slot_ready, 1)
            pipeline(pe, step, 8, 8, 1, total=EX0)

        def expert_scalar(act):
            def step(n, u, uses):
                p0, p1 = u % 2, (u - 1) % 2
                if live(n, 0, EX0):
                    act.wait_ge(d_xT_in_psum, n + 1)
                    await_count(act, d_gu_in_psum, n - 1)
                    nc.scalar.copy(d_xT[:, p0].rearrange("p t c -> p (t c)"),
                                   bank[:, 0, 0:KT * CAP]).then_inc(d_xT_ready, 1)
                if live(n, 1, EX0):
                    act.wait_ge(d_hidT_in_psum, n)
                    await_count(act, d_y_in_psum, n - 2)
                    nc.scalar.copy(d_hidT[:, p1, :], bank[:, 2, 0:CAP]).then_inc(d_hidT_ready, 1)
                if live(n, 0, EX0):
                    act.wait_ge(d_gu_in_psum, n + 1)
                    await_count(act, d_hid_ready, n)
                    nc.scalar.activation(d_sig[:, :], bank[0:CAP, 1, 0:I0],
                                         ACT.Sigmoid).then_inc(d_sig_ready, 1)

            pipeline(act, step, 8, 8, 1, total=EX0)

        def expert_vector(dve):
            count = Count(e_dve)

            def step(n, u, uses):
                p0, p1 = u % 2, (u - 1) % 2
                if live(n, 0, EX0):
                    dve.wait_ge(d_sig_ready, n + 1)
                    await_count(dve, d_hidT_in_psum, n - 1)
                    count.did(nc.vector.tensor_tensor(d_hid[:, p0, :], bank[0:CAP, 1, 0:I0], d_sig[:, :],
                                                      ALU.mult))
                    count.sync(dve)
                    nc.vector.tensor_tensor(d_hid[:, p0, :], bank[0:CAP, 1, I0:2 * I0], d_hid[:, p0, :],
                                            ALU.mult).then_inc(d_hid_ready, 1)
                if live(n, 1, EX0):
                    dve.wait_ge(d_y_in_psum, n)
                    if live(n, 3, EX0):
                        dve.wait_ge(y_stored[(u - 3) % 2], 16 * uses(3, 2))
                    nc.vector.tensor_copy(d_y[:, p1, :], bank[0:CAP, 3, 0:D]).then_inc(d_y_ready, 1)

            pipeline(dve, step, 8, 8, 1, count, 1, total=EX0)

        def expert_sync(sp):
            def step(n, u, uses):
                p0, p1 = u % 2, (u - 1) % 2
                if live(n, 0, EX0):
                    await_count(sp, d_xT_in_psum, n - 1)
                    sp.dma_start(d_x[:, p0, :], xp_dram[bass.ds(n * CAP, CAP), :]).then_inc(d_x_in[p0], 16)
                if live(n, 1, EX0):
                    sp.wait_ge(d_y_ready, n)
                    sp.dma_start(y_dram[bass.ds((n - 1) * CAP, CAP), :],
                                 d_y[:, p1, :]).then_inc(y_stored[p1], 16)
                    if not isinstance(n, int) or n - 1 + RING < EX0:
                        sp.wait_ge(d_y_in_psum, n)
                        load_expert(sp, n - 1 + RING, u - 1)

            sp.wait_ge(rows_sent, 16 * NB * TOP0)
            pipeline(sp, step, RING, RING, RING + 1, total=EX0 - RING)

        def load_expert(sp, e, u):
            sp.dma_start(wgu[:, u % RING, :, :],
                         A["W_gu"][bass.ds(e, 1)].rearrange("e (t p) i -> p (e t) i", p=128)
                         ).then_inc(ring_in[u % RING], 16)
            sp.dma_start(wdn[:, u % RING, :],
                         A["W_down"][bass.ds(e, 1)].rearrange("e p o -> p (e o)")).then_inc(ring_in[u % RING], 16)

        def shift_tensor(pe, done):
            def step(n, u, uses):
                p0, p2 = u % 2, u % 2
                if live(n, 2):
                    pe.wait_ge(f_state_ready, n - 1)
                    await_count(pe, x_ready, done + n - 2)
                    nc.tensor.matmul(bank[:, 4, 0:D], f_state[:, p2, :], f_wo[:, :],
                                     start=True, stop=True).then_inc(f_out_in_psum, 1)
                if live(n, 0):
                    pe.wait_ge(f_h_ready, n + 1)
                    await_count(pe, f_hT_ready, 2 * n)
                    for t in range(KT):
                        mm = nc.tensor.transpose(bank[:, 0, t * T:(t + 1) * T],
                                                 f_h[:, p0, t * 128:(t + 1) * 128], ident)
                    mm.then_inc(f_hT_in_psum, 1)
                if live(n, 1):
                    pe.wait_ge(f_z_ready, n)
                    await_count(pe, f_zT_ready, n - 1)
                    for t in range(KT):
                        mm = nc.tensor.transpose(bank[:, 2, t * T:(t + 1) * T],
                                                 f_z[:, t * 128:(t + 1) * 128], ident)
                    mm.then_inc(f_zT_in_psum, 1)
                if live(n, 0):
                    pe.wait_ge(f_hT_ready, 2 * (n + 1))
                    await_count(pe, f_xs_ready, n)
                    for t in range(KT):
                        mm = nc.tensor.matmul(bank[:, 1, 0:D], f_hT[:, p0, t, :], f_wshift[:, t, :],
                                              start=(t == 0), stop=(t == KT - 1))
                    mm.then_inc(f_shift_in_psum, 1)
                if live(n, 1):
                    pe.wait_ge(f_zT_ready, n)
                    await_count(pe, f_wkvx_ready, n - 1)
                    for kv in range(2):
                        for t in range(KT):
                            mm = nc.tensor.matmul(bank[0:NS, 3, kv * T:(kv + 1) * T],
                                                  f_wkv[:, 1, t, kv * NS:(kv + 1) * NS], f_zT[:, t, :],
                                                  start=(t == 0), stop=(t == KT - 1))
                    mm.then_inc(f_kv_in_psum, 1)

            pe.wait_ge(x_ready, done)
            pe.wait_ge(f_loaded, 16 * 8)
            for kv in range(2):
                for t in range(KT):
                    mm = nc.tensor.matmul(bank[0:NS, 3, kv:kv + 1], f_wkv[:, 0, t, kv * NS:(kv + 1) * NS],
                                          f_affine[:, 1, t:t + 1], start=(t == 0), stop=(t == KT - 1))
            mm.then_inc(f_pe, 1)
            pe.wait_ge(f_setup, 1)
            pipeline(pe, step, 4, 2, 2)

        def shift_scalar(act, done):
            count = Count(f_act)

            def step(n, u, uses):
                p0, p1 = u % 2, (u - 1) % 2
                if live(n, 0):
                    act.wait_ge(f_hT_in_psum, n + 1)
                    await_count(act, f_shift_in_psum, n - 1)
                    src = bank[:, 0, 0:D].rearrange("p (t c) -> p t c", t=KT)
                    half = T // 2
                    nc.scalar.copy(f_hT[:, p0, :, 0:half], src[:, :, half:T]).then_inc(f_hT_ready, 1)
                    nc.scalar.copy(f_hT[:, p0, :, half:T], src[:, :, 0:half]).then_inc(f_hT_ready, 1)
                if live(n, 1):
                    act.wait_ge(f_zT_in_psum, n)
                    await_count(act, f_kv_in_psum, n - 1)
                    nc.scalar.copy(f_zT[:, :, :].rearrange("p t c -> p (t c)"),
                                   bank[:, 2, 0:D]).then_inc(f_zT_ready, 1)
                    act.wait_ge(f_kv_in_psum, n)
                    await_count(act, f_wkvx_ready, n - 2)
                    e = f_k[:, p1, :]
                    count.did(nc.scalar.activation(e, bank[0:NS, 3, 0:T], ACT.Exp, bias=f_bias[:, 2:3],
                                                   scale=-1.0))
                    count.sync(act)
                    count.did(nc.scalar.activation(e, e, ACT.Ln, bias=1.0))
                    count.sync(act)
                    count.did(nc.scalar.activation(e, e, ACT.Exp, scale=-1.0))
                    count.sync(act)
                    nc.scalar.activation(e, e, ACT.Exp, scale=f_time[:, 3:4]).then_inc(f_k_ready, 1)

            nc.scalar.preload_act_table_set("natural_log_exp_and_others")
            act.wait_ge(x_ready, done)
            act.wait_ge(f_loaded, 16 * 8)
            gate = f_gate[:, 0, :]
            count.did(nc.scalar.activation(f_time[:, 2:3], f_time[:, 0:1], ACT.Exp))
            count.did(nc.scalar.activation(f_time[:, 3:4], f_time[:, 1:2], ACT.Exp))
            count.did(nc.scalar.activation(gate, gate, ACT.Exp, scale=-1.0))
            count.sync(act)
            count.did(nc.scalar.activation(gate, gate, ACT.Ln, bias=1.0))
            count.sync(act)
            nc.scalar.activation(gate, gate, ACT.Exp, scale=-1.0).then_inc(f_gate_exp, 1)
            act.wait_ge(f_setup, 1)
            pipeline(act, step, 4, 2, 1, count, 3)

        def shift_vector(dve, done, rdone):
            count = Count(f_dve)

            def step(n, u, uses):
                p0, p1, p2 = u % 2, (u - 1) % 2, u % 2
                if live(n, 0):
                    dve.wait_ge(rstd_ready, rdone + n + 1)
                    await_count(dve, f_hT_in_psum, n - 1)
                    nc.vector.tensor_scalar(
                        f_h[:, p0, :], x_sb[:, n, :], moments[:, n, 0:1],
                        rstd[:, bass.ds(n, 1)], ALU.subtract, ALU.mult).then_inc(f_h_ready, 1)
                if live(n, 1):
                    dve.wait_ge(f_rstd_ready, n)
                    await_count(dve, f_zT_in_psum, n - 1)
                    nc.vector.tensor_scalar(
                        f_z[:, :], f_xs[:, p1, :], f_mom[:, p1, 0:1], f_rstd[:, p1:p1 + 1],
                        ALU.subtract, ALU.mult).then_inc(f_z_ready, 1)
                if live(n, 2):
                    dve.wait_ge(f_out_in_psum, n - 1)
                    nc.vector.tensor_tensor(x_sb[:, n - 2, :], bank[:, 4, 0:D], x_sb[:, n - 2, :],
                                            ALU.add).then_inc(x_ready, 1)
                if live(n, 0):
                    dve.wait_ge(f_h_ready, n + 1)
                    count.did(nc.vector.tensor_tensor(f_part[:, :], f_h[:, p0, :], f_gate[:, 1, :],
                                                      ALU.mult))
                    count.sync(dve)
                    dve.wait_ge(f_shift_in_psum, n + 1)
                    nc.vector.tensor_tensor(f_xs[:, p0, :], bank[:, 1, 0:D], f_part[:, :],
                                            ALU.add).then_inc(f_xs_ready, 1)
                    dve.wait_ge(f_xs_ready, n + 1)
                    count.did(nc.vector.bn_stats(bn6[:, 1, :], f_xs[:, p0, :]))
                    count.sync(dve)
                    hold(dve)
                    count.did(nc.vector.bn_aggr(f_mom[:, p0, :], bn6[:, 1, :]))
                    count.sync(dve)
                    nc.vector.tensor_scalar(f_var[:, p0:p0 + 1], f_mom[:, p0, 1:2], EPS, None,
                                            ALU.add).then_inc(f_var_ready, 1)
                if live(n, 1):
                    dve.wait_ge(f_k_ready, n)
                    nc.vector.scalar_tensor_tensor(f_wkvx[:, :], bank[0:NS, 3, T:2 * T], f_bias[:, 1:2],
                                                   f_k[:, p1, :], ALU.add, ALU.mult).then_inc(f_wkvx_ready, 1)
                    dve.wait_ge(f_wkvx_ready, n)
                    await_count(dve, f_out_in_psum, n - 2)
                    nc.vector.tensor_tensor_scan(f_state[:, p1, :], f_decay[:, :], f_wkvx[:, :], 0.0,
                                                 ALU.mult, ALU.add).then_inc(f_state_ready, 1)
                if live(n, 2):
                    dve.wait_ge(x_ready, done + n - 1)
                    stats(dve, count, n - 2)

            seq = lambda ins: (count.did(ins), count.sync(dve))
            tt, ts = nc.vector.tensor_tensor, nc.vector.tensor_scalar
            dve.wait_ge(f_gate_exp, 1)
            count.did(ts(f_gate[:, 1, :], f_gate[:, 0, :], -1.0, 1.0, ALU.mult, ALU.add))
            for t in range(KT):
                count.did(tt(f_wshift[:, t, :], f_wshift[:, t, :], f_gate[:, 0, :], ALU.mult))
                count.did(ts(f_wkv[:, 1, t, :], f_wkv[:, 0, t, :], f_affine[:, 0, t:t + 1], None, ALU.mult))
            count.did(ts(f_decay[:, :], table("ones", NS), f_time[:, 2:3], None, ALU.mult))
            seq(ts(f_time[:, 3:4], f_time[:, 3:4], -1.0, None, ALU.mult))
            dve.wait_ge(f_pe, 1)
            seq(nc.vector.tensor_copy(f_bias[:, 0:2], bank[0:NS, 3, 0:2]))
            ts(f_bias[:, 2:3], f_bias[:, 0:1], -1.0, None, ALU.mult).then_inc(f_setup, 1)
            pipeline(dve, step, 4, 2, 2, count, 3 + 2)

        def shift_gpsimd(pool, done, rdone):
            def step(n, u, uses):
                p0 = u % 2
                if live(n, 0):
                    pool.wait_ge(f_var_ready, n + 1)
                    await_count(pool, f_z_ready, n - 1)
                    nc.gpsimd.tensor_tensor(f_rstd[:, p0:p0 + 1], f_var[:, p0:p0 + 1], minus_half[:, 0:1],
                                            ALU.pow).then_inc(f_rstd_ready, 1)
                if live(n, 2):
                    pool_rstd(pool, n - 2, rdone + NB)

            pipeline(pool, step, 4, 2, 2)

        def mlp_tensor(pe, done):
            def turned(n, u, i):
                idx = PAIRS * (n - 1) + i
                pe.wait_ge(l_hid_ready, idx + 1)
                await_count(pe, l_hidT_ready, idx if i == 0 else idx - 1)
                for e in range(2 * i, min(2 * i + 2, EXS)):
                    mm = nc.tensor.transpose(bank[:, 4 + i % 2, (e % 2) * T:(e % 2 + 1) * T],
                                             l_hid[:, i % 2, (e % 2) * I1:(e % 2 + 1) * I1], ident)
                mm.then_inc(l_hidT_in_psum, 1)

            def step(n, u, uses):
                p0, p1, p2 = u % 2, (u - 1) % 2, u % 2
                if live(n, 0):
                    pe.wait_ge(l_h_ready, n + 1)
                    await_count(pe, l_hT_ready, n)
                    for t in range(KT):
                        mm = nc.tensor.transpose(bank[:, 0, t * T:(t + 1) * T],
                                                 l_h[:, p0, t * 128:(t + 1) * 128], ident)
                    mm.then_inc(l_hT_in_psum, 1)
                for i in range(PAIRS):
                    if live(n, 1):
                        idx = PAIRS * (n - 1) + i
                        await_count(pe, l_hid_ready, idx if i == 0 else idx - 1)
                        w = 2 * I1 * (min(2 * i + 2, EXS) - 2 * i)
                        for t in range(KT):
                            mm = nc.tensor.matmul(
                                bank[:, 2 + i % 2, 0:w], l_hT[:, p1, t, :],
                                wgu[:, 2 * i:min(2 * i + 2, EXS), t, :], start=(t == 0), stop=(t == KT - 1))
                        mm.then_inc(l_gu_in_psum, 1)
                        if i >= 1:
                            turned(n, u, i - 1)
                    if i == 1 and live(n, 0):
                        pe.wait_ge(l_hT_ready, n + 1)
                        await_count(pe, l_prob_ready, n)
                        for t in range(KT):
                            mm = nc.tensor.matmul(bank[:, 1, 0:EX1], l_hT[:, p0, t, :], l_wr[:, t, :],
                                                  start=(t == 0), stop=(t == KT - 1))
                        mm.then_inc(l_logit_in_psum, 1)
                if live(n, 2):
                    pe.wait_ge(l_hidT_ready, PAIRS * (n - 1))
                    await_count(pe, x_ready, done + n - 2)
                    for e in range(EXS):
                        mm = nc.tensor.matmul(bank[:, 6, 0:D], l_hidT[:, p2, e, :], wdn[:, e, :],
                                              start=(e == 0), stop=(e == EXS - 1))
                    mm.then_inc(l_out_in_psum, 1)
                if live(n, 1):
                    turned(n, u, PAIRS - 1)

            pe.wait_ge(x_ready, done)
            pe.wait_ge(l_loaded, 16 * 6)
            pipeline(pe, step, 4, 2, 2)

        def mlp_scalar(act, done):
            def step(n, u, uses):
                p0, p1 = u % 2, (u - 1) % 2
                for i in range(PAIRS):
                    if live(n, 1):
                        idx = PAIRS * (n - 1) + i
                        act.wait_ge(l_gu_in_psum, idx + 1)
                        if i == 0:
                            act.wait_ge(l_p_ready, n)
                        await_count(act, l_hid_ready, idx if i == 0 else idx - 1)
                        for e in range(2 * i, min(2 * i + 2, EXS)):
                            c = (e % 2) * I1
                            ins = nc.scalar.activation(l_sig[:, i % 2, c:c + I1],
                                                       bank[:, 2 + i % 2, 2 * c:2 * c + I1],
                                                       ACT.Sigmoid, scale=l_p[:, p1, e:e + 1])
                            ins.then_inc(l_sig_ready, 1)
                    if i == 0 and live(n, 0):
                        act.wait_ge(l_hT_in_psum, n + 1)
                        await_count(act, l_gu_in_psum, PAIRS * (n - 1))
                        nc.scalar.copy(l_hT[:, p0].rearrange("p t c -> p (t c)"),
                                       bank[:, 0, 0:D]).then_inc(l_hT_ready, 1)
                    if i == 2 and live(n, 0):
                        act.wait_ge(l_logit_ready, n + 1)
                        await_count(act, l_p_ready, n)
                        nc.scalar.activation(l_prob[:, :], bank[:, 1, 0:EX1],
                                             ACT.Sigmoid).then_inc(l_prob_ready, 1)
                    if i >= 1 and live(n, 1):
                        copy_hidden(act, n, u, i - 1)
                if live(n, 1):
                    copy_hidden(act, n, u, PAIRS - 1)

            def copy_hidden(act, n, u, i):
                act.wait_ge(l_hidT_in_psum, PAIRS * (n - 1) + i + 1)
                if i == 0:
                    await_count(act, l_out_in_psum, n - 2)
                hi = min(2 * i + 2, EXS)
                nc.scalar.copy(l_hidT[:, (u - 1) % 2, 2 * i:hi, :].rearrange("p e c -> p (e c)"),
                               bank[:, 4 + i % 2, 0:(hi - 2 * i) * T]).then_inc(l_hidT_ready, 1)

            nc.scalar.preload_act_table(ACT.Sigmoid)
            pipeline(act, step, 4, 2, 1)

        def mlp_vector(dve, done, rdone):
            count = Count(l_dve)

            def step(n, u, uses):
                p0, p1 = u % 2, (u - 1) % 2
                if live(n, 0):
                    dve.wait_ge(rstd_ready, rdone + n + 1)
                    await_count(dve, l_hT_in_psum, n - 1)
                    nc.vector.tensor_scalar(
                        l_h[:, p0, :], x_sb[:, n, :], moments[:, n, 0:1],
                        rstd[:, bass.ds(n, 1)], ALU.subtract, ALU.mult).then_inc(l_h_ready, 1)
                for i in range(PAIRS):
                    if live(n, 1):
                        idx = PAIRS * (n - 1) + i
                        last = min(2 * i + 2, EXS)
                        dve.wait_ge(l_sig_ready, EXS * (n - 1) + last)
                        await_count(dve, l_hidT_in_psum, idx if i == 0 else idx - 1)
                        for e in range(2 * i, last):
                            c = (e % 2) * I1
                            count.did(nc.vector.scalar_tensor_tensor(
                                l_sig[:, i % 2, c:c + I1], bank[:, 2 + i % 2, 2 * c:2 * c + I1],
                                l_p[:, p1, e:e + 1], l_sig[:, i % 2, c:c + I1], ALU.mult, ALU.mult))
                        count.sync(dve)
                        for e in range(2 * i, last):
                            c = (e % 2) * I1
                            ins = nc.vector.scalar_tensor_tensor(
                                l_hid[:, i % 2, c:c + I1], bank[:, 2 + i % 2, 2 * c + I1:2 * c + 2 * I1],
                                l_p[:, p1, e:e + 1], l_sig[:, i % 2, c:c + I1], ALU.mult, ALU.mult)
                            if e == last - 1:
                                ins.then_inc(l_hid_ready, 1)
                            else:
                                count.did(ins)
                    if i == 2 and live(n, 0):
                        dve.wait_ge(l_logit_in_psum, n + 1)
                        nc.vector.tensor_copy(l_logit[:, :], bank[:, 1, 0:EX1]).then_inc(l_logit_ready, 1)
                        dve.wait_ge(l_logit_ready, n + 1)
                        hold(dve)
                        count.did(nc.vector.max(l_top[:, :], l_logit[:, :]))
                        count.sync(dve)
                        hold(dve)
                        count.did(nc.vector.max_index(l_topi[:, :], l_top[:, :], l_logit[:, :]))
                        count.sync(dve)
                        count.did(nc.vector.tensor_copy(l_pick[:, :], l_topi[:, 0:TOP1]))
                        count.sync(dve)
                        for k in range(TOP1):
                            count.did(nc.vector.tensor_scalar(l_mask[:, k, :], table("iota32")[:, 0:EX1],
                                                              l_pick[:, k:k + 1], None, ALU.is_equal))
                        count.sync(dve)
                        count.did(nc.vector.tensor_tensor(l_mask[:, 0, :], l_mask[:, 0, :], l_mask[:, 1, :],
                                                          ALU.add))
                        count.sync(dve)
                        dve.wait_ge(l_prob_ready, n + 1)
                        nc.vector.tensor_tensor(l_p[:, p0, 0:EX1], l_mask[:, 0, :], l_prob[:, :],
                                                ALU.mult).then_inc(l_p_ready, 1)
                if live(n, 2):
                    dve.wait_ge(l_out_in_psum, n - 1)
                    nc.vector.tensor_tensor(x_sb[:, n - 2, :], bank[:, 6, 0:D], x_sb[:, n - 2, :],
                                            ALU.add).then_inc(x_ready, 1)

            count.did(nc.vector.memset(l_p[:, :, EX1:EXS], 1.0))
            pipeline(dve, step, 4, 2, 2, count, EXS + PAIRS - 1 + 6)

        @block.tensor
        def _(pe):
            attn_tensor(pe)
            cross_tensor(pe, 0, NB, NB)
            shared_tensor(pe, 2 * NB)
            expert_tensor(pe)
            shift_tensor(pe, 4 * NB)
            cross_tensor(pe, 1, 5 * NB, 4 * NB)
            mlp_tensor(pe, 6 * NB)

        @block.scalar
        def _(act):
            attn_scalar(act)
            cross_scalar(act, 0, NB, NB)
            shared_scalar(act, 2 * NB)
            expert_scalar(act)
            shift_scalar(act, 4 * NB)
            cross_scalar(act, 1, 5 * NB, 4 * NB)
            mlp_scalar(act, 6 * NB)

        @block.vector
        def _(dve):
            attn_vector(dve)
            cross_vector(dve, 0, NB, NB)
            shared_vector(dve, 2 * NB)
            expert_vector(dve)
            collect_vector(dve, 3 * NB)
            shift_vector(dve, 4 * NB, 3 * NB)
            cross_vector(dve, 1, 5 * NB, 4 * NB)
            mlp_vector(dve, 6 * NB, 5 * NB)

        @block.gpsimd
        def _(pool):
            nc.gpsimd.memset(minus_half[:, :], -0.5).then_inc(const_ready, 1)
            nc.gpsimd.memset(zero_eps[:, 0:1], 0.0).then_inc(const_ready, 1)
            nc.gpsimd.memset(zero_eps[:, 1:2], EPS).then_inc(const_ready, 1)
            pool.wait_ge(const_ready, 3)
            attn_gpsimd(pool)
            nc.gpsimd.memset(c_vT[:, :, :, :, :], 0.0).then_inc(pad_ready, 1)
            for b in range(NB):
                pool_rstd(pool, b, NB)
            nc.gpsimd.memset(g_y[:, :, :, :], 0.0).then_inc(y_zero, 1)
            cross_gpsimd(pool, 0, NB, NB)
            dispatch_gpsimd(pool)
            collect_gpsimd(pool, 3 * NB)
            shift_gpsimd(pool, 4 * NB, 3 * NB)
            cross_gpsimd(pool, 1, 5 * NB, 4 * NB)

        @block.sync
        def _(sp):
            sp.dma_start(const[:, :], A["const"]).then_inc(const_loaded, 16)
            for q in range(4):
                sp.dma_start(x_sb[:, 4 * q:4 * q + 4, :],
                             A["x"][4 * q:4 * q + 4].rearrange("b t d -> t b d")).then_inc(x_loaded, 16)
            for t, name in ((wqk[:, :, 0:D], "wqT"), (wqk[:, :, D:2 * D], "wkT"), (wv[:, :, :], "wvT"),
                            (wo[:, :, :], "woT")):
                sp.dma_start(t, A[name].rearrange("(t p) o -> p t o", p=128)).then_inc(w_loaded, 16)
            sp.dma_start(bern[:, 0, :], A["bern_u"].to_broadcast([NK0, H0])).then_inc(w_loaded, 16)
            sp.wait_ge(x_ready, NB)
            for t, name in ((m_wr, "routerT"), (m_wgu, "shared_guT"), (m_wdn, "shared_downT")):
                sp.dma_start(t[:, :, :], A[name].rearrange("(t p) o -> p t o", p=128)
                             ).then_inc(m_w_loaded, 16)
            sp.dma_start(m_bias[:, :], A["e_bias"].to_broadcast([128, EX0])).then_inc(m_w_loaded, 16)
            for e in range(RING):
                load_expert(sp, e, e)
            for t, name in ((f_wshift[:, :, :], "shiftT"), (f_wkv[:, 0], "kvT")):
                sp.dma_start(t, A[name].rearrange("(t p) o -> p t o", p=128)).then_inc(f_loaded, 16)
            sp.dma_start(f_wo[:, :], A["outT"]).then_inc(f_loaded, 16)
            sp.dma_start(f_gate[:, 0, :], A["gate"].to_broadcast([128, D])).then_inc(f_loaded, 16)
            for i, name in enumerate(("ln_gamma", "ln_beta")):
                sp.dma_start(f_affine[:, i, :], A[name]).then_inc(f_loaded, 16)
            for i, name in enumerate(("time_decay", "time_first")):
                sp.dma_start(f_time[:, i:i + 1], A[name]).then_inc(f_loaded, 16)
            sp.wait_ge(y_zero, 1)
            for i in range(5):
                sp.dma_start(xp_dram[bass.ds(i * 512, 512), :].rearrange("(p r) d -> p (r d)", p=128),
                             g_y[:, i % GB].rearrange("p k d -> p (k d)")).then_inc(slots_zero, 16)
            cross_sync(sp, 0, NB, NB)
            expert_sync(sp)
            sp.wait_ge(d_y_in_psum, EX0)
            sp.dma_start(l_wr[:, :, :], A["router1"].rearrange("(t p) o -> p t o", p=128)
                         ).then_inc(l_loaded, 16)
            for t in range(KT):
                sp.dma_start(wgu[:, 0:EX1, t, :],
                             A["gate_up"][:, t * 128:(t + 1) * 128, :].rearrange("e p i -> p e i")
                             ).then_inc(l_loaded, 16)
            sp.dma_start(wgu[:, EX1], A["shared1_gu"].rearrange("(t p) i -> p t i", p=128)
                         ).then_inc(l_loaded, 16)
            sp.dma_start(wdn[:, 0:EX1, :], A["down"].rearrange("e p o -> p e o")).then_inc(l_loaded, 16)
            sp.dma_start(wdn[:, EX1, :], A["shared1_down"]).then_inc(l_loaded, 16)
            cross_sync(sp, 1, 5 * NB, 4 * NB)
            for q in range(NB // 2):
                sp.wait_ge(x_ready, 6 * NB + 2 * q + 2)
                sp.dma_start(out[2 * q:2 * q + 2].rearrange("b t d -> t b d"),
                             x_sb[:, 2 * q:2 * q + 2, :]).then_inc(out_stored, 16)
            sp.wait_ge(out_stored, 16 * (NB // 2))


def kernel(**inputs):
    import numpy as np
    import concourse.bacc as bacc
    from concourse import mybir as mb
    from concourse.bass_utils import run_bass_kernel_spmd

    laid = layout(inputs)
    nc = bacc.Bacc("TRN2", target_bir_lowering=False, num_devices=1)
    arrays, A = {}, {}
    for name, a in laid.items():
        a = np.ascontiguousarray(a)
        arrays[f"in_{name}"] = a
        A[name] = nc.dram_tensor(f"in_{name}", a.shape, mb.dt.from_np(a.dtype), kind="ExternalInput").ap()
    out = nc.dram_tensor("out_0", (NB, T, D), F32, kind="ExternalOutput").ap()
    decoder_kernel(nc, A, out)
    r = run_bass_kernel_spmd(nc, [arrays], core_ids=[0])
    return r.results[0]["out_0"]


def layout(inputs):
    import numpy as np

    i = {k: np.asarray(v) for k, v in inputs.items()}
    return {
        "x": i["x"], "context": i["ctx_2048"], "contextT": i["ctx_2048"].transpose(0, 2, 1), "const": constants(),
        "wqT": i["L0_attn_wq"].T, "wkT": i["L0_attn_wk"].T, "wvT": i["L0_attn_wv"].T,
        "routerT": i["L0_ffn_router_w"].T, "e_bias": i["L0_ffn_e_bias"][None],
        "shared_guT": np.concatenate([i["L0_ffn_shared_gate"].T, i["L0_ffn_shared_up"].T], axis=1),
        "shared_downT": i["L0_ffn_shared_down"].T,
        "W_gu": np.concatenate([i["L0_ffn_W_gate"], i["L0_ffn_W_up"]], axis=2),
        "W_down": i["L0_ffn_W_down"],
        "shiftT": i["L1_attn_W_shift"].T,
        "kvT": np.concatenate([i["L1_attn_W_key"].T, i["L1_attn_W_value"].T], axis=1),
        "outT": i["L1_attn_W_output"].T, "gate": i["L1_attn_gate"][None],
        "ln_gamma": i["L1_attn_ln_gamma"].reshape(KT, 128).T,
        "ln_beta": i["L1_attn_ln_beta"].reshape(KT, 128).T,
        "time_decay": i["L1_attn_time_decay"][:, None], "time_first": i["L1_attn_time_first"][:, None],
        "router1": i["L1_ffn_router_w"], "gate_up": i["L1_ffn_gate_up_w"], "down": i["L1_ffn_down_w"],
        "shared1_gu": np.concatenate([i["L1_ffn_shared_gate_w"], i["L1_ffn_shared_up_w"]], axis=1),
        "shared1_down": i["L1_ffn_shared_down_w"],
        "woT": i["L0_attn_wo"].T, "bern_u": i["L0_attn_bern_u"],
    }
```

```python
from contextlib import ExitStack

import concourse.bass as bass
from concourse import mybir

F32 = mybir.dt.float32
BF16 = mybir.dt.bfloat16
I32 = mybir.dt.int32
U32 = mybir.dt.uint32
ALU = mybir.AluOpType
ACT = mybir.ActivationFunctionType
AX = mybir.AxisListType

NB, T, D = 16, 128, 256
KT = D // 128
EPS = 1e-5

H0, HD0 = 16, 16
SINK = int(0.1 * T)
RECENT = int(0.5 * T)
REC0 = T - RECENT
NK0 = SINK + RECENT
HG = 128 // HD0

HX = 8
DX = T // HX
TERMS = 6
QPART = (0, 1, 2, 0, 1, 0)
KPART = (0, 0, 0, 1, 1, 2)
NSTACK = TERMS * DX


CONST_AT, CONST_COLS = {}, 0
for _name, _width in (("ident", 128), ("key_of_head", HG), ("spread", NK0), ("pick3", 3), ("ones", 128),
                      ("half_ones", 64), ("rope_cos", HD0), ("rope_sin", HD0), ("group_ones", 128),
                      ("before", 128), ("iota32", 32)):
    CONST_AT[_name] = (CONST_COLS, _width)
    CONST_COLS += _width


def constants():
    import numpy as np

    p = np.arange(128)
    t = {k: np.zeros((128, w), np.float32) for k, (_, w) in CONST_AT.items()}
    t["ident"][p, p] = 1
    t["key_of_head"][p, p // HD0] = 1
    t["spread"][SINK, SINK + 1:] = 1.0 / RECENT
    t["pick3"][SINK, 0] = 1
    t["pick3"][SINK + 1:NK0, 1] = 1
    t["pick3"][:NK0, 2] = 1
    t["ones"][:] = 1
    t["half_ones"][:, 0:16] = 1
    t["half_ones"][:, 48:64] = 1
    freq = 1.0 / np.float32(10000.0) ** (np.arange(0, HD0, 2, dtype=np.float32) / HD0)
    angle = (p.astype(np.float32)[:, None] * freq[None, :].astype(np.float32)).astype(np.float32)
    t["rope_cos"][:] = np.tile(np.cos(angle), 2)
    t["rope_sin"][:] = np.concatenate([-np.sin(angle), np.sin(angle)], axis=1)
    t["group_ones"][:] = p[:, None] // DX == p[None, :] // DX
    t["iota32"][:] = np.arange(32)
    t["before"][:] = p[:, None] < p[None, :]
    return np.concatenate([t[k] for k in CONST_AT], axis=1)


EX0, TOP0, GROUPS, TOPG = 32, 4, 8, 3
CAP = -(-5 * NB * T // (4 * EX0))
SLOTS = EX0 * CAP
I0 = 128
SH0 = 2 * I0
DROPPED = 8192.0
NS = 64
EX1, TOP1, I1 = 8, 2, 128
EXS = EX1 + 1


def await_count(eng, sem, count):
    if isinstance(count, int) and count <= 0:
        return
    eng.wait_ge(sem, count)


def hold(eng):
    eng.nop(nofuse=True)


def live(n, k, total=NB):
    return not isinstance(n, int) or 0 <= n - k < total


def seen(n, k=0):
    return min(n - k, NB - 1) + 1 if isinstance(n, int) else n - k + 1


class Count:

    def __init__(self, sem):
        self.sem, self.base, self.n = sem, 0, 0

    def did(self, ins):
        ins.then_inc(self.sem, 1)
        self.n += 1

    def sync(self, eng):
        await_count(eng, self.sem, self.base + self.n)


def pipeline(eng, step, head, unroll, last_phase, count=None, per_step=0, total=NB,
             past=0):
    def peeled(n):
        step(n, n, lambda k, m: (n - k + past) // m + 1)

    def looped(j, c):
        step(j * unroll + c, c, lambda k, m: j * (unroll // m) + ((c - k + past) // m + 1))

    for n in range(head):
        peeled(n)
    turns = (total - head) // unroll
    assert turns * unroll == total - head
    if count is not None:
        base, n0 = count.base + count.n, per_step * unroll
    with eng.Fori(0, turns) as j:
        if count is not None:
            count.base, count.n = j * n0 + base, 0
        for u in range(unroll):
            looped(j, head + u)
        if count is not None:
            assert count.n == n0, (count.n, n0)
    if count is not None:
        count.base, count.n = base + turns * n0, 0
    for n in range(total, total + last_phase):
        peeled(n)


def decoder_kernel(nc, A, out):
    with ExitStack() as ctx:
        def keep(name, shape, dt=F32):
            return ctx.enter_context(nc.sbuf_tensor(name, shape, dt))

        def sem(name):
            return ctx.enter_context(nc.semaphore(name))

        bank = ctx.enter_context(nc.psum_tensor("bank", [128, 8, 512], F32))
        x_sb = keep("x_sb", [128, NB, D])
        moments = keep("moments", [128, NB, 2])
        mean_var = keep("mean_var", [128, 2])
        zero_eps = keep("zero_eps", [128, 2])
        rstd = keep("rstd", [128, NB])
        minus_half = keep("minus_half", [128, 1])
        bn6 = keep("bn6", [128, 2, 6])
        const = keep("const", [128, CONST_COLS])

        def table(name, rows=128):
            at, width = CONST_AT[name]
            return const[0:rows, at:at + width]

        ident = table("ident")

        x_loaded = sem("x_loaded")
        const_loaded = sem("const_loaded")
        stats_ready = sem("stats_ready")
        rstd_ready = sem("rstd_ready")
        x_ready = sem("x_ready")
        out_stored = sem("out_stored")

        NBUF = 4
        STACK_DMAS = 6
        PART_DMAS = 6
        ORDER = (0, 2, 4, 6, 1, 3, 5, 7)
        c_rows = keep("c_rows", [128, 4, 2 * D])
        c_raw = c_rows[:, 0:2]
        c_unit = c_rows[:, 2:4]
        c_rest = keep("c_rest", [128, 2, 2 * D])
        c_part = keep("c_part", [128, 2, 3, 2 * D], BF16)
        q_stack = keep("q_stack", [128, NBUF, HX, D], BF16)
        k_stack = keep("k_stack", [128, NBUF, HX, D], BF16)
        c_vT_in = keep("c_vT_in", [128, 2, 2, T])
        c_vT = keep("c_vT", [128, 2, 2, HX, 32])
        c_max = keep("c_max", [128, 2, HX, 2])
        c_neg = keep("c_neg", [2 * HX, 3, 128], BF16)
        c_nrest = keep("c_nrest", [2 * HX, 2, 128])
        c_e = keep("c_e", [128, HX, 2, D])
        c_inv = keep("c_inv", [128, D])
        c_att = keep("c_att", [128, D])
        c_sq = keep("c_sq", [128, 2 * D])
        c_ss = keep("c_ss", [128, 2 * D])
        part_dram = nc.dram_tensor("part_dram", (2, 2, 3 * DX, HX, D), BF16).ap()
        neg_dram = nc.dram_tensor("neg_dram", (2, 2 * HX, 3, 128), BF16).ap()
        pad_ready = sem("pad_ready")

        cross = {k: [sem(f"c_{k}{i}") for i in range(m)] for k, m in (
            ("ctx_in", 2), ("vT_in", 2), ("neg_in", NBUF), ("stack_in", NBUF))}
        cross |= {k: sem(f"c_{k}") for k in (
            "dve", "act", "h_ready", "sq_ready", "ss_in_psum", "ss_ready", "inv_norm", "unit_ready",
            "hi", "rest1", "mid", "rest2", "lo", "part_stored", "s_in_psum", "max_ready",
            "maxT_in_psum", "neg_ready", "neg_stored", "sT_in_psum", "e_ready", "pv_done",
            "vT_ready", "inv_ready")}
        cross_count = {k: Count(cross[k]) for k in ("dve", "act")}

        scope = ExitStack()

        def sb(name, shape, dt=F32):
            return scope.enter_context(nc.sbuf_tensor(name, shape, dt))

        wqk = sb("wqk", [128, KT, 2 * D])
        wv = sb("wv", [128, KT, D])
        wo = sb("wo", [128, KT, D])
        rope_cos, rope_sin = table("rope_cos"), table("rope_sin")
        key_of_head = table("key_of_head")
        spread = table("spread", NK0)
        pick3 = table("pick3", NK0)
        ones = table("ones")
        half_ones = table("half_ones").rearrange("p (o c) -> p o c", o=2)
        bern = sb("bern", [NK0, 3, H0])
        a_h = sb("a_h", [128, 2, D])
        a_hT = sb("a_hT", [128, 2, KT, T])
        a_hTk = sb("a_hTk", [128, 2, KT, NK0])
        a_v = sb("a_v", [NK0, 2, D])
        a_rot = sb("a_rot", [128, 2 * D])
        a_cos = sb("a_cos", [128, 2 * D])
        a_qk = sb("a_qk", [128, 2, 2 * D])
        a_qT = sb("a_qT", [128, 2, KT, T])
        a_kb = sb("a_kb", [128, 2, KT, HG, NK0])
        a_max = sb("a_max", [128, H0])
        a_p = sb("a_p", [128, 2, H0, NK0])
        a_pT = sb("a_pT", [NK0, H0, T])
        a_e3 = sb("a_e3", [NK0, 3, H0])
        a_lim = sb("a_lim", [NK0, 3, H0])
        a_add = sb("a_add", [NK0, D])
        a_vp = sb("a_vp", [NK0, H0, 32])
        a_inv = sb("a_inv", [128, 2 * T])
        a_oT = sb("a_oT", [128, 2, KT, T])
        w_loaded = sem("w_loaded")
        const_ready = sem("const_ready")
        a_dve = sem("a_dve")
        a_act = sem("a_act")
        a_h_ready = sem("a_h_ready")
        a_hT_in_psum = sem("a_hT_in_psum")
        a_hT_ready = sem("a_hT_ready")
        a_qkv_in_psum = sem("a_qkv_in_psum")
        a_v_ready = sem("a_v_ready")
        a_qk_ready = sem("a_qk_ready")
        a_qkT_in_psum = sem("a_qkT_in_psum")
        a_qT_ready = sem("a_qT_ready")
        a_kb_ready = sem("a_kb_ready")
        a_s_in_psum = sem("a_s_in_psum")
        a_s_shifted = sem("a_s_shifted")
        a_p_ready = sem("a_p_ready")
        a_pT_in_psum = sem("a_pT_in_psum")
        a_pT_ready = sem("a_pT_ready")
        a_e3_ready = sem("a_e3_ready")
        a_spread_in_psum = sem("a_spread_in_psum")
        a_vp_ready = sem("a_vp_ready")
        a_o_in_psum = sem("a_o_in_psum")
        a_inv_ready = sem("a_inv_ready")
        a_oT_ready = sem("a_oT_ready")
        a_out_in_psum = sem("a_out_in_psum")

        scope.close()
        ctx.callback(scope.close)

        h_all = sb("h_all", [128, NB, D])
        m_hc = sb("m_hc", [128, 2, D])
        RING = 8
        wgu = sb("wgu", [128, EXS, KT, 2 * I0])
        wdn = sb("wdn", [128, EXS, D])
        m_wr = sb("m_wr", [128, KT, EX0])
        m_wgu = sb("m_wgu", [128, KT, 2 * SH0])
        m_wdn = sb("m_wdn", [128, KT, D])
        m_hT = sb("m_hT", [128, 2, KT, T])
        m_sig = sb("m_sig", [128, 2, SH0])
        m_hid = sb("m_hid", [128, 2, SH0])
        m_hidT = sb("m_hidT", [128, KT, T])
        m_bias = sb("m_bias", [128, EX0])
        m_s = sb("m_s", [128, NB, EX0])
        m_t = [c_e[:, i * HX // 2:(i + 1) * HX // 2].rearrange("p h o (b e) -> p (h o b) e", e=EX0)
               .rearrange("p (b k) e -> p b k e", k=TOP0) for i in range(2)]
        m_hot = c_rows[:, :, :].rearrange("p a (b k e) -> p (a b) k e", k=TOP0, e=EX0)
        m_g = [sb(f"m_g{i}", [128, NB, GROUPS]) for i in range(6)]
        m_top = sb("m_top", [128, NB, 8])
        m_topi = sb("m_topi", [128, NB, 8], U32)
        m_pick = sb("m_pick", [128, NB, TOP0])
        m_w = sb("m_w", [128, NB, TOP0])
        m_k = [sb(f"m_k{i}", [128, NB, TOP0]) for i in range(3)]
        m_sum = sb("m_sum", [128, NB])
        m_slot = sb("m_slot", [128, NB, TOP0], U32)
        XBUF = 4
        STORE = 5
        GU = (1, 4)
        d_x = sb("d_x", [CAP, XBUF, D])
        d_xT = sb("d_xT", [128, 2, KT, CAP])
        d_sig = sb("d_sig", [CAP, I0])
        d_hid = sb("d_hid", [CAP, 2, I0])
        d_hidT = sb("d_hidT", [128, 2, CAP])
        d_y = sb("d_y", [CAP, 2, D])
        GB = 2
        g_y = sb("g_y", [128, GB, TOP0, D])
        xp_dram = nc.dram_tensor("xp_dram", (SLOTS, D), F32).ap()
        y_dram = nc.dram_tensor("y_dram", (SLOTS, D), F32).ap()
        m_w_loaded = sem("m_w_loaded")
        ring_in = [sem(f"ring_in{i}") for i in range(RING)]
        slots_zero, y_zero, y_used = sem("slots_zero"), sem("y_zero"), sem("y_used")
        m_dve, e_dve, r_dve, f_dve, l_dve, l_act = (sem(x) for x in (
            "m_dve", "e_dve", "r_dve", "f_dve", "l_dve", "l_act"))
        (m_h_ready, m_hT_in_psum, m_hT_ready, m_gu_in_psum, m_sig_ready, m_hid_ready, m_hidT_in_psum,
         m_hidT_ready, m_out_in_psum, m_s_ready, m_hot_ready, m_rank_in_psum, m_slot_ready, rows_sent) = (
            sem(x) for x in (
                "m_h_ready", "m_hT_in_psum", "m_hT_ready", "m_gu_in_psum", "m_sig_ready", "m_hid_ready",
                "m_hidT_in_psum", "m_hidT_ready", "m_out_in_psum", "m_s_ready", "m_hot_ready",
                "m_rank_in_psum", "m_slot_ready", "rows_sent"))
        d_x_in = [sem(f"d_x_in{i}") for i in range(XBUF)]
        (d_xT_in_psum, d_xT_ready, d_gu_in_psum, d_sig_ready, d_hid_ready, d_hidT_in_psum, d_hidT_ready,
         d_y_in_psum, d_y_ready) = (sem(x) for x in (
             "d_xT_in_psum", "d_xT_ready", "d_gu_in_psum", "d_sig_ready", "d_hid_ready", "d_hidT_in_psum",
             "d_hidT_ready", "d_y_in_psum", "d_y_ready"))
        y_stored = [sem(f"y_stored{i}") for i in range(2)]
        y_in = [sem(f"y_in{i}") for i in range(4)]

        f_wshift = sb("f_wshift", [128, KT, D])
        f_wkv = sb("f_wkv", [128, 2, KT, 2 * NS])
        f_wo = sb("f_wo", [NS, D])
        f_gate = sb("f_gate", [128, 2, D])
        f_affine = sb("f_affine", [128, 2, KT])
        f_time = sb("f_time", [NS, 4])
        f_decay = sb("f_decay", [NS, T])
        f_bias = sb("f_bias", [NS, 3])
        f_h = h_all[:, 10:12, :]
        f_hT = h_all[:, 12:14, :].rearrange("p b (t c) -> p b t c", t=KT)
        f_part = sb("f_part", [128, D])
        f_xs = h_all[:, 14:16, :]
        f_mom = sb("f_mom", [128, 2, 2])
        f_var = sb("f_var", [128, 2])
        f_rstd = sb("f_rstd", [128, 2])
        f_z = sb("f_z", [128, D])
        f_zT = sb("f_zT", [128, KT, T])
        f_k = sb("f_k", [NS, 2, T])
        f_wkvx = sb("f_wkvx", [NS, T])
        f_state = sb("f_state", [NS, 2, T])
        (f_loaded, f_act, f_pe, f_h_ready, f_hT_in_psum, f_hT_ready, f_shift_in_psum, f_xs_ready, f_var_ready,
         f_rstd_ready, f_z_ready, f_zT_in_psum, f_zT_ready, f_kv_in_psum, f_k_ready, f_wkvx_ready,
         f_state_ready, f_out_in_psum, f_gate_exp, f_setup) = (sem(x) for x in (
             "f_loaded", "f_act", "f_pe", "f_h_ready", "f_hT_in_psum", "f_hT_ready", "f_shift_in_psum",
             "f_xs_ready", "f_var_ready", "f_rstd_ready", "f_z_ready", "f_zT_in_psum", "f_zT_ready",
             "f_kv_in_psum", "f_k_ready", "f_wkvx_ready", "f_state_ready", "f_out_in_psum", "f_gate_exp",
             "f_setup"))
        PAIRS = -(-EXS // 2)
        l_wr = sb("l_wr", [128, KT, EX1])
        l_h = m_hc
        l_hT = m_hT
        l_logit = sb("l_logit", [128, EX1])
        l_top = sb("l_top", [128, 8])
        l_topi = sb("l_topi", [128, 8], U32)
        l_pick = sb("l_pick", [128, TOP1])
        l_mask = sb("l_mask", [128, TOP1, EX1])
        l_p = sb("l_p", [128, 2, EXS])
        l_prob = sb("l_prob", [128, EX1])
        l_sig = sb("l_sig", [128, 2, 2 * I1])
        l_hid = sb("l_hid", [128, 2, 2 * I1])
        l_hidT = h_all[:, 0:EXS, :].rearrange("p b (i c) -> p (b i) c", c=T).rearrange(
            "p (b e) c -> p b e c", b=2)
        (l_loaded, l_h_ready, l_hT_in_psum, l_hT_ready, l_logit_in_psum, l_logit_ready, l_prob_ready, l_p_ready,
         l_gu_in_psum, l_sig_ready, l_hid_ready, l_hidT_in_psum, l_hidT_ready, l_out_in_psum) = (
             sem(x) for x in (
                 "l_loaded", "l_h_ready", "l_hT_in_psum", "l_hT_ready", "l_logit_in_psum", "l_logit_ready",
                 "l_prob_ready", "l_p_ready", "l_gu_in_psum", "l_sig_ready", "l_hid_ready", "l_hidT_in_psum",
                 "l_hidT_ready", "l_out_in_psum"))

        block = ctx.enter_context(nc.Block())

        def stats(dve, count, b):
            hold(dve)
            count.did(nc.vector.bn_stats(bn6[:, 0, :], x_sb[:, b, :]))
            count.sync(dve)
            hold(dve)
            count.did(nc.vector.bn_aggr(mean_var[:, :], bn6[:, 0, :]))
            count.sync(dve)
            nc.vector.tensor_tensor(moments[:, b, :], mean_var[:, :], zero_eps[:, :],
                                    ALU.add).then_inc(stats_ready, 1)

        def pool_rstd(pool, b, done):
            await_count(pool, stats_ready, done + b + 1)
            nc.gpsimd.tensor_tensor(rstd[:, bass.ds(b, 1)], moments[:, b, 1:2], minus_half[:, 0:1],
                                    ALU.pow).then_inc(rstd_ready, 1)

        s_bank = bank[:, 4:8, 0:4 * NK0].rearrange("p b (h k) -> p b h k", h=4)

        def attn_tensor(pe):
            def step(n, u, uses):
                p0, p1, p2, p3 = u % 2, (u - 1) % 2, u % 2, (u - 1) % 2
                if live(n, 1):
                    pe.wait_ge(a_qk_ready, n)
                    await_count(pe, a_oT_ready, n - 2)
                    for t in range(2 * KT):
                        mm = nc.tensor.transpose(bank[:, 3, t * T:(t + 1) * T],
                                                 a_qk[:, p1, t * 128:(t + 1) * 128], ident)
                    mm.then_inc(a_qkT_in_psum, 1)
                if live(n, 2):
                    pe.wait_ge(a_p_ready, n - 1)
                    for h in range(H0):
                        mm = nc.tensor.transpose(
                            bank[0:NK0, 4 + h // 4, (h % 4) * T:(h % 4 + 1) * T], a_p[:, p2, h, :],
                            ident)
                        if h % 4 == 3:
                            mm.then_inc(a_pT_in_psum, 1)
                if live(n, 0):
                    pe.wait_ge(a_h_ready, n + 1)
                    await_count(pe, x_ready, n - 3)
                    for t in range(KT):
                        mm = nc.tensor.transpose(bank[:, 0, t * T:(t + 1) * T],
                                                 a_h[:, p0, t * 128:(t + 1) * 128], ident)
                    mm.then_inc(a_hT_in_psum, 1)
                if live(n, 3):
                    pe.wait_ge(a_oT_ready, n - 2)
                    await_count(pe, a_hT_ready, 3 * seen(n))
                    for t in range(KT):
                        mm = nc.tensor.matmul(bank[:, 0, 0:D], a_oT[:, p3, t, :], wo[:, t, :],
                                              start=(t == 0), stop=(t == KT - 1))
                    mm.then_inc(a_out_in_psum, 1)
                if live(n, 0):
                    pe.wait_ge(a_hT_ready, 3 * (n + 1))
                    await_count(pe, a_qk_ready, n)
                    for t in range(KT):
                        nc.tensor.matmul(bank[:, 1, :], a_hT[:, p0, t, :], wqk[:, t, :],
                                         start=(t == 0), stop=(t == KT - 1))
                    await_count(pe, a_v_ready, n)
                    for t in range(KT):
                        mm = nc.tensor.matmul(bank[0:NK0, 2, 0:D], a_hTk[:, p0, t, :], wv[:, t, :],
                                              start=(t == 0), stop=(t == KT - 1))
                    mm.then_inc(a_qkv_in_psum, 1)
                if live(n, 2):
                    pe.wait_ge(a_e3_ready, n - 1)
                    await_count(pe, x_ready, seen(n, 3))
                    nc.tensor.matmul(bank[0:NK0, 0, 0:D], spread, a_v[:, p2, :],
                                     start=True, stop=True)
                    mm = nc.tensor.matmul(bank[0:NK0, 0, D:D + 3 * H0], ones[0:NK0, 0:NK0],
                                          a_e3[:, :, :].rearrange("p a h -> p (a h)"),
                                          start=True, stop=True)
                    mm.then_inc(a_spread_in_psum, 1)
                if live(n, 1):
                    pe.wait_ge(a_kb_ready, 2 * n)
                    pe.wait_ge(a_qT_ready, n)
                    await_count(pe, a_pT_ready, 4 * seen(n, 2))
                    for g in range(KT):
                        for half in range(2):
                            mm = nc.tensor.matmul(
                                s_bank[:, 2 * g + half, :, :], a_qT[:, p1, g, :],
                                a_kb[:, p1, g, 4 * half:4 * half + 4, :], start=True, stop=True)
                    mm.then_inc(a_s_in_psum, 1)
                if live(n, 2):
                    pe.wait_ge(a_vp_ready, 2 * (n - 1))
                    await_count(pe, a_qT_ready, seen(n, 1))
                    await_count(pe, a_kb_ready, 2 * seen(n, 1))
                    for g in range(KT):
                        for den in range(2):
                            col = (den * KT + g) * T
                            for odd in range(2):
                                for j in range(4):
                                    h = HG * g + 2 * j + odd
                                    w = half_ones[0:NK0, odd, :] if den else a_vp[:, h, :]
                                    mm = nc.tensor.matmul(
                                        bank[32 * j:32 * j + 32, 3, col:col + T], w, a_pT[:, h, :],
                                        start=(odd == 0), stop=(odd == 1))
                    mm.then_inc(a_o_in_psum, 1)

            pe.wait_ge(const_loaded, 16)
            pe.wait_ge(w_loaded, 16 * 5)
            pipeline(pe, step, 4, 2, 3)

        def attn_scalar(act):
            nc.scalar.preload_act_table_set("natural_log_exp_and_others")
            count = Count(a_act)

            def step(n, u, uses):
                p0, p1 = u % 2, (u - 1) % 2
                if live(n, 0):
                    act.wait_ge(a_hT_in_psum, n + 1)
                    await_count(act, a_qkv_in_psum, n - 1)
                    src = bank[:, 0, 0:D].rearrange("p (t c) -> p t c", t=KT)
                    nc.scalar.copy(a_hT[:, p0], src).then_inc(a_hT_ready, 1)
                    nc.scalar.copy(a_hTk[:, p0, :, 0:SINK], src[:, :, 0:SINK]).then_inc(a_hT_ready, 1)
                    nc.scalar.copy(a_hTk[:, p0, :, SINK:NK0], src[:, :, REC0:T]).then_inc(a_hT_ready, 1)
                if live(n, 1):
                    act.wait_ge(a_qkT_in_psum, n)
                    await_count(act, a_s_in_psum, n - 2)
                    nc.scalar.copy(a_qT[:, p1].rearrange("p t c -> p (t c)"),
                                   bank[:, 3, 0:KT * T]).then_inc(a_qT_ready, 1)
                if live(n, 2):
                    await_count(act, a_o_in_psum, n - 2)
                    for q in range(4):
                        act.wait_ge(a_pT_in_psum, 4 * (n - 2) + q + 1)
                        nc.scalar.copy(a_pT[:, 4 * q:4 * q + 4, :].rearrange("p h c -> p (h c)"),
                                       bank[0:NK0, 4 + q, :]).then_inc(a_pT_ready, 1)
                if live(n, 0):
                    act.wait_ge(a_qkv_in_psum, n + 1)
                    await_count(act, a_vp_ready, 2 * (n - 1))
                    nc.scalar.copy(a_v[:, p0, :], bank[0:NK0, 2, 0:D]).then_inc(a_v_ready, 1)
                if live(n, 1):
                    act.wait_ge(a_s_shifted, n)
                    nc.scalar.activation(a_p[:, p1], a_p[:, p1], ACT.Exp,
                                         scale=HD0 ** -0.5).then_inc(a_p_ready, 1)
                if live(n, 2):
                    act.wait_ge(a_o_in_psum, n - 1)
                    await_count(act, a_oT_ready, n - 2)
                    count.did(nc.scalar.activation(a_inv[:, :], bank[:, 3, KT * T:2 * KT * T], ACT.Ln))
                    count.sync(act)
                    nc.scalar.activation(a_inv[:, :], a_inv[:, :], ACT.Exp,
                                         scale=-1.0).then_inc(a_inv_ready, 1)

            pipeline(act, step, 4, 2, 3, count, 1)

        def attn_vector(dve):
            count = Count(a_dve)

            def step(n, u, uses):
                p0, p1, p2, p3 = u % 2, (u - 1) % 2, u % 2, (u - 1) % 2
                if live(n, 0):
                    dve.wait_ge(rstd_ready, n + 1)
                    await_count(dve, a_hT_in_psum, n - 1)
                    nc.vector.tensor_scalar(a_h[:, p0, :], x_sb[:, n, :], moments[:, n, 0:1],
                                            rstd[:, bass.ds(n, 1)], ALU.subtract, ALU.mult).then_inc(a_h_ready, 1)
                if live(n, 1):
                    dve.wait_ge(a_qT_ready, n)
                    await_count(dve, a_s_in_psum, n - 2)
                    kT = bank[:, 3, KT * T:2 * KT * T].rearrange("p (t c) -> p t c", t=KT)
                    for c0, c1, k0 in ((0, SINK, 0), (SINK, NK0, REC0)):
                        w = c1 - c0
                        nc.vector.tensor_tensor(
                            a_kb[:, p1, :, :, c0:c1],
                            kT[:, :, k0:k0 + w].unsqueeze(2).to_broadcast([128, KT, HG, w]),
                            key_of_head.unsqueeze(1).unsqueeze(3).to_broadcast([128, KT, HG, w]),
                            ALU.mult).then_inc(a_kb_ready, 1)
                if live(n, 3):
                    b = n - 3
                    dve.wait_ge(a_out_in_psum, n - 2)
                    nc.vector.tensor_tensor(x_sb[:, b, :], bank[:, 0, 0:D], x_sb[:, b, :],
                                            ALU.add).then_inc(x_ready, 1)
                if live(n, 2):
                    dve.wait_ge(a_pT_ready, 4 * (n - 1))
                    await_count(dve, a_spread_in_psum, n - 2)
                    nc.vector.tensor_tensor(
                        a_e3[:, :, :], a_pT[:, :, T - 1].unsqueeze(1).to_broadcast([NK0, 3, H0]),
                        pick3.unsqueeze(2).to_broadcast([NK0, 3, H0]),
                        ALU.mult).then_inc(a_e3_ready, 1)
                if live(n, 0):
                    dve.wait_ge(a_qkv_in_psum, n + 1)
                    await_count(dve, a_qkT_in_psum, n - 1)
                    heads = 2 * H0
                    raw = bank[:, 1, :].rearrange("p (h c) -> p h c", h=heads)
                    rot = a_rot[:, :].rearrange("p (h c) -> p h c", h=heads)
                    half = HD0 // 2
                    for c, s in ((0, half), (half, 0)):
                        count.did(nc.vector.tensor_tensor(
                            rot[:, :, c:c + half], raw[:, :, s:s + half],
                            rope_sin[:, c:c + half].unsqueeze(1).to_broadcast([128, heads, half]),
                            ALU.mult))
                    count.did(nc.vector.tensor_tensor(
                        a_cos[:, :].rearrange("p (h c) -> p h c", h=heads), raw,
                        rope_cos.unsqueeze(1).to_broadcast([128, heads, HD0]), ALU.mult))
                    count.sync(dve)
                    nc.vector.tensor_tensor(a_qk[:, p0, :], a_cos[:, :], a_rot[:, :],
                                            ALU.add).then_inc(a_qk_ready, 1)
                if live(n, 2):
                    dve.wait_ge(a_spread_in_psum, n - 1)
                    sums = bank[0:NK0, 0, D:D + 3 * H0].rearrange("p (a h) -> p a h", a=3)
                    count.did(nc.vector.tensor_scalar(a_lim[:, 0, :], sums[:, 1, :],
                                                      1.0 / (RECENT - 1), None, ALU.mult))
                    count.sync(dve)
                    count.did(nc.vector.scalar_tensor_tensor(
                        a_lim[:, 1, :], sums[:, 2, :], 1e-6, a_lim[:, 0, :], ALU.mult, ALU.add))
                    count.sync(dve)
                    count.did(nc.vector.tensor_tensor(a_lim[:, 2, :], a_lim[:, 1, :], bern[:, 2, :], ALU.mult))
                    count.sync(dve)
                    count.did(nc.vector.tensor_tensor(a_lim[:, 0, :], a_lim[:, 2, :], sums[:, 0, :],
                                                      ALU.is_lt))
                    count.sync(dve)
                    count.did(nc.vector.tensor_tensor(
                        a_add[:, :].rearrange("p (h c) -> p h c", h=H0),
                        bank[0:NK0, 0, 0:D].rearrange("p (h c) -> p h c", h=H0),
                        a_lim[:, 0, :].unsqueeze(2).to_broadcast([NK0, H0, HD0]), ALU.mult))
                    count.sync(dve)
                    await_count(dve, a_o_in_psum, n - 2)
                    for odd in range(2):
                        pick = [x.rearrange("p (j o c) -> p j o c", o=2, c=HD0)[:, :, odd, :]
                                for x in (a_add[:, :], a_v[:, p2, :])]
                        nc.vector.tensor_tensor(
                            a_vp[:, :, :].rearrange("p (j o) c -> p j o c", o=2)[
                                :, :, odd, HD0 * odd:HD0 * odd + HD0],
                            pick[0], pick[1], ALU.add).then_inc(a_vp_ready, 1)
                if live(n, 1):
                    dve.wait_ge(a_s_in_psum, n)
                    await_count(dve, a_pT_in_psum, 4 * (n - 2))
                    count.did(nc.vector.tensor_reduce(
                        a_max[:, :].rearrange("p (b h) -> p b h", b=4), s_bank, AX.X, ALU.max))
                    count.sync(dve)
                    nc.vector.tensor_tensor(
                        a_p[:, p1].rearrange("p (b h) k -> p b h k", b=4), s_bank,
                        a_max[:, :].rearrange("p (b h) -> p b h", b=4).unsqueeze(3)
                        .to_broadcast([128, 4, 4, NK0]), ALU.subtract).then_inc(a_s_shifted, 1)
                if live(n, 3):
                    dve.wait_ge(x_ready, n - 2)
                    stats(dve, count, n - 3)
                if live(n, 2):
                    dve.wait_ge(a_inv_ready, n - 1)
                    await_count(dve, a_out_in_psum, n - 3)
                    nc.vector.tensor_tensor(a_oT[:, p2].rearrange("p t c -> p (t c)"),
                                            bank[:, 3, 0:KT * T], a_inv[:, :],
                                            ALU.mult).then_inc(a_oT_ready, 1)

            dve.wait_ge(const_ready, 3)
            dve.wait_ge(w_loaded, 16 * 5)
            dve.wait_ge(const_loaded, 16)
            count.did(nc.vector.tensor_scalar(bern[:, 1, :], bern[:, 0, :], 1.0, 1e30, ALU.is_ge, ALU.mult))
            count.did(nc.vector.memset(a_vp[:, :, :], 0.0))
            nc.vector.memset(k_stack[NSTACK:NSTACK + 3, :, :, :], 1.0).then_inc(pad_ready, 1)
            count.sync(dve)
            count.did(nc.vector.tensor_tensor(bern[:, 2, :], bern[:, 0, :], bern[:, 1, :], ALU.add))
            for b in range(NB):
                dve.wait_ge(x_loaded, 16 * (b // 4 + 1))
                if b:
                    dve.wait_ge(stats_ready, b)
                stats(dve, count, b)
            pipeline(dve, step, 4, 2, 3, count, 3 + 5 + 1 + 2)

        def attn_gpsimd(pool):
            for b in range(NB):
                pool_rstd(pool, b, 0)

        def cross_phases(layer):
            return (0, 4, 0) if layer == 0 else (1, 3, NB)

        def cross_tensor(pe, layer, done, rdone):
            S = cross
            SPLIT, WEIGH, past = cross_phases(layer)
            rows = NSTACK + (3 if layer == 0 else 0)

            def weigh(n, u, odd):
                pe.wait_ge(S["e_ready"], HX * (n + past - WEIGH) + 4 + 4 * odd)
                for half in range(2):
                    for den in range(2):
                        for j in range(4):
                            w = half_ones[:, odd, :] if den else c_vT[:, (u - WEIGH) % 2, half, 2 * j + odd, :]
                            mm = nc.tensor.matmul(
                                bank[32 * j:32 * j + 32, 5 + den, 0:D], w, c_e[:, j + 4 * odd, half, :],
                                start=(odd == 0 and half == 0), stop=(odd == 1 and half == 1))
                mm.then_inc(S["pv_done"], 1)

            def step(n, u, uses):
                c = n + past
                buf = (u - WEIGH) % NBUF
                if live(n, WEIGH):
                    pe.wait_ge(S["stack_in"][buf], 16 * STACK_DMAS * uses(WEIGH, NBUF))
                    if layer == 0:
                        pe.wait_ge(S["neg_in"][buf], 16 * uses(WEIGH, NBUF))
                for i in range(HX):
                    if live(n, WEIGH):
                        await_count(pe, S["e_ready"], HX * (c - WEIGH) + i - 1)
                        for half in range(2):
                            mm = nc.tensor.matmul(
                                bank[:, 2 + i % 2, half * D:half * D + D],
                                k_stack[0:rows, buf, ORDER[i], half * 128:half * 128 + 128],
                                q_stack[0:rows, buf, ORDER[i], :], start=True, stop=True)
                        mm.then_inc(S["sT_in_psum"], 1)
                    if layer == 0 and live(n, 2):
                        if i == 0:
                            pe.wait_ge(S["stack_in"][(u - 2) % NBUF], 16 * STACK_DMAS * uses(2, NBUF))
                        await_count(pe, S["max_ready"], HX * (n - 2) + i - 1)
                        for half in range(2):
                            mm = nc.tensor.matmul(
                                bank[:, i % 2, half * D:half * D + D],
                                q_stack[0:NSTACK, (u - 2) % NBUF, i, half * 128:half * 128 + 128],
                                k_stack[0:NSTACK, (u - 2) % NBUF, i, :], start=True, stop=True)
                        mm.then_inc(S["s_in_psum"], 1)
                    if layer == 1 and i == 3 and live(n, 0):
                        pe.wait_ge(S["sq_ready"], n + 1)
                        await_count(pe, S["ss_ready"], n)
                        nc.tensor.matmul(bank[:, 7, :], table("group_ones"), c_sq[:, :],
                                         start=True, stop=True).then_inc(S["ss_in_psum"], 1)
                    if i == 5 and live(n, WEIGH):
                        pe.wait_ge(S["vT_ready"], 2 * (c - WEIGH + 1))
                        await_count(pe, x_ready, done + n - WEIGH)
                        weigh(n, u, 0)
                if layer == 0 and live(n, 2):
                    pe.wait_ge(S["max_ready"], HX * (n - 1))
                    await_count(pe, S["neg_ready"], n - 2)
                    nc.tensor.transpose(bank[0:2 * HX, 4, 0:128],
                                        c_max[:, u % 2].rearrange("p h a -> p (h a)"),
                                        ident).then_inc(S["maxT_in_psum"], 1)
                if live(n, WEIGH):
                    weigh(n, u, 1)

            pe.wait_ge(x_ready, done)
            pe.wait_ge(pad_ready, 2)
            pipeline(pe, step, 8, 4, WEIGH, past=past)

        def cross_scalar(act, layer, done, rdone):
            S = cross
            SPLIT, WEIGH, past = cross_phases(layer)
            count = cross_count["act"]
            scale = DX ** -0.5 if layer == 0 else 5.0
            src = c_raw if layer == 0 else c_unit
            per_step = 1 if layer == 0 else 2

            def step(n, u, uses):
                c = n + past
                ps = (u - SPLIT) % 2

                def part(k):
                    if not live(n, SPLIT):
                        return
                    if k:
                        act.wait_ge(S["rest1" if k == 1 else "rest2"], c - SPLIT + 1)
                    elif layer == 0:
                        act.wait_ge(S["h_ready"], c + 1)
                        act.wait_ge(S["ctx_in"][ps], 16 * uses(0, 2))
                    else:
                        act.wait_ge(S["unit_ready"], n)
                    if k == 0:
                        await_count(act, S["part_stored"], 16 * PART_DMAS * (c - SPLIT - 1))
                    nc.scalar.copy(c_part[:, ps, k, :], (src if k == 0 else c_rest)[:, ps, :]
                                   ).then_inc(S[("hi", "mid", "lo")[k]], 1)

                if layer == 1 and live(n, SPLIT):
                    act.wait_ge(S["ss_ready"], n)
                    count.did(nc.scalar.activation(c_ss[:, :], c_ss[:, :], ACT.Ln))
                    count.sync(act)
                    nc.scalar.activation(c_ss[:, :], c_ss[:, :], ACT.Exp,
                                         scale=-0.5).then_inc(S["inv_norm"], 1)
                for i in range(HX):
                    if live(n, WEIGH):
                        act.wait_ge(S["sT_in_psum"], HX * (c - WEIGH) + i + 1)
                        await_count(act, S["pv_done"], 2 * (c - WEIGH - 1) + 1 + i // 4)
                        nc.scalar.activation(c_e[:, i].rearrange("p a m -> p (a m)"), bank[:, 2 + i % 2, :],
                                             ACT.Exp, scale=scale).then_inc(S["e_ready"], 1)
                    if i == 1 and live(n, WEIGH + 1):
                        act.wait_ge(S["pv_done"], 2 * (c - WEIGH))
                        await_count(act, x_ready, done + n - WEIGH - 1)
                        count.did(nc.scalar.activation(c_inv[:, :], bank[:, 6, 0:D], ACT.Ln))
                        count.sync(act)
                        nc.scalar.activation(c_inv[:, :], c_inv[:, :], ACT.Exp,
                                             scale=-1.0).then_inc(S["inv_ready"], 1)
                    if i in (1, 4, 7):
                        part(i // 3)

            nc.scalar.preload_act_table_set("natural_log_exp_and_others")
            pipeline(act, step, 8, 4, WEIGH + 1, count, per_step, past=past)

        def cross_vector(dve, layer, done, rdone):
            S = cross
            SPLIT, WEIGH, past = cross_phases(layer)
            count = cross_count["dve"]

            def step(n, u, uses):
                c = n + past
                p0, p1 = u % 2, (u - 1) % 2
                if layer == 1 and live(n, 1):
                    dve.wait_ge(S["inv_norm"], n)
                    await_count(dve, S["rest1"], NB + n - 2)
                    nc.vector.tensor_tensor(c_unit[:, p1, :], c_raw[:, p1, :], c_ss[:, :],
                                            ALU.mult).then_inc(S["unit_ready"], 1)
                if live(n, 0):
                    dve.wait_ge(rstd_ready, rdone + n + 1)
                    if layer == 0:
                        await_count(dve, S["rest1"], n - 1)
                    else:
                        await_count(dve, S["unit_ready"], n - 1)
                    nc.vector.tensor_scalar(
                        c_raw[:, p0, 0:D], x_sb[:, n, :], moments[:, n, 0:1],
                        rstd[:, bass.ds(n, 1)], ALU.subtract, ALU.mult).then_inc(S["h_ready"], 1)
                if layer == 0 and live(n, 3):
                    dve.wait_ge(S["maxT_in_psum"], n - 2)
                    await_count(dve, S["neg_stored"], 16 * (n - 3))
                    maxT = bank[0:2 * HX, 4, 0:128]
                    count.did(nc.vector.tensor_scalar(c_neg[:, 0, :], maxT, -1.0, None, ALU.mult))
                    count.sync(dve)
                    count.did(nc.vector.scalar_tensor_tensor(c_nrest[:, 0, :], maxT, -1.0, c_neg[:, 0, :],
                                                             ALU.mult, ALU.subtract))
                    count.sync(dve)
                    count.did(nc.vector.tensor_copy(c_neg[:, 1, :], c_nrest[:, 0, :]))
                    count.sync(dve)
                    nc.vector.tensor_tensor(c_neg[:, 2, :], c_nrest[:, 0, :], c_neg[:, 1, :],
                                            ALU.subtract).then_inc(S["neg_ready"], 1)
                for i in range(HX):
                    if layer == 0 and live(n, 2):
                        dve.wait_ge(S["s_in_psum"], HX * (n - 2) + i + 1)
                        if i == 0:
                            await_count(dve, S["maxT_in_psum"], n - 3)
                        nc.vector.tensor_reduce(
                            c_max[:, p0, i, :], bank[:, i % 2, :].rearrange("p (a m) -> p a m", a=2),
                            AX.X, ALU.max).then_inc(S["max_ready"], 1)
                    if i == 3 and live(n, WEIGH + 1):
                        b = n - WEIGH - 1
                        dve.wait_ge(S["inv_ready"], c - WEIGH)
                        count.did(nc.vector.tensor_tensor(c_att[:, :], bank[:, 5, 0:D], c_inv[:, :], ALU.mult))
                        count.sync(dve)
                        nc.vector.tensor_tensor(x_sb[:, b, :], c_att[:, :], x_sb[:, b, :],
                                                ALU.add).then_inc(x_ready, 1)
                        dve.wait_ge(x_ready, done + b + 1)
                        stats(dve, count, b)
                if layer == 1 and live(n, 0):
                    dve.wait_ge(S["ss_in_psum"], n + 1)
                    await_count(dve, S["unit_ready"], n)
                    nc.vector.tensor_scalar(c_ss[:, :], bank[:, 7, :], 1e-24, None,
                                            ALU.max).then_inc(S["ss_ready"], 1)

            pipeline(dve, step, 8, 4, WEIGH + 1, count, 3 + (3 if layer == 0 else 0), past=past)

        def cross_gpsimd(pool, layer, done, rdone):
            S = cross
            SPLIT, WEIGH, past = cross_phases(layer)
            src = c_raw if layer == 0 else c_unit

            def step(n, u, uses):
                c = n + past
                p0, ps, pv = u % 2, (u - SPLIT) % 2, (u - WEIGH + 1) % 2
                if layer == 1 and live(n, 0):
                    pool.wait_ge(S["h_ready"], c + 1)
                    pool.wait_ge(S["ctx_in"][p0], 16 * uses(0, 2))
                    await_count(pool, S["ss_in_psum"], n)
                    nc.gpsimd.tensor_tensor(c_sq[:, :], c_raw[:, p0, :], c_raw[:, p0, :],
                                            ALU.mult).then_inc(S["sq_ready"], 1)
                if live(n, SPLIT):
                    pool.wait_ge(S["hi"], c - SPLIT + 1)
                    await_count(pool, S["lo"], c - SPLIT - 1)
                    nc.gpsimd.tensor_tensor(c_rest[:, ps, :], src[:, ps, :], c_part[:, ps, 0, :],
                                            ALU.subtract).then_inc(S["rest1"], 1)
                if live(n, WEIGH - 1):
                    pool.wait_ge(S["vT_in"][pv], 16 * uses(WEIGH - 1, 2))
                    await_count(pool, S["pv_done"], 2 * (c - WEIGH))
                    hold(pool)
                    for odd in range(2):
                        pick = c_vT_in[:, pv].rearrange("p a (j o c) -> p a j o c", o=2, c=DX)
                        nc.gpsimd.tensor_copy(
                            c_vT[:, pv].rearrange("p a (j o) c -> p a j o c", o=2)[
                                :, :, :, odd, DX * odd:DX * odd + DX],
                            pick[:, :, :, odd, :]).then_inc(S["vT_ready"], 1)
                if live(n, SPLIT):
                    pool.wait_ge(S["mid"], c - SPLIT + 1)
                    nc.gpsimd.tensor_tensor(c_rest[:, ps, :], c_rest[:, ps, :], c_part[:, ps, 1, :],
                                            ALU.subtract).then_inc(S["rest2"], 1)
                if live(n, WEIGH + 1):
                    pool_rstd(pool, n - WEIGH - 1, rdone + NB)

            pipeline(pool, step, 8, 4, WEIGH + 1, past=past)

        def cross_sync(sp, layer, done, rdone):
            S = cross
            SPLIT, WEIGH, past = cross_phases(layer)
            LOAD = SPLIT + 1

            def step(n, u, uses):
                c = n + past
                p0, ps, pl, pv, p1 = (u - x & 1 for x in (0, SPLIT, LOAD, WEIGH - 1, 1))
                if live(n, 0):
                    if layer == 0:
                        await_count(sp, S["rest1"], n - 1)
                    else:
                        await_count(sp, S["unit_ready"], n - 1)
                    sp.dma_start(c_raw[:, p0, D:2 * D],
                                 A["context"][bass.ds(n, 1)].rearrange("b t d -> (b t) d")
                                 ).then_inc(S["ctx_in"][p0], 16)
                if live(n, WEIGH - 1):
                    await_count(sp, S["vT_ready"], 2 * (c - WEIGH))
                    sp.dma_start(c_vT_in[:, pv],
                                 A["contextT"][bass.ds(n - WEIGH + 1, 1)].rearrange(
                                     "b (a p) t -> p (b a) t", p=128)).then_inc(S["vT_in"][pv], 16)
                if layer == 0 and live(n, 3):
                    sp.wait_ge(S["neg_ready"], n - 2)
                    hold(sp)
                    if live(n, 5):
                        sp.wait_ge(S["neg_in"][(u - 5) % NBUF], 16 * uses(5, NBUF))
                    sp.dma_start(neg_dram[p1], c_neg[:, :, :]).then_inc(S["neg_stored"], 16)
                if live(n, LOAD):
                    sp.wait_ge(S["part_stored"], 16 * PART_DMAS * (c - LOAD + 1))
                    hold(sp)
                    await_count(sp, S["sT_in_psum"], HX * (c - LOAD - 3))
                    hold(sp)
                    for a, (stack, parts) in enumerate(((q_stack, QPART), (k_stack, KPART))):
                        for r0, r1 in ((0, 3), (3, 5), (5, 6)):
                            rows = part_dram[pl, a, parts[r0] * DX:(parts[r1 - 1] + 1) * DX]
                            if parts[r0] == parts[r1 - 1]:
                                rows = rows.rearrange("d h m -> d (h m)").unsqueeze(0).to_broadcast(
                                    [r1 - r0, DX, HX * D])
                            else:
                                rows = rows.rearrange("d h m -> d (h m)")
                            sp.dma_start(stack[DX * r0:DX * r1, (u - LOAD) % NBUF, :, :].rearrange(
                                "p h m -> p (h m)"), rows).then_inc(S["stack_in"][(u - LOAD) % NBUF], 16)
                for k, part_ready in enumerate(("hi", "mid", "lo")):
                    if live(n, SPLIT):
                        sp.wait_ge(S[part_ready], c - SPLIT + 1)
                        hold(sp)
                        if k == 0 and live(n, SPLIT + 2):
                            sp.wait_ge(S["stack_in"][(u - SPLIT - 2) % NBUF],
                                       16 * STACK_DMAS * uses(SPLIT + 2, NBUF))
                        for a in range(2):
                            for_heads = part_dram[ps, a, k * DX:(k + 1) * DX].rearrange("d h m -> h d m")
                            sp.dma_start(for_heads, c_part[:, ps, k, a * D:a * D + D]
                                         ).then_inc(S["part_stored"], 16)
                    if k == 0 and layer == 0 and live(n, 3):
                        sp.wait_ge(S["neg_stored"], 16 * (n - 2))
                        sp.dma_start(
                            q_stack[NSTACK:NSTACK + 3, (u - 3) % NBUF, :, :].rearrange(
                                "c h (a m) -> c (h a) m", a=2),
                            neg_dram[p1].rearrange("a c m -> c a m")).then_inc(S["neg_in"][(u - 3) % NBUF], 16)

            pipeline(sp, step, 8, 4, WEIGH - 1, past=past)

        def shared_tensor(pe, done):
            def step(n, u, uses):
                p0 = u % 2
                if live(n, 1):
                    pe.wait_ge(m_hid_ready, n)
                    await_count(pe, m_hidT_ready, n - 1)
                    for t in range(KT):
                        mm = nc.tensor.transpose(bank[:, 3, t * T:(t + 1) * T],
                                                 m_hid[:, (u - 1) % 2, t * 128:(t + 1) * 128], ident)
                    mm.then_inc(m_hidT_in_psum, 1)
                if live(n, 0):
                    pe.wait_ge(m_h_ready, n + 1)
                    await_count(pe, m_hT_ready, n)
                    for t in range(KT):
                        mm = nc.tensor.transpose(bank[:, 0, t * T:(t + 1) * T],
                                                 m_hc[:, p0, t * 128:(t + 1) * 128], ident)
                    mm.then_inc(m_hT_in_psum, 1)
                if live(n, 1):
                    pe.wait_ge(m_hidT_ready, n)
                    await_count(pe, x_ready, done + n - 1)
                    for t in range(KT):
                        mm = nc.tensor.matmul(bank[:, 4, 0:D], m_hidT[:, t, :], m_wdn[:, t, :],
                                              start=(t == 0), stop=(t == KT - 1))
                    mm.then_inc(m_out_in_psum, 1)
                if live(n, 0):
                    pe.wait_ge(m_hT_ready, n + 1)
                    await_count(pe, m_hid_ready, n)
                    for t in range(KT):
                        nc.tensor.matmul(bank[:, 1, bass.ds(n * EX0, EX0)], m_hT[:, p0, t, :],
                                         m_wr[:, t, :], start=(t == 0), stop=(t == KT - 1))
                    for t in range(KT):
                        mm = nc.tensor.matmul(bank[:, 2, :], m_hT[:, p0, t, :], m_wgu[:, t, :],
                                              start=(t == 0), stop=(t == KT - 1))
                    mm.then_inc(m_gu_in_psum, 1)

            pe.wait_ge(x_ready, done)
            pe.wait_ge(m_w_loaded, 16 * 4)
            pipeline(pe, step, 4, 2, 1)
            pe.wait_ge(m_hot_ready, 1)
            pe.wait_ge(x_ready, done + NB)
            hot = m_s[:, :, :].rearrange("p b e -> p (b e)")
            nc.tensor.matmul(bank[:, 0, :], table("before"), hot, start=True, stop=True)
            nc.tensor.matmul(bank[:, 2, :], ones, hot, start=True, stop=True).then_inc(m_rank_in_psum, 1)

        def shared_scalar(act, done):
            def step(n, u, uses):
                p0 = u % 2
                if live(n, 0):
                    act.wait_ge(m_hT_in_psum, n + 1)
                    await_count(act, m_gu_in_psum, n - 1)
                    nc.scalar.copy(m_hT[:, p0].rearrange("p t c -> p (t c)"),
                                   bank[:, 0, 0:D]).then_inc(m_hT_ready, 1)
                if live(n, 1):
                    act.wait_ge(m_hidT_in_psum, n)
                    await_count(act, m_out_in_psum, n - 1)
                    nc.scalar.copy(m_hidT[:, :, :].rearrange("p t c -> p (t c)"),
                                   bank[:, 3, 0:D]).then_inc(m_hidT_ready, 1)
                if live(n, 0):
                    act.wait_ge(m_gu_in_psum, n + 1)
                    await_count(act, m_hid_ready, n - 1)
                    nc.scalar.activation(m_sig[:, p0, :], bank[:, 2, 0:SH0],
                                         ACT.Sigmoid).then_inc(m_sig_ready, 1)

            act.wait_ge(x_ready, done)
            nc.scalar.preload_act_table(ACT.Sigmoid)
            pipeline(act, step, 4, 2, 1)
            nc.scalar.activation(m_t[0][:, 0:NB // TOP0].rearrange("p b k e -> p (b k e)"), bank[:, 1, :],
                                 ACT.Sigmoid).then_inc(m_s_ready, 1)

        def shared_vector(dve, done):
            count = Count(m_dve)

            def step(n, u, uses):
                p0 = u % 2
                if live(n, 0):
                    dve.wait_ge(rstd_ready, done + n + 1)
                    await_count(dve, m_hT_in_psum, n - 1)
                    count.did(nc.vector.tensor_scalar(
                        m_hc[:, p0, :], x_sb[:, n, :], moments[:, n, 0:1],
                        rstd[:, bass.ds(n, 1)], ALU.subtract, ALU.mult))
                    count.sync(dve)
                    nc.vector.tensor_copy(h_all[:, n, :], m_hc[:, p0, :]).then_inc(m_h_ready, 1)
                    dve.wait_ge(m_sig_ready, n + 1)
                    await_count(dve, m_hidT_in_psum, n - 1)
                    count.did(nc.vector.tensor_tensor(m_sig[:, p0, :], bank[:, 2, 0:SH0], m_sig[:, p0, :],
                                                      ALU.mult))
                    count.sync(dve)
                    nc.vector.tensor_tensor(m_hid[:, p0, :], bank[:, 2, SH0:2 * SH0], m_sig[:, p0, :],
                                            ALU.mult).then_inc(m_hid_ready, 1)
                if live(n, 1):
                    dve.wait_ge(m_out_in_psum, n)
                    nc.vector.tensor_tensor(x_sb[:, n - 1, :], bank[:, 4, 0:D], x_sb[:, n - 1, :],
                                            ALU.add).then_inc(x_ready, 1)

            pipeline(dve, step, 4, 2, 1, count, 2)
            dve.wait_ge(x_ready, done + NB)
            dve.wait_ge(m_s_ready, 1)
            dve.wait_ge(m_w_loaded, 16 * 4)
            seq = lambda ins: (count.did(ins), count.sync(dve))
            tt, ts = nc.vector.tensor_tensor, nc.vector.tensor_scalar
            all_e = [128, NB, TOP0, EX0]
            score = m_t[0][:, 0:NB // TOP0].rearrange("p a k e -> p (a k) e")
            sc = m_t[1][:, 0:NB // TOP0].rearrange("p a k e -> p (a k) e")
            seq(tt(sc, score, m_bias[:, :].unsqueeze(1).to_broadcast([128, NB, EX0]), ALU.add))
            of = sc.rearrange("p b (g c) -> p b g c", c=EX0 // GROUPS)
            a, b_, c, d = (of[:, :, :, i] for i in range(4))
            g = [x[:, :, :] for x in m_g]
            for o, i0, i1, op in ((g[0], a, b_, ALU.max), (g[1], a, b_, ALU.min), (g[2], c, d, ALU.max),
                                  (g[3], c, d, ALU.min)):
                count.did(tt(o, i0, i1, op))
            count.sync(dve)
            count.did(tt(g[4], g[0], g[2], ALU.max))
            count.did(tt(g[5], g[0], g[2], ALU.min))
            seq(tt(g[1], g[1], g[3], ALU.max))
            seq(tt(g[5], g[5], g[1], ALU.max))
            seq(tt(g[4], g[4], g[5], ALU.add))
            for b in range(NB):
                count.did(nc.vector.max(m_top[:, b, :], g[4][:, b, :]))
            count.sync(dve)
            for b in range(NB):
                count.did(nc.vector.max_index(m_topi[:, b, :], m_top[:, b, :], g[4][:, b, :]))
            count.sync(dve)
            seq(nc.vector.tensor_copy(m_pick[:, :, 0:TOPG], m_topi[:, :, 0:TOPG]))
            iota = table("iota32")
            chosen = m_hot[:, :, 0:TOPG, 0:GROUPS]
            for k in range(TOPG):
                count.did(tt(m_hot[:, :, k, 0:GROUPS],
                             iota[:, 0:GROUPS].unsqueeze(1).to_broadcast([128, NB, GROUPS]),
                             m_pick[:, :, k:k + 1].to_broadcast([128, NB, GROUPS]), ALU.is_equal))
            count.sync(dve)
            seq(nc.vector.tensor_reduce(g[0], chosen.rearrange("p b k g -> p b g k"), AX.X, ALU.add))
            seq(tt(of, of, g[0].unsqueeze(3).to_broadcast([128, NB, GROUPS, EX0 // GROUPS]), ALU.mult))
            seq(ts(sc, sc, 0.0, None, ALU.add))
            for b in range(NB):
                count.did(nc.vector.max(m_top[:, b, :], sc[:, b, :]))
            count.sync(dve)
            for b in range(NB):
                count.did(nc.vector.max_index(m_topi[:, b, :], m_top[:, b, :], sc[:, b, :]))
            count.sync(dve)
            seq(nc.vector.tensor_copy(m_pick[:, :, :], m_topi[:, :, 0:TOP0]))
            for k in range(TOP0):
                count.did(tt(m_hot[:, :, k, :], iota.unsqueeze(1).to_broadcast([128, NB, EX0]),
                             m_pick[:, :, k:k + 1].to_broadcast([128, NB, EX0]), ALU.is_equal))
            count.sync(dve)
            nc.vector.tensor_reduce(m_s[:, :, :], m_hot[:, :, :, :].rearrange("p b k e -> p b e k"), AX.X,
                                    ALU.add).then_inc(m_hot_ready, 1)
            dve.wait_ge(m_hot_ready, 1)
            for k in range(TOP0):
                count.did(tt(m_t[1][:, :, k, :], m_hot[:, :, k, :], score, ALU.mult))
            count.sync(dve)
            seq(nc.vector.tensor_reduce(m_w[:, :, :], m_t[1][:, :, :, :], AX.X, ALU.add))
            seq(nc.vector.tensor_reduce(m_sum[:, :], m_w[:, :, :], AX.X, ALU.add))
            seq(ts(m_sum[:, :], m_sum[:, :], 1e-20, None, ALU.add))
            seq(nc.vector.reciprocal(m_sum[:, :], m_sum[:, :]))
            seq(ts(m_sum[:, :], m_sum[:, :], 2.5, None, ALU.mult))
            seq(tt(m_w[:, :, :], m_w[:, :, :], m_sum[:, :].unsqueeze(2).to_broadcast([128, NB, TOP0]),
                   ALU.mult))
            dve.wait_ge(m_rank_in_psum, 1)
            before = bank[:, 0, :].rearrange("p (b e) -> p b e", e=EX0)
            in_all = bank[:, 2, :].rearrange("p (b e) -> p b e", e=EX0)
            base = m_t[1][:, 0:NB // TOP0].rearrange("p a k e -> p (a k) e")
            seq(nc.vector.memset(base[:, 0, :], 0.0))
            for b in range(1, NB):
                seq(tt(base[:, b, :], in_all[:, b - 1, :], base[:, b - 1, :], ALU.add))
            seq(tt(m_s[:, :, :], before, base, ALU.add))
            for k in range(TOP0):
                count.did(tt(m_t[0][:, :, k, :], m_hot[:, :, k, :], m_s[:, :, :], ALU.mult))
            count.sync(dve)
            rank, slot, over = (x[:, :, :] for x in m_k)
            seq(nc.vector.tensor_reduce(rank, m_t[0][:, :, :, :], AX.X, ALU.add))
            count.did(ts(over, rank, float(CAP), DROPPED, ALU.is_ge, ALU.mult))
            seq(nc.vector.scalar_tensor_tensor(slot.rearrange("p b k -> p (b k)"),
                                               m_pick[:, :, :].rearrange("p b k -> p (b k)"), float(CAP),
                                               rank.rearrange("p b k -> p (b k)"), ALU.mult, ALU.add))
            seq(tt(slot, slot, over, ALU.add))
            nc.vector.tensor_copy(m_slot[:, :, :], slot).then_inc(m_slot_ready, 1)

        def dispatch_gpsimd(pool):
            pool.wait_ge(m_slot_ready, 1)
            pool.wait_ge(slots_zero, 16 * 5)
            for b in range(NB):
                for k in range(TOP0):
                    pool.indirect_dma_start(
                        out=xp_dram, out_offset=bass.IndirectOffsetOnAxis(ap=m_slot[:, b, k:k + 1], axis=0),
                        in_=h_all[:, b, :], in_offset=None, bounds_check=SLOTS - 1,
                        oob_is_err=False).then_inc(rows_sent, 16)

        def collect_gpsimd(pool, done):
            for n in range(NB):
                if n == 0:
                    for p in range(2):
                        pool.wait_ge(y_stored[p], 16 * (EX0 // 2))
                await_count(pool, y_zero, n - GB + 1 + 1)
                for k in range(TOP0):
                    pool.indirect_dma_start(
                        out=g_y[:, n % GB, k, :], out_offset=None, in_=y_dram,
                        in_offset=bass.IndirectOffsetOnAxis(ap=m_slot[:, n, k:k + 1], axis=0),
                        bounds_check=SLOTS - 1, oob_is_err=False).then_inc(y_in[n % GB], 16)
                if n >= 1:
                    pool_rstd(pool, n - 1, 3 * NB)
            pool_rstd(pool, NB - 1, 3 * NB)

        def collect_vector(dve, done):
            count = Count(r_dve)

            def step(n, u, uses):
                dve.wait_ge(y_in[u % GB], 16 * TOP0 * uses(0, GB))
                for k in range(TOP0):
                    ins = nc.vector.scalar_tensor_tensor(x_sb[:, n, :], g_y[:, u % GB, k, :],
                                                         m_w[:, n, k:k + 1], x_sb[:, n, :],
                                                         ALU.mult, ALU.add)
                    if k < TOP0 - 1:
                        count.did(ins)
                        count.sync(dve)
                    else:
                        ins.then_inc(x_ready, 1)
                dve.wait_ge(x_ready, done + n + 1)
                nc.vector.memset(g_y[:, u % GB], 0.0).then_inc(y_zero, 1)
                stats(dve, count, n)

            pipeline(dve, step, 4, 4, 0, count, TOP0 - 1 + 2)

        def expert_tensor(pe):
            def step(n, u, uses):
                if live(n, 0, EX0):
                    pe.wait_ge(d_x_in[u % XBUF], 16 * uses(0, XBUF))
                    await_count(pe, d_xT_ready, n)
                    for t in range(KT):
                        mm = nc.tensor.transpose(bank[:, 0, t * CAP:(t + 1) * CAP],
                                                 d_x[:, u % XBUF, t * 128:(t + 1) * 128],
                                                 ident[0:CAP, 0:CAP])
                    mm.then_inc(d_xT_in_psum, 1)
                if live(n, 1, EX0):
                    pe.wait_ge(d_xT_ready, n)
                    pe.wait_ge(ring_in[(u - 1) % RING], 32 * uses(1, RING))
                    await_count(pe, d_hid_ready, n - 2)
                    for t in range(KT):
                        mm = nc.tensor.matmul(bank[0:CAP, GU[(u - 1) % 2], 0:2 * I0], d_xT[:, (u - 1) % 2, t, :],
                                              wgu[:, (u - 1) % RING, t, :], start=(t == 0),
                                              stop=(t == KT - 1))
                    mm.then_inc(d_gu_in_psum, 1)
                if live(n, 2, EX0):
                    pe.wait_ge(d_hid_ready, n - 1)
                    await_count(pe, d_hidT_ready, n - 2)
                    nc.tensor.transpose(bank[:, 2, 0:CAP], d_hid[:, u % 2, :],
                                        ident[0:CAP, 0:CAP]).then_inc(d_hidT_in_psum, 1)
                if live(n, 3, EX0):
                    pe.wait_ge(d_hidT_ready, n - 2)
                    await_count(pe, d_y_ready, n - 3)
                    nc.tensor.matmul(bank[0:CAP, 3, 0:D], d_hidT[:, (u - 3) % 2, :], wdn[:, (u - 3) % RING, :],
                                     start=True, stop=True).then_inc(d_y_in_psum, 1)

            pe.wait_ge(m_slot_ready, 1)
            pipeline(pe, step, RING, RING, 3, total=EX0)

        def expert_scalar(act):
            def step(n, u, uses):
                if live(n, 0, EX0):
                    act.wait_ge(d_xT_in_psum, n + 1)
                    await_count(act, d_gu_in_psum, n - 1)
                    nc.scalar.copy(d_xT[:, u % 2].rearrange("p t c -> p (t c)"),
                                   bank[:, 0, 0:KT * CAP]).then_inc(d_xT_ready, 1)
                if live(n, 2, EX0):
                    act.wait_ge(d_hidT_in_psum, n - 1)
                    await_count(act, d_y_in_psum, n - 3)
                    nc.scalar.copy(d_hidT[:, u % 2, :], bank[:, 2, 0:CAP]).then_inc(d_hidT_ready, 1)
                if live(n, 1, EX0):
                    act.wait_ge(d_gu_in_psum, n)
                    await_count(act, d_hid_ready, n - 1)
                    nc.scalar.activation(d_sig[:, :], bank[0:CAP, GU[(u - 1) % 2], 0:I0],
                                         ACT.Sigmoid).then_inc(d_sig_ready, 1)

            pipeline(act, step, RING, RING, 2, total=EX0)

        def expert_vector(dve):
            count = Count(e_dve)

            def step(n, u, uses):
                if live(n, 1, EX0):
                    p1 = (u - 1) % 2
                    dve.wait_ge(d_sig_ready, n)
                    await_count(dve, d_hidT_in_psum, n - 2)
                    count.did(nc.vector.tensor_tensor(d_hid[:, p1, :], bank[0:CAP, GU[p1], 0:I0], d_sig[:, :],
                                                      ALU.mult))
                    count.sync(dve)
                    nc.vector.tensor_tensor(d_hid[:, p1, :], bank[0:CAP, GU[p1], I0:2 * I0], d_hid[:, p1, :],
                                            ALU.mult).then_inc(d_hid_ready, 1)
                if live(n, 3, EX0):
                    dve.wait_ge(d_y_in_psum, n - 2)
                    if live(n, 5, EX0):
                        dve.wait_ge(y_stored[(u - 5) % 2], 16 * uses(5, 2))
                    nc.vector.tensor_copy(d_y[:, (u - 3) % 2, :], bank[0:CAP, 3, 0:D]).then_inc(d_y_ready, 1)

            pipeline(dve, step, RING, RING, 3, count, 1, total=EX0)

        def expert_sync(sp):
            def step(n, u, uses):
                if live(n, 0, EX0):
                    await_count(sp, d_xT_in_psum, n - XBUF + 1)
                    sp.dma_start(d_x[:, u % XBUF, :],
                                 xp_dram[bass.ds(n * CAP, CAP), :]).then_inc(d_x_in[u % XBUF], 16)
                if live(n, STORE, EX0):
                    sp.wait_ge(d_y_ready, n - STORE + 1)
                    sp.dma_start(y_dram[bass.ds((n - STORE) * CAP, CAP), :],
                                 d_y[:, (u - STORE) % 2, :]).then_inc(y_stored[(u - STORE) % 2], 16)
                    if not isinstance(n, int) or n - STORE + RING < EX0:
                        load_expert(sp, n - STORE + RING, u - STORE)

            sp.wait_ge(rows_sent, 16 * NB * TOP0)
            pipeline(sp, step, RING, RING, RING + STORE, total=EX0 - RING)

        def load_expert(sp, e, u):
            sp.dma_start(wgu[:, u % RING, :, :],
                         A["W_gu"][bass.ds(e, 1)].rearrange("e (t p) i -> p (e t) i", p=128)
                         ).then_inc(ring_in[u % RING], 16)
            sp.dma_start(wdn[:, u % RING, :],
                         A["W_down"][bass.ds(e, 1)].rearrange("e p o -> p (e o)")).then_inc(ring_in[u % RING], 16)

        def shift_tensor(pe, done):
            def step(n, u, uses):
                p0, p2 = u % 2, u % 2
                if live(n, 2):
                    pe.wait_ge(f_state_ready, n - 1)
                    await_count(pe, x_ready, done + n - 2)
                    nc.tensor.matmul(bank[:, 4, 0:D], f_state[:, p2, :], f_wo[:, :],
                                     start=True, stop=True).then_inc(f_out_in_psum, 1)
                if live(n, 0):
                    pe.wait_ge(f_h_ready, n + 1)
                    await_count(pe, f_hT_ready, 2 * n)
                    for t in range(KT):
                        mm = nc.tensor.transpose(bank[:, 0, t * T:(t + 1) * T],
                                                 f_h[:, p0, t * 128:(t + 1) * 128], ident)
                    mm.then_inc(f_hT_in_psum, 1)
                if live(n, 1):
                    pe.wait_ge(f_z_ready, n)
                    await_count(pe, f_zT_ready, n - 1)
                    for t in range(KT):
                        mm = nc.tensor.transpose(bank[:, 2, t * T:(t + 1) * T],
                                                 f_z[:, t * 128:(t + 1) * 128], ident)
                    mm.then_inc(f_zT_in_psum, 1)
                if live(n, 0):
                    pe.wait_ge(f_hT_ready, 2 * (n + 1))
                    await_count(pe, f_xs_ready, n)
                    for t in range(KT):
                        mm = nc.tensor.matmul(bank[:, 1, 0:D], f_hT[:, p0, t, :], f_wshift[:, t, :],
                                              start=(t == 0), stop=(t == KT - 1))
                    mm.then_inc(f_shift_in_psum, 1)
                if live(n, 1):
                    pe.wait_ge(f_zT_ready, n)
                    await_count(pe, f_wkvx_ready, n - 1)
                    for kv in range(2):
                        for t in range(KT):
                            mm = nc.tensor.matmul(bank[0:NS, 3, kv * T:(kv + 1) * T],
                                                  f_wkv[:, 1, t, kv * NS:(kv + 1) * NS], f_zT[:, t, :],
                                                  start=(t == 0), stop=(t == KT - 1))
                    mm.then_inc(f_kv_in_psum, 1)

            pe.wait_ge(x_ready, done)
            pe.wait_ge(f_loaded, 16 * 8)
            for kv in range(2):
                for t in range(KT):
                    mm = nc.tensor.matmul(bank[0:NS, 3, kv:kv + 1], f_wkv[:, 0, t, kv * NS:(kv + 1) * NS],
                                          f_affine[:, 1, t:t + 1], start=(t == 0), stop=(t == KT - 1))
            mm.then_inc(f_pe, 1)
            pe.wait_ge(f_setup, 1)
            pipeline(pe, step, 4, 2, 2)

        def shift_scalar(act, done):
            count = Count(f_act)

            def step(n, u, uses):
                p0, p1 = u % 2, (u - 1) % 2
                if live(n, 0):
                    act.wait_ge(f_hT_in_psum, n + 1)
                    await_count(act, f_shift_in_psum, n - 1)
                    src = bank[:, 0, 0:D].rearrange("p (t c) -> p t c", t=KT)
                    half = T // 2
                    nc.scalar.copy(f_hT[:, p0, :, 0:half], src[:, :, half:T]).then_inc(f_hT_ready, 1)
                    nc.scalar.copy(f_hT[:, p0, :, half:T], src[:, :, 0:half]).then_inc(f_hT_ready, 1)
                if live(n, 1):
                    act.wait_ge(f_zT_in_psum, n)
                    await_count(act, f_kv_in_psum, n - 1)
                    nc.scalar.copy(f_zT[:, :, :].rearrange("p t c -> p (t c)"),
                                   bank[:, 2, 0:D]).then_inc(f_zT_ready, 1)
                    act.wait_ge(f_kv_in_psum, n)
                    await_count(act, f_wkvx_ready, n - 2)
                    e = f_k[:, p1, :]
                    count.did(nc.scalar.activation(e, bank[0:NS, 3, 0:T], ACT.Exp, bias=f_bias[:, 2:3],
                                                   scale=-1.0))
                    count.sync(act)
                    count.did(nc.scalar.activation(e, e, ACT.Ln, bias=1.0))
                    count.sync(act)
                    count.did(nc.scalar.activation(e, e, ACT.Exp, scale=-1.0))
                    count.sync(act)
                    nc.scalar.activation(e, e, ACT.Exp, scale=f_time[:, 3:4]).then_inc(f_k_ready, 1)

            nc.scalar.preload_act_table_set("natural_log_exp_and_others")
            act.wait_ge(x_ready, done)
            act.wait_ge(f_loaded, 16 * 8)
            gate = f_gate[:, 0, :]
            count.did(nc.scalar.activation(f_time[:, 2:3], f_time[:, 0:1], ACT.Exp))
            count.did(nc.scalar.activation(f_time[:, 3:4], f_time[:, 1:2], ACT.Exp))
            count.did(nc.scalar.activation(gate, gate, ACT.Exp, scale=-1.0))
            count.sync(act)
            count.did(nc.scalar.activation(gate, gate, ACT.Ln, bias=1.0))
            count.sync(act)
            nc.scalar.activation(gate, gate, ACT.Exp, scale=-1.0).then_inc(f_gate_exp, 1)
            act.wait_ge(f_setup, 1)
            pipeline(act, step, 4, 2, 1, count, 3)

        def shift_vector(dve, done, rdone):
            count = Count(f_dve)

            def step(n, u, uses):
                p0, p1, p2 = u % 2, (u - 1) % 2, u % 2
                if live(n, 0):
                    dve.wait_ge(rstd_ready, rdone + n + 1)
                    await_count(dve, f_hT_in_psum, n - 1)
                    nc.vector.tensor_scalar(
                        f_h[:, p0, :], x_sb[:, n, :], moments[:, n, 0:1],
                        rstd[:, bass.ds(n, 1)], ALU.subtract, ALU.mult).then_inc(f_h_ready, 1)
                if live(n, 1):
                    dve.wait_ge(f_rstd_ready, n)
                    await_count(dve, f_zT_in_psum, n - 1)
                    nc.vector.tensor_scalar(
                        f_z[:, :], f_xs[:, p1, :], f_mom[:, p1, 0:1], f_rstd[:, p1:p1 + 1],
                        ALU.subtract, ALU.mult).then_inc(f_z_ready, 1)
                if live(n, 2):
                    dve.wait_ge(f_out_in_psum, n - 1)
                    nc.vector.tensor_tensor(x_sb[:, n - 2, :], bank[:, 4, 0:D], x_sb[:, n - 2, :],
                                            ALU.add).then_inc(x_ready, 1)
                if live(n, 0):
                    dve.wait_ge(f_h_ready, n + 1)
                    count.did(nc.vector.tensor_tensor(f_part[:, :], f_h[:, p0, :], f_gate[:, 1, :],
                                                      ALU.mult))
                    count.sync(dve)
                    dve.wait_ge(f_shift_in_psum, n + 1)
                    nc.vector.tensor_tensor(f_xs[:, p0, :], bank[:, 1, 0:D], f_part[:, :],
                                            ALU.add).then_inc(f_xs_ready, 1)
                    dve.wait_ge(f_xs_ready, n + 1)
                    count.did(nc.vector.bn_stats(bn6[:, 1, :], f_xs[:, p0, :]))
                    count.sync(dve)
                    hold(dve)
                    count.did(nc.vector.bn_aggr(f_mom[:, p0, :], bn6[:, 1, :]))
                    count.sync(dve)
                    nc.vector.tensor_scalar(f_var[:, p0:p0 + 1], f_mom[:, p0, 1:2], EPS, None,
                                            ALU.add).then_inc(f_var_ready, 1)
                if live(n, 1):
                    dve.wait_ge(f_k_ready, n)
                    nc.vector.scalar_tensor_tensor(f_wkvx[:, :], bank[0:NS, 3, T:2 * T], f_bias[:, 1:2],
                                                   f_k[:, p1, :], ALU.add, ALU.mult).then_inc(f_wkvx_ready, 1)
                    dve.wait_ge(f_wkvx_ready, n)
                    await_count(dve, f_out_in_psum, n - 2)
                    nc.vector.tensor_tensor_scan(f_state[:, p1, :], f_decay[:, :], f_wkvx[:, :], 0.0,
                                                 ALU.mult, ALU.add).then_inc(f_state_ready, 1)
                if live(n, 2):
                    dve.wait_ge(x_ready, done + n - 1)
                    stats(dve, count, n - 2)

            seq = lambda ins: (count.did(ins), count.sync(dve))
            tt, ts = nc.vector.tensor_tensor, nc.vector.tensor_scalar
            dve.wait_ge(f_gate_exp, 1)
            count.did(ts(f_gate[:, 1, :], f_gate[:, 0, :], -1.0, 1.0, ALU.mult, ALU.add))
            for t in range(KT):
                count.did(tt(f_wshift[:, t, :], f_wshift[:, t, :], f_gate[:, 0, :], ALU.mult))
                count.did(ts(f_wkv[:, 1, t, :], f_wkv[:, 0, t, :], f_affine[:, 0, t:t + 1], None, ALU.mult))
            count.did(ts(f_decay[:, :], table("ones", NS), f_time[:, 2:3], None, ALU.mult))
            seq(ts(f_time[:, 3:4], f_time[:, 3:4], -1.0, None, ALU.mult))
            dve.wait_ge(f_pe, 1)
            seq(nc.vector.tensor_copy(f_bias[:, 0:2], bank[0:NS, 3, 0:2]))
            ts(f_bias[:, 2:3], f_bias[:, 0:1], -1.0, None, ALU.mult).then_inc(f_setup, 1)
            pipeline(dve, step, 4, 2, 2, count, 3 + 2)

        def shift_gpsimd(pool, done, rdone):
            def step(n, u, uses):
                p0 = u % 2
                if live(n, 0):
                    pool.wait_ge(f_var_ready, n + 1)
                    await_count(pool, f_z_ready, n - 1)
                    nc.gpsimd.tensor_tensor(f_rstd[:, p0:p0 + 1], f_var[:, p0:p0 + 1], minus_half[:, 0:1],
                                            ALU.pow).then_inc(f_rstd_ready, 1)
                if live(n, 2):
                    pool_rstd(pool, n - 2, rdone + NB)

            pipeline(pool, step, 4, 2, 2)

        def mlp_tensor(pe, done):
            def turned(n, u, i):
                idx = PAIRS * (n - 1) + i
                pe.wait_ge(l_hid_ready, idx + 1)
                await_count(pe, l_hidT_ready, idx if i == 0 else idx - 1)
                for e in range(2 * i, min(2 * i + 2, EXS)):
                    mm = nc.tensor.transpose(bank[:, 4 + i % 2, (e % 2) * T:(e % 2 + 1) * T],
                                             l_hid[:, i % 2, (e % 2) * I1:(e % 2 + 1) * I1], ident)
                mm.then_inc(l_hidT_in_psum, 1)

            def step(n, u, uses):
                p0, p1, p2 = u % 2, (u - 1) % 2, u % 2
                if live(n, 0):
                    pe.wait_ge(l_h_ready, n + 1)
                    await_count(pe, l_hT_ready, n)
                    for t in range(KT):
                        mm = nc.tensor.transpose(bank[:, 0, t * T:(t + 1) * T],
                                                 l_h[:, p0, t * 128:(t + 1) * 128], ident)
                    mm.then_inc(l_hT_in_psum, 1)
                for i in range(PAIRS):
                    if live(n, 1):
                        idx = PAIRS * (n - 1) + i
                        await_count(pe, l_hid_ready, idx if i == 0 else idx - 1)
                        w = 2 * I1 * (min(2 * i + 2, EXS) - 2 * i)
                        for t in range(KT):
                            mm = nc.tensor.matmul(
                                bank[:, 2 + i % 2, 0:w], l_hT[:, p1, t, :],
                                wgu[:, 2 * i:min(2 * i + 2, EXS), t, :], start=(t == 0), stop=(t == KT - 1))
                        mm.then_inc(l_gu_in_psum, 1)
                        if i >= 1:
                            turned(n, u, i - 1)
                    if i == 1 and live(n, 0):
                        pe.wait_ge(l_hT_ready, n + 1)
                        await_count(pe, l_prob_ready, n)
                        for t in range(KT):
                            mm = nc.tensor.matmul(bank[:, 1, 0:EX1], l_hT[:, p0, t, :], l_wr[:, t, :],
                                                  start=(t == 0), stop=(t == KT - 1))
                        mm.then_inc(l_logit_in_psum, 1)
                if live(n, 2):
                    pe.wait_ge(l_hidT_ready, PAIRS * (n - 1))
                    await_count(pe, x_ready, done + n - 2)
                    for e in range(EXS):
                        mm = nc.tensor.matmul(bank[:, 6, 0:D], l_hidT[:, p2, e, :], wdn[:, e, :],
                                              start=(e == 0), stop=(e == EXS - 1))
                    mm.then_inc(l_out_in_psum, 1)
                if live(n, 1):
                    turned(n, u, PAIRS - 1)

            pe.wait_ge(x_ready, done)
            pe.wait_ge(l_loaded, 16 * 6)
            pipeline(pe, step, 4, 2, 2)

        def mlp_scalar(act, done):
            def step(n, u, uses):
                p0, p1 = u % 2, (u - 1) % 2
                for i in range(PAIRS):
                    if live(n, 1):
                        idx = PAIRS * (n - 1) + i
                        act.wait_ge(l_gu_in_psum, idx + 1)
                        if i == 0:
                            act.wait_ge(l_p_ready, n)
                        await_count(act, l_hid_ready, idx if i == 0 else idx - 1)
                        for e in range(2 * i, min(2 * i + 2, EXS)):
                            c = (e % 2) * I1
                            ins = nc.scalar.activation(l_sig[:, i % 2, c:c + I1],
                                                       bank[:, 2 + i % 2, 2 * c:2 * c + I1],
                                                       ACT.Sigmoid, scale=l_p[:, p1, e:e + 1])
                            ins.then_inc(l_sig_ready, 1)
                    if i == 0 and live(n, 0):
                        act.wait_ge(l_hT_in_psum, n + 1)
                        await_count(act, l_gu_in_psum, PAIRS * (n - 1))
                        nc.scalar.copy(l_hT[:, p0].rearrange("p t c -> p (t c)"),
                                       bank[:, 0, 0:D]).then_inc(l_hT_ready, 1)
                    if i == 2 and live(n, 0):
                        act.wait_ge(l_logit_ready, n + 1)
                        await_count(act, l_p_ready, n)
                        nc.scalar.activation(l_prob[:, :], bank[:, 1, 0:EX1],
                                             ACT.Sigmoid).then_inc(l_prob_ready, 1)
                    if i >= 1 and live(n, 1):
                        copy_hidden(act, n, u, i - 1)
                if live(n, 1):
                    copy_hidden(act, n, u, PAIRS - 1)

            def copy_hidden(act, n, u, i):
                act.wait_ge(l_hidT_in_psum, PAIRS * (n - 1) + i + 1)
                if i == 0:
                    await_count(act, l_out_in_psum, n - 2)
                hi = min(2 * i + 2, EXS)
                nc.scalar.copy(l_hidT[:, (u - 1) % 2, 2 * i:hi, :].rearrange("p e c -> p (e c)"),
                               bank[:, 4 + i % 2, 0:(hi - 2 * i) * T]).then_inc(l_hidT_ready, 1)

            nc.scalar.preload_act_table(ACT.Sigmoid)
            pipeline(act, step, 4, 2, 1)

        def mlp_vector(dve, done, rdone):
            count = Count(l_dve)

            def step(n, u, uses):
                p0, p1 = u % 2, (u - 1) % 2
                if live(n, 0):
                    dve.wait_ge(rstd_ready, rdone + n + 1)
                    await_count(dve, l_hT_in_psum, n - 1)
                    nc.vector.tensor_scalar(
                        l_h[:, p0, :], x_sb[:, n, :], moments[:, n, 0:1],
                        rstd[:, bass.ds(n, 1)], ALU.subtract, ALU.mult).then_inc(l_h_ready, 1)
                for i in range(PAIRS):
                    if live(n, 1):
                        idx = PAIRS * (n - 1) + i
                        last = min(2 * i + 2, EXS)
                        dve.wait_ge(l_sig_ready, EXS * (n - 1) + last)
                        await_count(dve, l_hidT_in_psum, idx if i == 0 else idx - 1)
                        for e in range(2 * i, last):
                            c = (e % 2) * I1
                            count.did(nc.vector.scalar_tensor_tensor(
                                l_sig[:, i % 2, c:c + I1], bank[:, 2 + i % 2, 2 * c:2 * c + I1],
                                l_p[:, p1, e:e + 1], l_sig[:, i % 2, c:c + I1], ALU.mult, ALU.mult))
                        count.sync(dve)
                        for e in range(2 * i, last):
                            c = (e % 2) * I1
                            ins = nc.vector.scalar_tensor_tensor(
                                l_hid[:, i % 2, c:c + I1], bank[:, 2 + i % 2, 2 * c + I1:2 * c + 2 * I1],
                                l_p[:, p1, e:e + 1], l_sig[:, i % 2, c:c + I1], ALU.mult, ALU.mult)
                            if e == last - 1:
                                ins.then_inc(l_hid_ready, 1)
                            else:
                                count.did(ins)
                    if i == 2 and live(n, 0):
                        dve.wait_ge(l_logit_in_psum, n + 1)
                        nc.vector.tensor_copy(l_logit[:, :], bank[:, 1, 0:EX1]).then_inc(l_logit_ready, 1)
                        dve.wait_ge(l_logit_ready, n + 1)
                        hold(dve)
                        count.did(nc.vector.max(l_top[:, :], l_logit[:, :]))
                        count.sync(dve)
                        hold(dve)
                        count.did(nc.vector.max_index(l_topi[:, :], l_top[:, :], l_logit[:, :]))
                        count.sync(dve)
                        count.did(nc.vector.tensor_copy(l_pick[:, :], l_topi[:, 0:TOP1]))
                        count.sync(dve)
                        for k in range(TOP1):
                            count.did(nc.vector.tensor_scalar(l_mask[:, k, :], table("iota32")[:, 0:EX1],
                                                              l_pick[:, k:k + 1], None, ALU.is_equal))
                        count.sync(dve)
                        count.did(nc.vector.tensor_tensor(l_mask[:, 0, :], l_mask[:, 0, :], l_mask[:, 1, :],
                                                          ALU.add))
                        count.sync(dve)
                        dve.wait_ge(l_prob_ready, n + 1)
                        nc.vector.tensor_tensor(l_p[:, p0, 0:EX1], l_mask[:, 0, :], l_prob[:, :],
                                                ALU.mult).then_inc(l_p_ready, 1)
                if live(n, 2):
                    dve.wait_ge(l_out_in_psum, n - 1)
                    nc.vector.tensor_tensor(x_sb[:, n - 2, :], bank[:, 6, 0:D], x_sb[:, n - 2, :],
                                            ALU.add).then_inc(x_ready, 1)

            count.did(nc.vector.memset(l_p[:, :, EX1:EXS], 1.0))
            pipeline(dve, step, 4, 2, 2, count, EXS + PAIRS - 1 + 6)

        @block.tensor
        def _(pe):
            attn_tensor(pe)
            cross_tensor(pe, 0, NB, NB)
            shared_tensor(pe, 2 * NB)
            expert_tensor(pe)
            shift_tensor(pe, 4 * NB)
            cross_tensor(pe, 1, 5 * NB, 4 * NB)
            mlp_tensor(pe, 6 * NB)

        @block.scalar
        def _(act):
            attn_scalar(act)
            cross_scalar(act, 0, NB, NB)
            shared_scalar(act, 2 * NB)
            expert_scalar(act)
            shift_scalar(act, 4 * NB)
            cross_scalar(act, 1, 5 * NB, 4 * NB)
            mlp_scalar(act, 6 * NB)

        @block.vector
        def _(dve):
            attn_vector(dve)
            cross_vector(dve, 0, NB, NB)
            shared_vector(dve, 2 * NB)
            expert_vector(dve)
            collect_vector(dve, 3 * NB)
            shift_vector(dve, 4 * NB, 3 * NB)
            cross_vector(dve, 1, 5 * NB, 4 * NB)
            mlp_vector(dve, 6 * NB, 5 * NB)

        @block.gpsimd
        def _(pool):
            nc.gpsimd.memset(minus_half[:, :], -0.5).then_inc(const_ready, 1)
            nc.gpsimd.memset(zero_eps[:, 0:1], 0.0).then_inc(const_ready, 1)
            nc.gpsimd.memset(zero_eps[:, 1:2], EPS).then_inc(const_ready, 1)
            pool.wait_ge(const_ready, 3)
            attn_gpsimd(pool)
            nc.gpsimd.memset(c_vT[:, :, :, :, :], 0.0).then_inc(pad_ready, 1)
            for b in range(NB):
                pool_rstd(pool, b, NB)
            nc.gpsimd.memset(g_y[:, :, :, :], 0.0).then_inc(y_zero, 1)
            cross_gpsimd(pool, 0, NB, NB)
            dispatch_gpsimd(pool)
            collect_gpsimd(pool, 3 * NB)
            shift_gpsimd(pool, 4 * NB, 3 * NB)
            cross_gpsimd(pool, 1, 5 * NB, 4 * NB)

        @block.sync
        def _(sp):
            sp.dma_start(const[:, :], A["const"]).then_inc(const_loaded, 16)
            for q in range(4):
                sp.dma_start(x_sb[:, 4 * q:4 * q + 4, :],
                             A["x"][4 * q:4 * q + 4].rearrange("b t d -> t b d")).then_inc(x_loaded, 16)
            for t, name in ((wqk[:, :, 0:D], "wqT"), (wqk[:, :, D:2 * D], "wkT"), (wv[:, :, :], "wvT"),
                            (wo[:, :, :], "woT")):
                sp.dma_start(t, A[name].rearrange("(t p) o -> p t o", p=128)).then_inc(w_loaded, 16)
            sp.dma_start(bern[:, 0, :], A["bern_u"].to_broadcast([NK0, H0])).then_inc(w_loaded, 16)
            sp.wait_ge(x_ready, NB)
            for t, name in ((m_wr, "routerT"), (m_wgu, "shared_guT"), (m_wdn, "shared_downT")):
                sp.dma_start(t[:, :, :], A[name].rearrange("(t p) o -> p t o", p=128)
                             ).then_inc(m_w_loaded, 16)
            sp.dma_start(m_bias[:, :], A["e_bias"].to_broadcast([128, EX0])).then_inc(m_w_loaded, 16)
            for e in range(RING):
                load_expert(sp, e, e)
            for t, name in ((f_wshift[:, :, :], "shiftT"), (f_wkv[:, 0], "kvT")):
                sp.dma_start(t, A[name].rearrange("(t p) o -> p t o", p=128)).then_inc(f_loaded, 16)
            sp.dma_start(f_wo[:, :], A["outT"]).then_inc(f_loaded, 16)
            sp.dma_start(f_gate[:, 0, :], A["gate"].to_broadcast([128, D])).then_inc(f_loaded, 16)
            for i, name in enumerate(("ln_gamma", "ln_beta")):
                sp.dma_start(f_affine[:, i, :], A[name]).then_inc(f_loaded, 16)
            for i, name in enumerate(("time_decay", "time_first")):
                sp.dma_start(f_time[:, i:i + 1], A[name]).then_inc(f_loaded, 16)
            sp.wait_ge(y_zero, 1)
            for i in range(5):
                sp.dma_start(xp_dram[bass.ds(i * 512, 512), :].rearrange("(p r) d -> p (r d)", p=128),
                             g_y[:, i % GB].rearrange("p k d -> p (k d)")).then_inc(slots_zero, 16)
            cross_sync(sp, 0, NB, NB)
            expert_sync(sp)
            sp.wait_ge(d_y_in_psum, EX0)
            sp.dma_start(l_wr[:, :, :], A["router1"].rearrange("(t p) o -> p t o", p=128)
                         ).then_inc(l_loaded, 16)
            for t in range(KT):
                sp.dma_start(wgu[:, 0:EX1, t, :],
                             A["gate_up"][:, t * 128:(t + 1) * 128, :].rearrange("e p i -> p e i")
                             ).then_inc(l_loaded, 16)
            sp.dma_start(wgu[:, EX1], A["shared1_gu"].rearrange("(t p) i -> p t i", p=128)
                         ).then_inc(l_loaded, 16)
            sp.dma_start(wdn[:, 0:EX1, :], A["down"].rearrange("e p o -> p e o")).then_inc(l_loaded, 16)
            sp.dma_start(wdn[:, EX1, :], A["shared1_down"]).then_inc(l_loaded, 16)
            cross_sync(sp, 1, 5 * NB, 4 * NB)
            for q in range(NB // 2):
                sp.wait_ge(x_ready, 6 * NB + 2 * q + 2)
                sp.dma_start(out[2 * q:2 * q + 2].rearrange("b t d -> t b d"),
                             x_sb[:, 2 * q:2 * q + 2, :]).then_inc(out_stored, 16)
            sp.wait_ge(out_stored, 16 * (NB // 2))


def kernel(**inputs):
    import numpy as np
    import concourse.bacc as bacc
    from concourse import mybir as mb
    from concourse.bass_utils import run_bass_kernel_spmd

    laid = layout(inputs)
    nc = bacc.Bacc("TRN2", target_bir_lowering=False, num_devices=1)
    arrays, A = {}, {}
    for name, a in laid.items():
        a = np.ascontiguousarray(a)
        arrays[f"in_{name}"] = a
        A[name] = nc.dram_tensor(f"in_{name}", a.shape, mb.dt.from_np(a.dtype), kind="ExternalInput").ap()
    out = nc.dram_tensor("out_0", (NB, T, D), F32, kind="ExternalOutput").ap()
    decoder_kernel(nc, A, out)
    r = run_bass_kernel_spmd(nc, [arrays], core_ids=[0])
    return r.results[0]["out_0"]


def layout(inputs):
    import numpy as np

    i = {k: np.asarray(v) for k, v in inputs.items()}
    return {
        "x": i["x"], "context": i["ctx_2048"], "contextT": i["ctx_2048"].transpose(0, 2, 1), "const": constants(),
        "wqT": i["L0_attn_wq"].T, "wkT": i["L0_attn_wk"].T, "wvT": i["L0_attn_wv"].T,
        "routerT": i["L0_ffn_router_w"].T, "e_bias": i["L0_ffn_e_bias"][None],
        "shared_guT": np.concatenate([i["L0_ffn_shared_gate"].T, i["L0_ffn_shared_up"].T], axis=1),
        "shared_downT": i["L0_ffn_shared_down"].T,
        "W_gu": np.concatenate([i["L0_ffn_W_gate"], i["L0_ffn_W_up"]], axis=2),
        "W_down": i["L0_ffn_W_down"],
        "shiftT": i["L1_attn_W_shift"].T,
        "kvT": np.concatenate([i["L1_attn_W_key"].T, i["L1_attn_W_value"].T], axis=1),
        "outT": i["L1_attn_W_output"].T, "gate": i["L1_attn_gate"][None],
        "ln_gamma": i["L1_attn_ln_gamma"].reshape(KT, 128).T,
        "ln_beta": i["L1_attn_ln_beta"].reshape(KT, 128).T,
        "time_decay": i["L1_attn_time_decay"][:, None], "time_first": i["L1_attn_time_first"][:, None],
        "router1": i["L1_ffn_router_w"], "gate_up": i["L1_ffn_gate_up_w"], "down": i["L1_ffn_down_w"],
        "shared1_gu": np.concatenate([i["L1_ffn_shared_gate_w"], i["L1_ffn_shared_up_w"]], axis=1),
        "shared1_down": i["L1_ffn_shared_down_w"],
        "woT": i["L0_attn_wo"].T, "bern_u": i["L0_attn_bern_u"],
    }
```

```python
from contextlib import ExitStack

import concourse.bass as bass
from concourse import mybir

F32 = mybir.dt.float32
BF16 = mybir.dt.bfloat16
I32 = mybir.dt.int32
U32 = mybir.dt.uint32
ALU = mybir.AluOpType
ACT = mybir.ActivationFunctionType
AX = mybir.AxisListType

NB, T, D = 16, 128, 256
KT = D // 128
EPS = 1e-5

H0, HD0 = 16, 16
SINK = int(0.1 * T)
RECENT = int(0.5 * T)
REC0 = T - RECENT
NK0 = SINK + RECENT
HG = 128 // HD0

HX = 8
DX = T // HX
TERMS = 6
QPART = (0, 1, 2, 0, 1, 0)
KPART = (0, 0, 0, 1, 1, 2)
NSTACK = TERMS * DX


CONST_AT, CONST_COLS = {}, 0
for _name, _width in (("ident", 128), ("key_of_head", HG), ("spread", NK0), ("pick3", 3), ("ones", 128),
                      ("half_ones", 64), ("rope_cos", HD0), ("rope_sin", HD0), ("group_ones", 128),
                      ("before", 128), ("iota32", 32)):
    CONST_AT[_name] = (CONST_COLS, _width)
    CONST_COLS += _width


def constants():
    import numpy as np

    p = np.arange(128)
    t = {k: np.zeros((128, w), np.float32) for k, (_, w) in CONST_AT.items()}
    t["ident"][p, p] = 1
    t["key_of_head"][p, p // HD0] = 1
    t["spread"][SINK, SINK + 1:] = 1.0 / RECENT
    t["pick3"][SINK, 0] = 1
    t["pick3"][SINK + 1:NK0, 1] = 1
    t["pick3"][:NK0, 2] = 1
    t["ones"][:] = 1
    t["half_ones"][:, 0:16] = 1
    t["half_ones"][:, 48:64] = 1
    freq = 1.0 / np.float32(10000.0) ** (np.arange(0, HD0, 2, dtype=np.float32) / HD0)
    angle = (p.astype(np.float32)[:, None] * freq[None, :].astype(np.float32)).astype(np.float32)
    t["rope_cos"][:] = np.tile(np.cos(angle), 2)
    t["rope_sin"][:] = np.concatenate([-np.sin(angle), np.sin(angle)], axis=1)
    t["group_ones"][:] = p[:, None] // DX == p[None, :] // DX
    t["iota32"][:] = np.arange(32)
    t["before"][:] = p[:, None] < p[None, :]
    return np.concatenate([t[k] for k in CONST_AT], axis=1)


EX0, TOP0, GROUPS, TOPG = 32, 4, 8, 3
CAP = -(-5 * NB * T // (4 * EX0))
SLOTS = EX0 * CAP
I0 = 128
SH0 = 2 * I0
DROPPED = 8192.0
NS = 64
EX1, TOP1, I1 = 8, 2, 128
EXS = EX1 + 1


def await_count(eng, sem, count):
    if isinstance(count, int) and count <= 0:
        return
    eng.wait_ge(sem, count)


def hold(eng):
    eng.nop(nofuse=True)


def live(n, k, total=NB):
    return not isinstance(n, int) or 0 <= n - k < total


def seen(n, k=0):
    return min(n - k, NB - 1) + 1 if isinstance(n, int) else n - k + 1


class Count:

    def __init__(self, sem):
        self.sem, self.base, self.n = sem, 0, 0

    def did(self, ins):
        ins.then_inc(self.sem, 1)
        self.n += 1

    def sync(self, eng, but=0):
        await_count(eng, self.sem, self.base + self.n - but)


def buffer_uses(n, past=0):
    return lambda k, m: (n - k + past) // m + 1


def pipeline(eng, step, head, unroll, last_phase, count=None, per_step=0, total=NB,
             past=0, per_turn=None, begun=0, between=None):
    def peeled(n):
        step(n, n, buffer_uses(n, past))

    def looped(j, c):
        step(j * unroll + c, c, lambda k, m: j * (unroll // m) + ((c - k + past) // m + 1))

    for n in range(begun, head):
        peeled(n)
    turns = (total - head) // unroll
    assert turns * unroll == total - head
    if count is not None:
        base, n0 = count.base + count.n, per_turn or per_step * unroll
    with eng.Fori(0, turns) as j:
        if count is not None:
            count.base, count.n = j * n0 + base, 0
        for u in range(unroll):
            looped(j, head + u)
        if count is not None:
            assert count.n == n0, (count.n, n0)
    if count is not None:
        count.base, count.n = base + turns * n0, 0
    for n in range(total, total + last_phase):
        peeled(n)
        if between is not None:
            between(n - total)


def decoder_kernel(nc, A, out):
    with ExitStack() as ctx:
        def keep(name, shape, dt=F32):
            return ctx.enter_context(nc.sbuf_tensor(name, shape, dt))

        def sem(name):
            return ctx.enter_context(nc.semaphore(name))

        bank = ctx.enter_context(nc.psum_tensor("bank", [128, 8, 512], F32))
        x_sb = keep("x_sb", [128, NB, D])
        moments = keep("moments", [128, NB, 2])
        mean_var = keep("mean_var", [128, 2, 2])
        zero_eps = keep("zero_eps", [128, 2])
        rstd = keep("rstd", [128, NB])
        minus_half = keep("minus_half", [128, 1])
        bn6 = keep("bn6", [128, 3, 6])
        const = keep("const", [128, CONST_COLS])

        def table(name, rows=128):
            at, width = CONST_AT[name]
            return const[0:rows, at:at + width]

        ident = table("ident")

        x_loaded = [sem(f"x_loaded{i}") for i in range(4)]
        const_loaded = sem("const_loaded")
        stats_ready = sem("stats_ready")
        rstd_ready = sem("rstd_ready")
        x_ready = sem("x_ready")
        out_stored = sem("out_stored")
        dve_chain, act_chain = Count(sem("dve_done")), Count(sem("act_done"))

        NBUF = 4
        STACK_DMAS = 6
        PART_DMAS = 6
        ORDER = (0, 2, 4, 6, 1, 3, 5, 7)
        c_rows = keep("c_rows", [128, 4, 2 * D])
        c_raw = c_rows[:, 0:2]
        c_unit = c_rows[:, 2:4]
        c_rest = keep("c_rest", [128, 2, 2 * D])
        c_part = keep("c_part", [128, 2, 3, 2 * D], BF16)
        q_stack = keep("q_stack", [128, NBUF, HX, D], BF16)
        k_stack = keep("k_stack", [128, NBUF, HX, D], BF16)
        c_vT_in = keep("c_vT_in", [128, 2, 2, T])
        c_vT = keep("c_vT", [128, 2, 2, HX, 32])
        c_max = keep("c_max", [128, 2, HX, 2])
        c_neg = keep("c_neg", [2 * HX, 3, 128], BF16)
        c_nrest = keep("c_nrest", [2 * HX, 2, 128])
        c_e = keep("c_e", [128, HX, 2, D])
        c_inv = keep("c_inv", [128, D])
        c_att = keep("c_att", [128, D])
        c_sq = keep("c_sq", [128, 2 * D])
        c_ss = keep("c_ss", [128, 2 * D])
        part_dram = nc.dram_tensor("part_dram", (2, 2, 3 * DX, HX, D), BF16).ap()
        neg_dram = nc.dram_tensor("neg_dram", (2, 2 * HX, 3, 128), BF16).ap()
        pad_ready = sem("pad_ready")

        cross = {k: [sem(f"c_{k}{i}") for i in range(m)] for k, m in (
            ("ctx_in", 2), ("vT_in", 2), ("neg_in", NBUF), ("stack_in", NBUF))}
        cross |= {k: sem(f"c_{k}") for k in (
            "h_ready", "sq_ready", "ss_in_psum", "ss_ready", "inv_norm", "unit_ready",
            "hi", "rest1", "mid", "rest2", "lo", "part_stored", "s_in_psum", "max_ready",
            "maxT_in_psum", "neg_ready", "neg_stored", "sT_in_psum", "e_ready", "pv_done",
            "vT_ready", "inv_ready")}

        scope = ExitStack()

        def sb(name, shape, dt=F32):
            return scope.enter_context(nc.sbuf_tensor(name, shape, dt))

        wqk = sb("wqk", [128, KT, 2 * D])
        wv = sb("wv", [128, KT, D])
        wo = sb("wo", [128, KT, D])
        rope_cos, rope_sin = table("rope_cos"), table("rope_sin")
        key_of_head = table("key_of_head")
        spread = table("spread", NK0)
        pick3 = table("pick3", NK0)
        ones = table("ones")
        half_ones = table("half_ones").rearrange("p (o c) -> p o c", o=2)
        bern = sb("bern", [NK0, 3, H0])
        in_bn6 = sb("in_bn6", [128, 4, 4, 6])
        in_moments = sb("in_moments", [128, 4, 4, 2])
        a_h = sb("a_h", [128, 2, D])
        a_hT = sb("a_hT", [128, 2, KT, T])
        a_hTk = sb("a_hTk", [128, 2, KT, NK0])
        VBUF = 4
        a_v = sb("a_v", [NK0, VBUF, D])
        a_rot = sb("a_rot", [128, 2 * D])
        a_cos = sb("a_cos", [128, 2 * D])
        a_qk = sb("a_qk", [128, 2, 2 * D])
        a_qT = sb("a_qT", [128, 2, KT, T])
        a_kb = sb("a_kb", [128, 2, KT, HG, NK0])
        a_max = sb("a_max", [128, H0])
        a_p = sb("a_p", [128, 2, H0, NK0])
        a_pT = sb("a_pT", [NK0, 2, H0, T])
        a_e3 = sb("a_e3", [NK0, 3, H0])
        a_lim = sb("a_lim", [NK0, 3, H0])
        a_add = sb("a_add", [NK0, D])
        a_vp = sb("a_vp", [NK0, H0, 32])
        a_inv = sb("a_inv", [128, 2 * T])
        a_oT = sb("a_oT", [128, 2, KT, T])
        w_loaded = sem("w_loaded")
        const_ready = sem("const_ready")
        a_h_ready = sem("a_h_ready")
        a_hT_in_psum = sem("a_hT_in_psum")
        a_hT_ready = sem("a_hT_ready")
        a_qkv_in_psum = sem("a_qkv_in_psum")
        a_v_ready = sem("a_v_ready")
        a_qk_ready = sem("a_qk_ready")
        a_qkT_in_psum = sem("a_qkT_in_psum")
        a_qT_ready = sem("a_qT_ready")
        a_kb_ready = sem("a_kb_ready")
        a_s_in_psum = sem("a_s_in_psum")
        a_s_shifted = sem("a_s_shifted")
        a_p_ready = sem("a_p_ready")
        a_pT_in_psum = sem("a_pT_in_psum")
        a_pT_ready = sem("a_pT_ready")
        a_e3_ready = sem("a_e3_ready")
        a_spread_in_psum = sem("a_spread_in_psum")
        a_vp_ready = sem("a_vp_ready")
        a_o_in_psum = sem("a_o_in_psum")
        a_inv_ready = sem("a_inv_ready")
        a_oT_ready = sem("a_oT_ready")
        a_out_in_psum = sem("a_out_in_psum")

        scope.close()
        ctx.callback(scope.close)

        h_all = sb("h_all", [128, NB, D])
        m_hc = sb("m_hc", [128, 2, D])
        RING = 8
        wgu = sb("wgu", [128, EXS, KT, 2 * I0])
        wdn = sb("wdn", [128, EXS, D])
        m_wr = sb("m_wr", [128, KT, EX0])
        m_wgu = sb("m_wgu", [128, KT, 2 * SH0])
        m_wdn = sb("m_wdn", [128, KT, D])
        m_hT = sb("m_hT", [128, 2, KT, T])
        m_sig = sb("m_sig", [128, 2, SH0])
        m_hid = sb("m_hid", [128, 2, SH0])
        m_hidT = sb("m_hidT", [128, KT, T])
        m_bias = sb("m_bias", [128, EX0])
        RG = 4
        SGU = (2, 6)
        r_score = sb("r_score", [128, RG, EX0])
        r_own = sb("r_own", [128, RG, EX0])
        r_sc = sb("r_sc", [128, RG, EX0])
        r_hot = sb("r_hot", [128, RG, TOP0, EX0])
        r_t = sb("r_t", [128, RG, TOP0, EX0])
        r_g = [sb(f"r_g{i}", [128, RG, GROUPS]) for i in range(6)]
        r_top = sb("r_top", [128, RG, 8])
        r_topi = sb("r_topi", [128, RG, 8], U32)
        r_pick = sb("r_pick", [128, RG, TOP0])
        r_chosen = sb("r_chosen", [128, RG, EX0])
        r_seen = sb("r_seen", [128, EX0])
        r_all = sb("r_all", [128, EX0])
        r_w = sb("r_w", [128, RG, TOP0])
        r_sum = sb("r_sum", [128, RG])
        r_k = [sb(f"r_k{i}", [128, RG, TOP0]) for i in range(3)]
        m_w = sb("m_w", [128, NB, TOP0])
        m_slot = sb("m_slot", [128, NB, TOP0], U32)
        r_taken, m_logit_in_psum, m_hall_ready = (sem(x) for x in (
            "r_taken", "m_logit_in_psum", "m_hall_ready"))
        XBUF = 4
        STORE = 5
        GU = (1, 4)
        d_x = sb("d_x", [CAP, XBUF, D])
        d_xT = sb("d_xT", [128, 2, KT, CAP])
        d_sig = sb("d_sig", [CAP, I0])
        d_hid = sb("d_hid", [CAP, 2, I0])
        d_hidT = sb("d_hidT", [128, 2, CAP])
        d_y = sb("d_y", [CAP, 2, D])
        GB = 4
        g_y = sb("g_y", [128, GB, TOP0, D])
        xp_dram = nc.dram_tensor("xp_dram", (SLOTS, D), F32).ap()
        y_dram = nc.dram_tensor("y_dram", (SLOTS + 1, D), F32).ap()
        m_w_loaded = sem("m_w_loaded")
        ring_in = [sem(f"ring_in{i}") for i in range(RING)]
        slots_zero, y_zero, y_used = sem("slots_zero"), sem("y_zero"), sem("y_used")
        collect_stats, collect_rstd = sem("collect_stats"), sem("collect_rstd")
        (m_h_ready, m_hT_in_psum, m_hT_ready, m_gu_in_psum, m_sig_ready, m_hid_ready, m_hidT_in_psum,
         m_hidT_ready, m_out_in_psum, m_s_ready, m_hot_ready, m_rank_in_psum, m_slot_ready, rows_sent) = (
            sem(x) for x in (
                "m_h_ready", "m_hT_in_psum", "m_hT_ready", "m_gu_in_psum", "m_sig_ready", "m_hid_ready",
                "m_hidT_in_psum", "m_hidT_ready", "m_out_in_psum", "m_s_ready", "m_hot_ready",
                "m_rank_in_psum", "m_slot_ready", "rows_sent"))
        d_x_in = [sem(f"d_x_in{i}") for i in range(XBUF)]
        (d_xT_in_psum, d_xT_ready, d_gu_in_psum, d_sig_ready, d_hid_ready, d_hidT_in_psum, d_hidT_ready,
         d_y_in_psum, d_y_ready) = (sem(x) for x in (
             "d_xT_in_psum", "d_xT_ready", "d_gu_in_psum", "d_sig_ready", "d_hid_ready", "d_hidT_in_psum",
             "d_hidT_ready", "d_y_in_psum", "d_y_ready"))
        y_stored = [sem(f"y_stored{i}") for i in range(2)]
        y_in = [sem(f"y_in{i}") for i in range(GB)]

        f_wshift = sb("f_wshift", [128, KT, D])
        f_wkv = sb("f_wkv", [128, 2, KT, 2 * NS])
        f_wo = sb("f_wo", [NS, D])
        f_gate = sb("f_gate", [128, 2, D])
        f_affine = sb("f_affine", [128, 2, KT])
        f_time = sb("f_time", [NS, 4])
        f_decay = sb("f_decay", [NS, T])
        f_bias = sb("f_bias", [NS, 3])
        f_h = h_all[:, 10:12, :]
        f_hT = h_all[:, 12:14, :].rearrange("p b (t c) -> p b t c", t=KT)
        f_part = sb("f_part", [128, 2, D])
        f_xs = h_all[:, 14:16, :]
        f_mom = sb("f_mom", [128, 2, 2])
        f_var = sb("f_var", [128, 2])
        f_rstd = sb("f_rstd", [128, 2])
        f_z = sb("f_z", [128, D])
        f_zT = sb("f_zT", [128, KT, T])
        f_k = sb("f_k", [NS, 2, T])
        f_wkvx = sb("f_wkvx", [NS, T])
        f_state = sb("f_state", [NS, 2, T])
        (f_loaded, f_pe, f_h_ready, f_hT_in_psum, f_hT_ready, f_shift_in_psum, f_xs_ready, f_var_ready,
         f_rstd_ready, f_z_ready, f_zT_in_psum, f_zT_ready, f_kv_in_psum, f_k_ready, f_wkvx_ready,
         f_state_ready, f_out_in_psum, f_gate_exp, f_setup) = (sem(x) for x in (
             "f_loaded", "f_pe", "f_h_ready", "f_hT_in_psum", "f_hT_ready", "f_shift_in_psum",
             "f_xs_ready", "f_var_ready", "f_rstd_ready", "f_z_ready", "f_zT_in_psum", "f_zT_ready",
             "f_kv_in_psum", "f_k_ready", "f_wkvx_ready", "f_state_ready", "f_out_in_psum", "f_gate_exp",
             "f_setup"))
        PAIRS = -(-EXS // 2)
        l_wr = sb("l_wr", [128, KT, EX1])
        l_h = m_hc
        HBUF = 4
        l_hT = h_all[:, EXS:EXS + HBUF, :].rearrange("p b (t c) -> p b t c", t=KT)
        l_logit = sb("l_logit", [128, EX1])
        l_top = sb("l_top", [128, 8])
        l_topi = sb("l_topi", [128, 8], U32)
        l_pick = sb("l_pick", [128, TOP1])
        l_mask = sb("l_mask", [128, TOP1, EX1])
        l_p = sb("l_p", [128, 2, EXS])
        l_prob = sb("l_prob", [128, EX1])
        l_sig, l_hid = m_sig, m_hid
        l_hidT = h_all[:, 0:EXS, :].rearrange("p b (i c) -> p (b i) c", c=T).rearrange(
            "p (b e) c -> p b e c", b=2)
        l_top_ready, l_index_ready, l_pick_ready = (sem(x) for x in (
            "l_top_ready", "l_index_ready", "l_pick_ready"))
        (l_loaded, l_h_ready, l_hT_in_psum, l_hT_ready, l_logit_in_psum, l_logit_ready, l_prob_ready, l_p_ready,
         l_gu_in_psum, l_sig_ready, l_hid_ready, l_hidT_in_psum, l_hidT_ready, l_out_in_psum) = (
             sem(x) for x in (
                 "l_loaded", "l_h_ready", "l_hT_in_psum", "l_hT_ready", "l_logit_in_psum", "l_logit_ready",
                 "l_prob_ready", "l_p_ready", "l_gu_in_psum", "l_sig_ready", "l_hid_ready", "l_hidT_in_psum",
                 "l_hidT_ready", "l_out_in_psum"))

        block = ctx.enter_context(nc.Block())

        def stats(dve, count, b, ready=None, way=0):
            for part in range(3):
                if part:
                    count.sync(dve)
                stats_part(dve, count, b, part, ready, way)

        def stats_part(dve, count, b, part, ready=None, way=0):
            if part == 0:
                hold(dve)
                count.did(nc.vector.bn_stats(bn6[:, way, :], x_sb[:, b, :]))
            elif part == 1:
                hold(dve)
                count.did(nc.vector.bn_aggr(mean_var[:, way, :], bn6[:, way, :]))
            else:
                nc.vector.tensor_tensor(moments[:, b, :], mean_var[:, way, :], zero_eps[:, :],
                                        ALU.add).then_inc(ready or stats_ready, 1)

        def pool_rstd(pool, b, done, stats_of=None, ready=None):
            await_count(pool, stats_of or stats_ready, done + b + 1)
            nc.gpsimd.tensor_tensor(rstd[:, bass.ds(b, 1)], moments[:, b, 1:2], minus_half[:, 0:1],
                                    ALU.pow).then_inc(ready or rstd_ready, 1)

        s_bank = bank[:, 4:8, 0:4 * NK0].rearrange("p b (h k) -> p b h k", h=4)

        def attn_tensor(pe):
            def step(n, u, uses):
                p0, p1 = u % 2, (u - 1) % 2
                if live(n, 4):
                    pe.wait_ge(a_p_ready, n - 3)
                    for h in range(H0):
                        mm = nc.tensor.transpose(
                            bank[0:NK0, 4 + h // 4, (h % 4) * T:(h % 4 + 1) * T], a_p[:, p0, h, :],
                            ident)
                        if h % 4 == 3:
                            mm.then_inc(a_pT_in_psum, 1)
                if live(n, 2):
                    pe.wait_ge(a_qk_ready, n - 1)
                    await_count(pe, a_oT_ready, n - 5)
                    for t in range(2 * KT):
                        mm = nc.tensor.transpose(bank[:, 3, t * T:(t + 1) * T],
                                                 a_qk[:, p0, t * 128:(t + 1) * 128], ident)
                    mm.then_inc(a_qkT_in_psum, 1)
                if live(n, 6):
                    pe.wait_ge(a_oT_ready, n - 5)
                    await_count(pe, a_vp_ready, 2 * seen(n, 5))
                    for t in range(KT):
                        mm = nc.tensor.matmul(bank[:, 0, 0:D], a_oT[:, p0, t, :], wo[:, t, :],
                                              start=(t == 0), stop=(t == KT - 1))
                    mm.then_inc(a_out_in_psum, 1)
                if live(n, 3):
                    pe.wait_ge(a_kb_ready, 2 * (n - 2))
                    pe.wait_ge(a_qT_ready, n - 2)
                    for q in range(4):
                        await_count(pe, a_pT_ready, 4 * seen(n, 4) - 3 + q)
                        mm = nc.tensor.matmul(
                            s_bank[:, q, :, :], a_qT[:, p1, q // 2, :],
                            a_kb[:, p1, q // 2, 4 * (q % 2):4 * (q % 2) + 4, :], start=True, stop=True)
                    mm.then_inc(a_s_in_psum, 1)
                if live(n, 0):
                    pe.wait_ge(a_h_ready, n + 1)
                    await_count(pe, a_hT_ready, 3 * n)
                    await_count(pe, x_ready, n - 5)
                    await_count(pe, a_vp_ready, 2 * (n - 4))
                    for t in range(KT):
                        mm = nc.tensor.transpose(bank[:, 0, t * T:(t + 1) * T],
                                                 a_h[:, p0, t * 128:(t + 1) * 128], ident)
                    mm.then_inc(a_hT_in_psum, 1)
                if live(n, 4):
                    pe.wait_ge(a_e3_ready, n - 3)
                    await_count(pe, x_ready, seen(n, 6))
                    await_count(pe, a_hT_ready, 3 * seen(n, 0))
                    nc.tensor.matmul(bank[0:NK0, 0, 0:D], spread, a_v[:, u % VBUF, :],
                                     start=True, stop=True)
                    mm = nc.tensor.matmul(bank[0:NK0, 0, D:D + 3 * H0], ones[0:NK0, 0:NK0],
                                          a_e3[:, :, :].rearrange("p a h -> p (a h)"),
                                          start=True, stop=True)
                    mm.then_inc(a_spread_in_psum, 1)
                if live(n, 1):
                    pe.wait_ge(a_hT_ready, 3 * n)
                    await_count(pe, a_qk_ready, n - 1)
                    for t in range(KT):
                        nc.tensor.matmul(bank[:, 1, :], a_hT[:, p1, t, :], wqk[:, t, :],
                                         start=(t == 0), stop=(t == KT - 1))
                    await_count(pe, a_v_ready, n - 1)
                    for t in range(KT):
                        mm = nc.tensor.matmul(bank[0:NK0, 2, 0:D], a_hTk[:, p1, t, :], wv[:, t, :],
                                              start=(t == 0), stop=(t == KT - 1))
                    mm.then_inc(a_qkv_in_psum, 1)
                if live(n, 5):
                    pe.wait_ge(a_vp_ready, 2 * (n - 4))
                    await_count(pe, a_qT_ready, seen(n, 2))
                    await_count(pe, a_kb_ready, 2 * seen(n, 2))
                    for g in range(KT):
                        for den in range(2):
                            col = (den * KT + g) * T
                            for odd in range(2):
                                for j in range(4):
                                    h = HG * g + 2 * j + odd
                                    w = half_ones[0:NK0, odd, :] if den else a_vp[:, h, :]
                                    mm = nc.tensor.matmul(
                                        bank[32 * j:32 * j + 32, 3, col:col + T], w, a_pT[:, p1, h, :],
                                        start=(odd == 0), stop=(odd == 1))
                    mm.then_inc(a_o_in_psum, 1)

            pe.wait_ge(const_loaded, 16)
            pe.wait_ge(w_loaded, 16 * 5)
            pipeline(pe, step, 8, 4, 6)

        def attn_scalar(act):
            nc.scalar.preload_act_table_set("natural_log_exp_and_others")
            count = act_chain

            def step(n, u, uses):
                p0, p1 = u % 2, (u - 1) % 2
                if live(n, 4):
                    await_count(act, a_o_in_psum, n - 5)
                    for q in range(4):
                        act.wait_ge(a_pT_in_psum, 4 * (n - 4) + q + 1)
                        nc.scalar.copy(a_pT[:, p0, 4 * q:4 * q + 4, :].rearrange("p h c -> p (h c)"),
                                       bank[0:NK0, 4 + q, :]).then_inc(a_pT_ready, 1)
                if live(n, 2):
                    act.wait_ge(a_qkT_in_psum, n - 1)
                    await_count(act, a_s_in_psum, n - 3)
                    nc.scalar.copy(a_qT[:, p0].rearrange("p t c -> p (t c)"),
                                   bank[:, 3, 0:KT * T]).then_inc(a_qT_ready, 1)
                if live(n, 0):
                    act.wait_ge(a_hT_in_psum, n + 1)
                    await_count(act, a_qkv_in_psum, n - 1)
                    src = bank[:, 0, 0:D].rearrange("p (t c) -> p t c", t=KT)
                    nc.scalar.copy(a_hT[:, p0], src).then_inc(a_hT_ready, 1)
                    nc.scalar.copy(a_hTk[:, p0, :, 0:SINK], src[:, :, 0:SINK]).then_inc(a_hT_ready, 1)
                    nc.scalar.copy(a_hTk[:, p0, :, SINK:NK0], src[:, :, REC0:T]).then_inc(a_hT_ready, 1)
                if live(n, 3):
                    act.wait_ge(a_s_shifted, n - 2)
                    nc.scalar.activation(a_p[:, p1], a_p[:, p1], ACT.Exp,
                                         scale=HD0 ** -0.5).then_inc(a_p_ready, 1)
                if live(n, 1):
                    act.wait_ge(a_qkv_in_psum, n)
                    await_count(act, a_vp_ready, 2 * (n - VBUF))
                    nc.scalar.copy(a_v[:, (u - 1) % VBUF, :], bank[0:NK0, 2, 0:D]).then_inc(a_v_ready, 1)
                if live(n, 5):
                    act.wait_ge(a_o_in_psum, n - 4)
                    await_count(act, a_oT_ready, n - 5)
                    count.did(nc.scalar.activation(a_inv[:, :], bank[:, 3, KT * T:2 * KT * T], ACT.Ln))
                    count.sync(act)
                    nc.scalar.activation(a_inv[:, :], a_inv[:, :], ACT.Exp,
                                         scale=-1.0).then_inc(a_inv_ready, 1)

            early = ([(0, 0)], [(0, 1)], [(0, 2), (1, 0)], [(1, 1)], [(1, 2)])
            pipeline(act, step, 8, 4, 5, count, 1, between=lambda i: cross_scalar(act, 0, NB, NB, early[i]))

        def attn_vector(dve):
            count = dve_chain

            def step(n, u, uses):
                p0, p1 = u % 2, (u - 1) % 2
                if live(n, 6):
                    dve.wait_ge(a_inv_ready, n - 5)
                    await_count(dve, a_out_in_psum, n - 7)
                    nc.vector.tensor_tensor(a_oT[:, p0].rearrange("p t c -> p (t c)"),
                                            bank[:, 3, 0:KT * T], a_inv[:, :],
                                            ALU.mult).then_inc(a_oT_ready, 1)
                if live(n, 0):
                    dve.wait_ge(rstd_ready, n + 1)
                    await_count(dve, a_hT_in_psum, n - 1)
                    nc.vector.tensor_scalar(a_h[:, p0, :], x_sb[:, n, :], moments[:, n, 0:1],
                                            rstd[:, bass.ds(n, 1)], ALU.subtract, ALU.mult).then_inc(a_h_ready, 1)
                if live(n, 2):
                    dve.wait_ge(a_qT_ready, n - 1)
                    await_count(dve, a_s_in_psum, n - 3)
                    kT = bank[:, 3, KT * T:2 * KT * T].rearrange("p (t c) -> p t c", t=KT)
                    for c0, c1, k0 in ((0, SINK, 0), (SINK, NK0, REC0)):
                        w = c1 - c0
                        nc.vector.tensor_tensor(
                            a_kb[:, p0, :, :, c0:c1],
                            kT[:, :, k0:k0 + w].unsqueeze(2).to_broadcast([128, KT, HG, w]),
                            key_of_head.unsqueeze(1).unsqueeze(3).to_broadcast([128, KT, HG, w]),
                            ALU.mult).then_inc(a_kb_ready, 1)
                if live(n, 6):
                    b = n - 6
                    dve.wait_ge(a_out_in_psum, n - 5)
                    nc.vector.tensor_tensor(x_sb[:, b, :], bank[:, 0, 0:D], x_sb[:, b, :],
                                            ALU.add).then_inc(x_ready, 1)
                if live(n, 4):
                    dve.wait_ge(a_pT_ready, 4 * (n - 3))
                    await_count(dve, a_spread_in_psum, n - 4)
                    nc.vector.tensor_tensor(
                        a_e3[:, :, :], a_pT[:, p0, :, T - 1].unsqueeze(1).to_broadcast([NK0, 3, H0]),
                        pick3.unsqueeze(2).to_broadcast([NK0, 3, H0]),
                        ALU.mult).then_inc(a_e3_ready, 1)
                if live(n, 3):
                    dve.wait_ge(a_s_in_psum, n - 2)
                    await_count(dve, a_pT_in_psum, 4 * (n - 4))
                    count.did(nc.vector.tensor_reduce(
                        a_max[:, :].rearrange("p (b h) -> p b h", b=4), s_bank, AX.X, ALU.max))
                    count.sync(dve)
                    nc.vector.tensor_tensor(
                        a_p[:, p1].rearrange("p (b h) k -> p b h k", b=4), s_bank,
                        a_max[:, :].rearrange("p (b h) -> p b h", b=4).unsqueeze(3)
                        .to_broadcast([128, 4, 4, NK0]), ALU.subtract).then_inc(a_s_shifted, 1)
                if live(n, 4):
                    dve.wait_ge(a_spread_in_psum, n - 3)
                    sums = bank[0:NK0, 0, D:D + 3 * H0].rearrange("p (a h) -> p a h", a=3)
                    count.did(nc.vector.tensor_scalar(a_lim[:, 0, :], sums[:, 1, :],
                                                      1.0 / (RECENT - 1), None, ALU.mult))
                    count.sync(dve)
                    count.did(nc.vector.scalar_tensor_tensor(
                        a_lim[:, 1, :], sums[:, 2, :], 1e-6, a_lim[:, 0, :], ALU.mult, ALU.add))
                    count.sync(dve)
                    count.did(nc.vector.tensor_tensor(a_lim[:, 2, :], a_lim[:, 1, :], bern[:, 2, :], ALU.mult))
                    count.sync(dve)
                    count.did(nc.vector.tensor_tensor(a_lim[:, 0, :], a_lim[:, 2, :], sums[:, 0, :],
                                                      ALU.is_lt))
                    count.sync(dve)
                    count.did(nc.vector.tensor_tensor(
                        a_add[:, :].rearrange("p (h c) -> p h c", h=H0),
                        bank[0:NK0, 0, 0:D].rearrange("p (h c) -> p h c", h=H0),
                        a_lim[:, 0, :].unsqueeze(2).to_broadcast([NK0, H0, HD0]), ALU.mult))
                if live(n, 1):
                    dve.wait_ge(a_qkv_in_psum, n)
                    await_count(dve, a_qkT_in_psum, n - 2)
                    heads = 2 * H0
                    raw = bank[:, 1, :].rearrange("p (h c) -> p h c", h=heads)
                    rot = a_rot[:, :].rearrange("p (h c) -> p h c", h=heads)
                    half = HD0 // 2
                    for c, s in ((0, half), (half, 0)):
                        count.did(nc.vector.tensor_tensor(
                            rot[:, :, c:c + half], raw[:, :, s:s + half],
                            rope_sin[:, c:c + half].unsqueeze(1).to_broadcast([128, heads, half]),
                            ALU.mult))
                    count.did(nc.vector.tensor_tensor(
                        a_cos[:, :].rearrange("p (h c) -> p h c", h=heads), raw,
                        rope_cos.unsqueeze(1).to_broadcast([128, heads, HD0]), ALU.mult))
                    count.sync(dve)
                    nc.vector.tensor_tensor(a_qk[:, p1, :], a_cos[:, :], a_rot[:, :],
                                            ALU.add).then_inc(a_qk_ready, 1)
                if live(n, 4):
                    count.sync(dve)
                    await_count(dve, a_o_in_psum, n - 4)
                    dve.wait_ge(pad_ready, 1)
                    for odd in range(2):
                        pick = [x.rearrange("p (j o c) -> p j o c", o=2, c=HD0)[:, :, odd, :]
                                for x in (a_add[:, :], a_v[:, u % VBUF, :])]
                        nc.vector.tensor_tensor(
                            a_vp[:, :, :].rearrange("p (j o) c -> p j o c", o=2)[
                                :, :, odd, HD0 * odd:HD0 * odd + HD0],
                            pick[0], pick[1], ALU.add).then_inc(a_vp_ready, 1)
                if live(n, 6):
                    dve.wait_ge(x_ready, n - 5)
                    stats(dve, count, n - 6)

            dve.wait_ge(const_ready, 3)
            for q in range(4):
                dve.wait_ge(x_loaded[q], 16)
                for b in range(4):
                    count.did(nc.vector.bn_stats(in_bn6[:, q, b, :], x_sb[:, 4 * q + b, :]))
                count.sync(dve)
                for b in range(4):
                    count.did(nc.vector.bn_aggr(in_moments[:, q, b, :], in_bn6[:, q, b, :]))
                count.sync(dve)
                nc.vector.tensor_tensor(moments[:, 4 * q:4 * q + 4, :], in_moments[:, q],
                                        zero_eps[:, :].unsqueeze(1).to_broadcast([128, 4, 2]),
                                        ALU.add).then_inc(stats_ready, 4)
            dve.wait_ge(w_loaded, 16 * 5)
            dve.wait_ge(const_loaded, 16)
            count.did(nc.vector.tensor_scalar(bern[:, 1, :], bern[:, 0, :], 1.0, 1e30, ALU.is_ge, ALU.mult))
            count.sync(dve)
            count.did(nc.vector.tensor_tensor(bern[:, 2, :], bern[:, 0, :], bern[:, 1, :], ALU.add))
            pipeline(dve, step, 8, 4, 6, count, 3 + 5 + 1 + 2,
                     between=lambda i: i < EARLY[0] and cross_vector(dve, 0, NB, NB, i))

        def attn_gpsimd(pool):
            for q in range(4):
                pool.wait_ge(stats_ready, 4 * q + 4)
                nc.gpsimd.tensor_tensor(rstd[:, 4 * q:4 * q + 4], moments[:, 4 * q:4 * q + 4, 1],
                                        minus_half[:, 0:1].to_broadcast([128, 4]),
                                        ALU.pow).then_inc(rstd_ready, 4)

        EARLY, EARLY_AFTER = (2, 1), (10, 12)

        def cross_phases(layer):
            return (0, 4, 0) if layer == 0 else (1, 3, NB)

        EVEN_AT, ODD_AT, INV_AT, RES_AT, STATS_AT, PARTS_AT = 7, 1, 1, 4, 7, (0, 2, 5)

        def cross_tensor(pe, layer, done, rdone, early=None):
            S = cross
            SPLIT, WEIGH, past = cross_phases(layer)
            rows = NSTACK + (3 if layer == 0 else 0)

            def weigh(n, u, odd):
                phase = WEIGH + odd
                pe.wait_ge(S["e_ready"], HX * (n + past - phase) + 4 + 4 * odd)
                for half in range(2):
                    for den in range(2):
                        for j in range(4):
                            w = half_ones[:, odd, :] if den else c_vT[:, (u - phase) % 2, half, 2 * j + odd, :]
                            mm = nc.tensor.matmul(
                                bank[32 * j:32 * j + 32, 5 + den, 0:D], w, c_e[:, j + 4 * odd, half, :],
                                start=(odd == 0 and half == 0), stop=(odd == 1 and half == 1))
                mm.then_inc(S["pv_done"], 1)

            def step(n, u, uses):
                c = n + past
                buf = (u - WEIGH) % NBUF
                if live(n, WEIGH):
                    pe.wait_ge(S["stack_in"][buf], 16 * STACK_DMAS * uses(WEIGH, NBUF))
                    if layer == 0:
                        pe.wait_ge(S["neg_in"][buf], 16 * uses(WEIGH, NBUF))
                for i in range(HX):
                    if live(n, WEIGH):
                        await_count(pe, S["e_ready"], HX * (c - WEIGH) + i - 1)
                        for half in range(2):
                            mm = nc.tensor.matmul(
                                bank[:, 2 + i % 2, half * D:half * D + D],
                                k_stack[0:rows, buf, ORDER[i], half * 128:half * 128 + 128],
                                q_stack[0:rows, buf, ORDER[i], :], start=True, stop=True)
                        mm.then_inc(S["sT_in_psum"], 1)
                    if layer == 0 and live(n, 2):
                        if i == 0:
                            pe.wait_ge(S["stack_in"][(u - 2) % NBUF], 16 * STACK_DMAS * uses(2, NBUF))
                        await_count(pe, S["max_ready"], HX * (n - 2) + i - 1)
                        for half in range(2):
                            mm = nc.tensor.matmul(
                                bank[:, i % 2, half * D:half * D + D],
                                q_stack[0:NSTACK, (u - 2) % NBUF, i, half * 128:half * 128 + 128],
                                k_stack[0:NSTACK, (u - 2) % NBUF, i, :], start=True, stop=True)
                        mm.then_inc(S["s_in_psum"], 1)
                    if layer == 1 and i == 3 and live(n, 0):
                        pe.wait_ge(S["sq_ready"], n + 1)
                        await_count(pe, S["ss_ready"], n)
                        nc.tensor.matmul(bank[:, 7, :], table("group_ones"), c_sq[:, :],
                                         start=True, stop=True).then_inc(S["ss_in_psum"], 1)
                    if i == ODD_AT and live(n, WEIGH + 1):
                        weigh(n, u, 1)
                    if i == EVEN_AT and live(n, WEIGH):
                        pe.wait_ge(S["vT_ready"], 2 * (c - WEIGH + 1))
                        await_count(pe, x_ready, done + n - WEIGH)
                        weigh(n, u, 0)
                if layer == 0 and live(n, 2):
                    pe.wait_ge(S["max_ready"], HX * (n - 1))
                    await_count(pe, S["neg_ready"], n - 2)
                    nc.tensor.transpose(bank[0:2 * HX, 4, 0:128],
                                        c_max[:, u % 2].rearrange("p h a -> p (h a)"),
                                        ident).then_inc(S["maxT_in_psum"], 1)

            if early is not None:
                step(early, early, buffer_uses(early, past))
                return
            pe.wait_ge(x_ready, done)
            pe.wait_ge(pad_ready, 3)
            pipeline(pe, step, 8, 4, WEIGH + 1, past=past, begun=EARLY[layer])

        def cross_scalar(act, layer, done, rdone, early=None):
            S = cross
            SPLIT, WEIGH, past = cross_phases(layer)
            count = act_chain
            scale = DX ** -0.5 if layer == 0 else 5.0
            src = c_raw if layer == 0 else c_unit
            per_step = 1 if layer == 0 else 2

            def part(n, u, uses, k):
                c, ps = n + past, (u - SPLIT) % 2
                if k:
                    act.wait_ge(S["rest1" if k == 1 else "rest2"], c - SPLIT + 1)
                elif layer == 0:
                    act.wait_ge(S["h_ready"], c + 1)
                    act.wait_ge(S["ctx_in"][ps], 16 * uses(0, 2))
                else:
                    act.wait_ge(S["unit_ready"], n)
                if k == 0:
                    await_count(act, S["part_stored"], 16 * PART_DMAS * (c - SPLIT - 1))
                nc.scalar.copy(c_part[:, ps, k, :], (src if k == 0 else c_rest)[:, ps, :]
                               ).then_inc(S[("hi", "mid", "lo")[k]], 1)

            def step(n, u, uses):
                c = n + past
                if layer == 1 and live(n, SPLIT):
                    act.wait_ge(S["ss_ready"], n)
                    count.did(nc.scalar.activation(c_ss[:, :], c_ss[:, :], ACT.Ln))
                    count.sync(act)
                    nc.scalar.activation(c_ss[:, :], c_ss[:, :], ACT.Exp,
                                         scale=-0.5).then_inc(S["inv_norm"], 1)
                for i in range(HX):
                    if live(n, WEIGH):
                        act.wait_ge(S["sT_in_psum"], HX * (c - WEIGH) + i + 1)
                        await_count(act, S["pv_done"], 2 * (c - WEIGH - 1) + 1 + i // 4)
                        nc.scalar.activation(c_e[:, i].rearrange("p a m -> p (a m)"), bank[:, 2 + i % 2, :],
                                             ACT.Exp, scale=scale).then_inc(S["e_ready"], 1)
                    if i == INV_AT and live(n, WEIGH + 1):
                        act.wait_ge(S["pv_done"], 2 * (c - WEIGH))
                        await_count(act, x_ready, done + n - WEIGH - 1)
                        count.did(nc.scalar.activation(c_inv[:, :], bank[:, 6, 0:D], ACT.Ln))
                        count.sync(act)
                        nc.scalar.activation(c_inv[:, :], c_inv[:, :], ACT.Exp,
                                             scale=-1.0).then_inc(S["inv_ready"], 1)
                    if i in PARTS_AT and live(n, SPLIT):
                        part(n, u, uses, PARTS_AT.index(i))

            if early is not None:
                for n, k in early:
                    part(n, n, buffer_uses(n), k)
                return
            nc.scalar.preload_act_table_set("natural_log_exp_and_others")
            pipeline(act, step, 8, 4, WEIGH + 1, count, per_step, past=past, begun=0 if layer else EARLY[0])

        def cross_vector(dve, layer, done, rdone, early=None):
            S = cross
            SPLIT, WEIGH, past = cross_phases(layer)
            count = dve_chain

            def step(n, u, uses):
                c = n + past
                p0, p1 = u % 2, (u - 1) % 2
                if layer == 1 and live(n, 1):
                    dve.wait_ge(S["inv_norm"], n)
                    await_count(dve, S["rest1"], NB + n - 2)
                    nc.vector.tensor_tensor(c_unit[:, p1, :], c_raw[:, p1, :], c_ss[:, :],
                                            ALU.mult).then_inc(S["unit_ready"], 1)
                if live(n, 0):
                    dve.wait_ge(rstd_ready, rdone + n + 1)
                    if layer == 0:
                        await_count(dve, S["rest1"], n - 1)
                    else:
                        await_count(dve, S["unit_ready"], n - 1)
                    nc.vector.tensor_scalar(
                        c_raw[:, p0, 0:D], x_sb[:, n, :], moments[:, n, 0:1],
                        rstd[:, bass.ds(n, 1)], ALU.subtract, ALU.mult).then_inc(S["h_ready"], 1)
                if layer == 0 and live(n, 3):
                    dve.wait_ge(S["maxT_in_psum"], n - 2)
                    await_count(dve, S["neg_stored"], 16 * (n - 3))
                    maxT = bank[0:2 * HX, 4, 0:128]
                    count.did(nc.vector.tensor_scalar(c_neg[:, 0, :], maxT, -1.0, None, ALU.mult))
                    count.sync(dve)
                    count.did(nc.vector.scalar_tensor_tensor(c_nrest[:, 0, :], maxT, -1.0, c_neg[:, 0, :],
                                                             ALU.mult, ALU.subtract))
                    count.sync(dve)
                    count.did(nc.vector.tensor_copy(c_neg[:, 1, :], c_nrest[:, 0, :]))
                    count.sync(dve)
                    nc.vector.tensor_tensor(c_neg[:, 2, :], c_nrest[:, 0, :], c_neg[:, 1, :],
                                            ALU.subtract).then_inc(S["neg_ready"], 1)
                for i in range(HX):
                    if layer == 0 and live(n, 2):
                        dve.wait_ge(S["s_in_psum"], HX * (n - 2) + i + 1)
                        if i == 0:
                            await_count(dve, S["maxT_in_psum"], n - 3)
                        nc.vector.tensor_reduce(
                            c_max[:, p0, i, :], bank[:, i % 2, :].rearrange("p (a m) -> p a m", a=2),
                            AX.X, ALU.max).then_inc(S["max_ready"], 1)
                    if i == RES_AT and live(n, WEIGH + 1):
                        b = n - WEIGH - 1
                        dve.wait_ge(S["inv_ready"], c - WEIGH)
                        count.did(nc.vector.tensor_tensor(c_att[:, :], bank[:, 5, 0:D], c_inv[:, :], ALU.mult))
                        count.sync(dve)
                        nc.vector.tensor_tensor(x_sb[:, b, :], c_att[:, :], x_sb[:, b, :],
                                                ALU.add).then_inc(x_ready, 1)
                    if i == STATS_AT and live(n, WEIGH + 1):
                        dve.wait_ge(x_ready, done + n - WEIGH)
                        stats(dve, count, n - WEIGH - 1)
                if layer == 1 and live(n, 0):
                    dve.wait_ge(S["ss_in_psum"], n + 1)
                    await_count(dve, S["unit_ready"], n)
                    nc.vector.tensor_scalar(c_ss[:, :], bank[:, 7, :], 1e-24, None,
                                            ALU.max).then_inc(S["ss_ready"], 1)

            if early is not None:
                step(early, early, buffer_uses(early, past))
                return
            pipeline(dve, step, 8, 4, WEIGH + 1, count, 3 + (3 if layer == 0 else 0), past=past,
                     begun=EARLY[layer])

        def cross_gpsimd(pool, layer, done, rdone, early=None):
            S = cross
            SPLIT, WEIGH, past = cross_phases(layer)
            src = c_raw if layer == 0 else c_unit

            def step(n, u, uses):
                c = n + past
                p0, ps, pv = u % 2, (u - SPLIT) % 2, (u - WEIGH + 1) % 2
                if layer == 1 and live(n, 0):
                    pool.wait_ge(S["h_ready"], c + 1)
                    pool.wait_ge(S["ctx_in"][p0], 16 * uses(0, 2))
                    await_count(pool, S["ss_in_psum"], n)
                    nc.gpsimd.tensor_tensor(c_sq[:, :], c_raw[:, p0, :], c_raw[:, p0, :],
                                            ALU.mult).then_inc(S["sq_ready"], 1)
                if live(n, SPLIT):
                    pool.wait_ge(S["hi"], c - SPLIT + 1)
                    await_count(pool, S["lo"], c - SPLIT - 1)
                    nc.gpsimd.tensor_tensor(c_rest[:, ps, :], src[:, ps, :], c_part[:, ps, 0, :],
                                            ALU.subtract).then_inc(S["rest1"], 1)
                if live(n, SPLIT):
                    pool.wait_ge(S["mid"], c - SPLIT + 1)
                    nc.gpsimd.tensor_tensor(c_rest[:, ps, :], c_rest[:, ps, :], c_part[:, ps, 1, :],
                                            ALU.subtract).then_inc(S["rest2"], 1)
                if live(n, WEIGH - 1):
                    pool.wait_ge(S["vT_in"][pv], 16 * uses(WEIGH - 1, 2))
                    await_count(pool, S["pv_done"], 2 * (c - WEIGH))
                    hold(pool)
                    for odd in range(2):
                        pick = c_vT_in[:, pv].rearrange("p a (j o c) -> p a j o c", o=2, c=DX)
                        nc.gpsimd.tensor_copy(
                            c_vT[:, pv].rearrange("p a (j o) c -> p a j o c", o=2)[
                                :, :, :, odd, DX * odd:DX * odd + DX],
                            pick[:, :, :, odd, :]).then_inc(S["vT_ready"], 1)
                if live(n, WEIGH + 1):
                    pool_rstd(pool, n - WEIGH - 1, rdone + NB)
                if layer == 0 and isinstance(n, int):
                    load_mlp_inputs(pool, n - EARLY[0])

            if early is not None:
                step(early, early, buffer_uses(early, past))
                return
            pipeline(pool, step, 8, 4, WEIGH + 1, past=past, begun=EARLY[layer])

        def cross_sync(sp, layer, done, rdone):
            S = cross
            SPLIT, WEIGH, past = cross_phases(layer)
            LOAD = SPLIT + 1

            def step(n, u, uses):
                c = n + past
                p0, ps, pl, pv, p1 = (u - x & 1 for x in (0, SPLIT, LOAD, WEIGH - 1, 1))
                if live(n, 0):
                    if layer == 0:
                        await_count(sp, S["rest1"], n - 1)
                    else:
                        await_count(sp, S["unit_ready"], n - 1)
                    sp.dma_start(c_raw[:, p0, D:2 * D],
                                 A["context"][bass.ds(n, 1)].rearrange("b t d -> (b t) d")
                                 ).then_inc(S["ctx_in"][p0], 16)
                if live(n, WEIGH - 1):
                    await_count(sp, S["vT_ready"], 2 * (c - WEIGH))
                    sp.dma_start(c_vT_in[:, pv],
                                 A["contextT"][bass.ds(n - WEIGH + 1, 1)].rearrange(
                                     "b (a p) t -> p (b a) t", p=128)).then_inc(S["vT_in"][pv], 16)
                if layer == 0 and live(n, 3):
                    sp.wait_ge(S["neg_ready"], n - 2)
                    hold(sp)
                    if live(n, 5):
                        sp.wait_ge(S["neg_in"][(u - 5) % NBUF], 16 * uses(5, NBUF))
                    sp.dma_start(neg_dram[p1], c_neg[:, :, :]).then_inc(S["neg_stored"], 16)
                if live(n, LOAD):
                    sp.wait_ge(S["part_stored"], 16 * PART_DMAS * (c - LOAD + 1))
                    hold(sp)
                    await_count(sp, S["sT_in_psum"], HX * (c - LOAD - 3))
                    hold(sp)
                    for a, (stack, parts) in enumerate(((q_stack, QPART), (k_stack, KPART))):
                        for r0, r1 in ((0, 3), (3, 5), (5, 6)):
                            rows = part_dram[pl, a, parts[r0] * DX:(parts[r1 - 1] + 1) * DX]
                            if parts[r0] == parts[r1 - 1]:
                                rows = rows.rearrange("d h m -> d (h m)").unsqueeze(0).to_broadcast(
                                    [r1 - r0, DX, HX * D])
                            else:
                                rows = rows.rearrange("d h m -> d (h m)")
                            sp.dma_start(stack[DX * r0:DX * r1, (u - LOAD) % NBUF, :, :].rearrange(
                                "p h m -> p (h m)"), rows).then_inc(S["stack_in"][(u - LOAD) % NBUF], 16)
                for k, part_ready in enumerate(("hi", "mid", "lo")):
                    if live(n, SPLIT):
                        sp.wait_ge(S[part_ready], c - SPLIT + 1)
                        hold(sp)
                        if k == 0 and live(n, SPLIT + 2):
                            sp.wait_ge(S["stack_in"][(u - SPLIT - 2) % NBUF],
                                       16 * STACK_DMAS * uses(SPLIT + 2, NBUF))
                        for a in range(2):
                            for_heads = part_dram[ps, a, k * DX:(k + 1) * DX].rearrange("d h m -> h d m")
                            sp.dma_start(for_heads, c_part[:, ps, k, a * D:a * D + D]
                                         ).then_inc(S["part_stored"], 16)
                    if k == 0 and layer == 0 and live(n, 3):
                        sp.wait_ge(S["neg_stored"], 16 * (n - 2))
                        sp.dma_start(
                            q_stack[NSTACK:NSTACK + 3, (u - 3) % NBUF, :, :].rearrange(
                                "c h (a m) -> c (h a) m", a=2),
                            neg_dram[p1].rearrange("a c m -> c a m")).then_inc(S["neg_in"][(u - 3) % NBUF], 16)

            pipeline(sp, step, 8, 4, WEIGH - 1, past=past)

        def shared_tensor(pe, done):
            def step(n, u, uses):
                if live(n, 1):
                    pe.wait_ge(m_hT_ready, n)
                    await_count(pe, m_hid_ready, n - 2)
                    for t in range(KT):
                        mm = nc.tensor.matmul(bank[:, SGU[(u - 1) % 2], :], m_hT[:, (u - 1) % 2, t, :],
                                              m_wgu[:, t, :], start=(t == 0), stop=(t == KT - 1))
                    mm.then_inc(m_gu_in_psum, 1)
                if live(n, 0):
                    pe.wait_ge(m_h_ready, n + 1)
                    await_count(pe, m_hT_ready, n)
                    for t in range(KT):
                        mm = nc.tensor.transpose(bank[:, 0, t * T:(t + 1) * T],
                                                 m_hc[:, u % 2, t * 128:(t + 1) * 128], ident)
                    mm.then_inc(m_hT_in_psum, 1)
                if live(n, 2):
                    pe.wait_ge(m_hid_ready, n - 1)
                    await_count(pe, m_hidT_ready, n - 2)
                    for t in range(KT):
                        mm = nc.tensor.transpose(bank[:, 3, t * T:(t + 1) * T],
                                                 m_hid[:, u % 2, t * 128:(t + 1) * 128], ident)
                    mm.then_inc(m_hidT_in_psum, 1)
                if live(n, 0):
                    pe.wait_ge(m_hT_ready, n + 1)
                    await_count(pe, m_s_ready, n)
                    for t in range(KT):
                        mm = nc.tensor.matmul(bank[:, 1, 0:EX0], m_hT[:, u % 2, t, :],
                                              m_wr[:, t, :], start=(t == 0), stop=(t == KT - 1))
                    mm.then_inc(m_logit_in_psum, 1)
                if live(n, 2):
                    pe.wait_ge(m_hidT_ready, n - 1)
                    await_count(pe, x_ready, done + n - 2)
                    for t in range(KT):
                        mm = nc.tensor.matmul(bank[:, 4, 0:D], m_hidT[:, t, :], m_wdn[:, t, :],
                                              start=(t == 0), stop=(t == KT - 1))
                    mm.then_inc(m_out_in_psum, 1)
                if live(n, RG) and u % RG == 2:
                    pe.wait_ge(m_hot_ready, uses(RG, RG))
                    await_count(pe, m_slot_ready, uses(RG, RG) - 1)
                    rank = bank[:, 5, 0:RG * EX0].rearrange("p (b e) -> p b e", e=EX0)
                    nc.tensor.matmul(rank, table("before"), r_chosen[:, :, :], start=True, stop=False)
                    for b in range(RG - 1):
                        nc.tensor.matmul(rank[:, b + 1:RG, :], ones,
                                         r_chosen[:, b:b + 1, :].to_broadcast([128, RG - 1 - b, EX0]),
                                         start=False, stop=False)
                    nc.tensor.matmul(rank, ones, r_seen[:, :].unsqueeze(1).to_broadcast([128, RG, EX0]),
                                     start=False, stop=True).then_inc(m_rank_in_psum, 1)

            pe.wait_ge(x_ready, done)
            pe.wait_ge(m_w_loaded, 16 * 4)
            pipeline(pe, step, RG, RG, RG)

        def shared_scalar(act, done):
            def step(n, u, uses):
                if live(n, 1):
                    act.wait_ge(m_gu_in_psum, n)
                    await_count(act, m_hid_ready, n - 2)
                    nc.scalar.activation(m_sig[:, (u - 1) % 2, :], bank[:, SGU[(u - 1) % 2], 0:SH0],
                                         ACT.Sigmoid).then_inc(m_sig_ready, 1)
                if live(n, 0):
                    act.wait_ge(m_hT_in_psum, n + 1)
                    await_count(act, m_gu_in_psum, n - 1)
                    await_count(act, m_logit_in_psum, n - 1)
                    nc.scalar.copy(m_hT[:, u % 2].rearrange("p t c -> p (t c)"),
                                   bank[:, 0, 0:D]).then_inc(m_hT_ready, 1)
                if live(n, 2):
                    act.wait_ge(m_hidT_in_psum, n - 1)
                    await_count(act, m_out_in_psum, n - 2)
                    nc.scalar.copy(m_hidT[:, :, :].rearrange("p t c -> p (t c)"),
                                   bank[:, 3, 0:D]).then_inc(m_hidT_ready, 1)
                if live(n, 0):
                    act.wait_ge(m_logit_in_psum, n + 1)
                    await_count(act, r_taken, uses(RG, RG))
                    nc.scalar.activation(r_score[:, u % RG, :], bank[:, 1, 0:EX0],
                                         ACT.Sigmoid).then_inc(m_s_ready, 1)

            act.wait_ge(x_ready, done)
            nc.scalar.preload_act_table(ACT.Sigmoid)
            pipeline(act, step, RG, RG, 2)

        def shared_vector(dve, done):
            count = dve_chain
            tt, ts = nc.vector.tensor_tensor, nc.vector.tensor_scalar
            iota = table("iota32")
            g = [x[:, :, :] for x in r_g]
            of = r_sc[:, :, :].rearrange("p b (g c) -> p b g c", c=EX0 // GROUPS)

            def seq(ins):
                count.did(ins)
                count.sync(dve)

            def top8():
                src = lambda b: g[4][:, b, :] if not experts else r_sc[:, b, :]
                for b in range(RG):
                    count.did(nc.vector.max(r_top[:, b, :], src(b)))
                count.sync(dve)
                for b in range(RG):
                    if b == 0:
                        hold(dve)
                    count.did(nc.vector.max_index(r_topi[:, b, :], r_top[:, b, :], src(b)))
                count.sync(dve)
                seq(nc.vector.tensor_copy(r_pick[:, :, :], r_topi[:, :, 0:TOP0]))

            experts = False

            def groups_chosen(n, uses):
                dve.wait_ge(m_s_ready, n)
                count.did(tt(r_sc[:, :, :], r_score[:, :, :],
                             m_bias[:, :].unsqueeze(1).to_broadcast([128, RG, EX0]), ALU.add))
                nc.vector.tensor_copy(r_own[:, :, :], r_score[:, :, :]).then_inc(r_taken, 1)
                count.sync(dve)
                a, b_, c, d = (of[:, :, :, i] for i in range(4))
                for o, i0, i1, op in ((g[0], a, b_, ALU.max), (g[1], a, b_, ALU.min), (g[2], c, d, ALU.max),
                                      (g[3], c, d, ALU.min)):
                    count.did(tt(o, i0, i1, op))
                count.sync(dve)
                count.did(tt(g[4], g[0], g[2], ALU.max))
                count.did(tt(g[5], g[0], g[2], ALU.min))
                seq(tt(g[1], g[1], g[3], ALU.max))
                seq(tt(g[5], g[5], g[1], ALU.max))
                seq(tt(g[4], g[4], g[5], ALU.add))
                hold(dve)
                top8()

            def experts_chosen():
                for k in range(TOPG):
                    count.did(tt(r_hot[:, :, k, 0:GROUPS],
                                 iota[:, 0:GROUPS].unsqueeze(1).to_broadcast([128, RG, GROUPS]),
                                 r_pick[:, :, k:k + 1].to_broadcast([128, RG, GROUPS]), ALU.is_equal))
                count.sync(dve)
                seq(nc.vector.tensor_reduce(g[0], r_hot[:, :, 0:TOPG, 0:GROUPS].rearrange(
                    "p b k g -> p b g k"), AX.X, ALU.add))
                seq(tt(of, of, g[0].unsqueeze(3).to_broadcast([128, RG, GROUPS, EX0 // GROUPS]), ALU.mult))
                seq(ts(r_sc[:, :, :], r_sc[:, :, :], 0.0, None, ALU.add))
                hold(dve)
                top8()

            def weights(n, uses):
                for k in range(TOP0):
                    count.did(tt(r_hot[:, :, k, :], iota.unsqueeze(1).to_broadcast([128, RG, EX0]),
                                 r_pick[:, :, k:k + 1].to_broadcast([128, RG, EX0]), ALU.is_equal))
                count.sync(dve)
                nc.vector.tensor_reduce(r_chosen[:, :, :], r_hot[:, :, :, :].rearrange("p b k e -> p b e k"),
                                        AX.X, ALU.add).then_inc(m_hot_ready, 1)
                seq(tt(r_t[:, :, :, :], r_hot[:, :, :, :],
                       r_own[:, :, :].unsqueeze(2).to_broadcast([128, RG, TOP0, EX0]), ALU.mult))
                seq(nc.vector.tensor_reduce(r_w[:, :, :], r_t[:, :, :, :], AX.X, ALU.add))
                seq(nc.vector.tensor_reduce(r_sum[:, :], r_w[:, :, :], AX.X, ALU.add))
                seq(ts(r_sum[:, :], r_sum[:, :], 1e-20, None, ALU.add))
                seq(nc.vector.reciprocal(r_sum[:, :], r_sum[:, :]))
                seq(ts(r_sum[:, :], r_sum[:, :], 2.5, None, ALU.mult))
                count.did(tt(m_w[:, bass.ds(n - RG - 2, RG), :], r_w[:, :, :],
                             r_sum[:, :].unsqueeze(2).to_broadcast([128, RG, TOP0]), ALU.mult))

            def slots(n, uses):
                dve.wait_ge(m_rank_in_psum, uses(RG, RG))
                rank_of = bank[:, 5, 0:RG * EX0].rearrange("p (b e) -> p b e", e=EX0)
                rank, slot, over = (x[:, :, :] for x in r_k)
                seq(tt(r_t[:, :, :, :], r_hot[:, :, :, :],
                       rank_of.unsqueeze(2).to_broadcast([128, RG, TOP0, EX0]), ALU.mult))
                seq(nc.vector.tensor_reduce(rank, r_t[:, :, :, :], AX.X, ALU.add))
                count.did(ts(over, rank, float(CAP), DROPPED, ALU.is_ge, ALU.mult))
                seq(nc.vector.scalar_tensor_tensor(slot.rearrange("p b k -> p (b k)"),
                                                   r_pick[:, :, :].rearrange("p b k -> p (b k)"), float(CAP),
                                                   rank.rearrange("p b k -> p (b k)"), ALU.mult, ALU.add))
                seq(tt(slot, slot, over, ALU.add))
                ts(m_slot[:, bass.ds(n - RG - 3, RG), :], slot, float(SLOTS), None,
                   ALU.min).then_inc(m_slot_ready, 1)
                seq(nc.vector.tensor_reduce(r_all[:, :], r_chosen[:, :, :].rearrange("p b e -> p e b"), AX.X,
                                            ALU.add))
                seq(tt(r_seen[:, :], r_seen[:, :], r_all[:, :], ALU.add))

            def step(n, u, uses):
                nonlocal experts
                if live(n, 0):
                    dve.wait_ge(rstd_ready, done + n + 1)
                    await_count(dve, m_hT_in_psum, n - 1)
                    await_count(dve, m_h_ready, n - 1)
                    nc.vector.tensor_scalar(
                        m_hc[:, u % 2, :], x_sb[:, n, :], moments[:, n, 0:1],
                        rstd[:, bass.ds(n, 1)], ALU.subtract, ALU.mult).then_inc(m_h_ready, 1)
                if live(n, 3):
                    dve.wait_ge(m_out_in_psum, n - 2)
                    nc.vector.tensor_tensor(x_sb[:, n - 3, :], bank[:, 4, 0:D], x_sb[:, n - 3, :],
                                            ALU.add).then_inc(x_ready, 1)
                if live(n, 0):
                    dve.wait_ge(m_h_ready, n + 1)
                    nc.vector.tensor_copy(h_all[:, n, :], m_hc[:, u % 2, :]).then_inc(m_hall_ready, 1)
                if live(n, RG):
                    experts = u % RG == 1
                    if u % RG == 0:
                        groups_chosen(n, uses)
                    elif u % RG == 1:
                        experts_chosen()
                    elif u % RG == 2:
                        weights(n, uses)
                    else:
                        slots(n, uses)
                if live(n, 1):
                    p1 = (u - 1) % 2
                    dve.wait_ge(m_sig_ready, n)
                    await_count(dve, m_hidT_in_psum, n - 2)
                    seq(tt(m_sig[:, p1, :], bank[:, SGU[p1], 0:SH0], m_sig[:, p1, :], ALU.mult))
                    tt(m_hid[:, p1, :], bank[:, SGU[p1], SH0:2 * SH0], m_sig[:, p1, :],
                       ALU.mult).then_inc(m_hid_ready, 1)

            dve.wait_ge(m_w_loaded, 16 * 4)
            seq(nc.vector.memset(r_seen[:, :], 0.0))
            per_turn = RG + (11 + 2 * RG) + (TOPG + 4 + 2 * RG) + (TOP0 + 7) + 7
            pipeline(dve, step, RG, RG, RG, count, per_turn=per_turn)

        def dispatch_gpsimd(pool):
            pool.wait_ge(slots_zero, 16 * 6)
            for b in range(NB):
                if b % RG == 0:
                    pool.wait_ge(m_slot_ready, b // RG + 1)
                    pool.wait_ge(m_hall_ready, b + RG)
                for k in range(TOP0):
                    pool.indirect_dma_start(
                        out=xp_dram, out_offset=bass.IndirectOffsetOnAxis(ap=m_slot[:, b, k:k + 1], axis=0),
                        in_=h_all[:, b, :], in_offset=None, bounds_check=SLOTS - 1,
                        oob_is_err=False).then_inc(rows_sent, 16)

        def expert_tensor(pe):
            def step(n, u, uses):
                if live(n, 0, EX0):
                    pe.wait_ge(d_x_in[u % XBUF], 16 * uses(0, XBUF))
                    await_count(pe, d_xT_ready, n)
                    for t in range(KT):
                        mm = nc.tensor.transpose(bank[:, 0, t * CAP:(t + 1) * CAP],
                                                 d_x[:, u % XBUF, t * 128:(t + 1) * 128],
                                                 ident[0:CAP, 0:CAP])
                    mm.then_inc(d_xT_in_psum, 1)
                if live(n, 1, EX0):
                    pe.wait_ge(d_xT_ready, n)
                    pe.wait_ge(ring_in[(u - 1) % RING], 32 * uses(1, RING))
                    await_count(pe, d_hid_ready, n - 2)
                    for t in range(KT):
                        mm = nc.tensor.matmul(bank[0:CAP, GU[(u - 1) % 2], 0:2 * I0], d_xT[:, (u - 1) % 2, t, :],
                                              wgu[:, (u - 1) % RING, t, :], start=(t == 0),
                                              stop=(t == KT - 1))
                    mm.then_inc(d_gu_in_psum, 1)
                if live(n, 2, EX0):
                    pe.wait_ge(d_hid_ready, n - 1)
                    await_count(pe, d_hidT_ready, n - 2)
                    nc.tensor.transpose(bank[:, 2, 0:CAP], d_hid[:, u % 2, :],
                                        ident[0:CAP, 0:CAP]).then_inc(d_hidT_in_psum, 1)
                if live(n, 3, EX0):
                    pe.wait_ge(d_hidT_ready, n - 2)
                    await_count(pe, d_y_ready, n - 3)
                    nc.tensor.matmul(bank[0:CAP, 3, 0:D], d_hidT[:, (u - 3) % 2, :], wdn[:, (u - 3) % RING, :],
                                     start=True, stop=True).then_inc(d_y_in_psum, 1)

            pe.wait_ge(x_ready, 3 * NB)
            pipeline(pe, step, RING, RING, 3, total=EX0)

        def expert_scalar(act):
            def step(n, u, uses):
                if live(n, 0, EX0):
                    act.wait_ge(d_xT_in_psum, n + 1)
                    await_count(act, d_gu_in_psum, n - 1)
                    nc.scalar.copy(d_xT[:, u % 2].rearrange("p t c -> p (t c)"),
                                   bank[:, 0, 0:KT * CAP]).then_inc(d_xT_ready, 1)
                if live(n, 2, EX0):
                    act.wait_ge(d_hidT_in_psum, n - 1)
                    await_count(act, d_y_in_psum, n - 3)
                    nc.scalar.copy(d_hidT[:, u % 2, :], bank[:, 2, 0:CAP]).then_inc(d_hidT_ready, 1)
                if live(n, 1, EX0):
                    act.wait_ge(d_gu_in_psum, n)
                    await_count(act, d_hid_ready, n - 1)
                    nc.scalar.activation(d_sig[:, :], bank[0:CAP, GU[(u - 1) % 2], 0:I0],
                                         ACT.Sigmoid).then_inc(d_sig_ready, 1)

            pipeline(act, step, RING, RING, 2, total=EX0)

        def expert_vector(dve):
            count = dve_chain

            def step(n, u, uses):
                if live(n, 1, EX0):
                    p1 = (u - 1) % 2
                    dve.wait_ge(d_sig_ready, n)
                    await_count(dve, d_hidT_in_psum, n - 2)
                    count.did(nc.vector.tensor_tensor(d_hid[:, p1, :], bank[0:CAP, GU[p1], 0:I0], d_sig[:, :],
                                                      ALU.mult))
                    count.sync(dve)
                    nc.vector.tensor_tensor(d_hid[:, p1, :], bank[0:CAP, GU[p1], I0:2 * I0], d_hid[:, p1, :],
                                            ALU.mult).then_inc(d_hid_ready, 1)
                if live(n, 3, EX0):
                    dve.wait_ge(d_y_in_psum, n - 2)
                    if live(n, 5, EX0):
                        dve.wait_ge(y_stored[(u - 5) % 2], 16 * uses(5, 2))
                    nc.vector.tensor_copy(d_y[:, (u - 3) % 2, :], bank[0:CAP, 3, 0:D]).then_inc(d_y_ready, 1)

            pipeline(dve, step, RING, RING, 3, count, 1, total=EX0)

        def expert_sync(sp):
            def step(n, u, uses):
                if live(n, 0, EX0):
                    await_count(sp, d_xT_in_psum, n - XBUF + 1)
                    sp.dma_start(d_x[:, u % XBUF, :],
                                 xp_dram[bass.ds(n * CAP, CAP), :]).then_inc(d_x_in[u % XBUF], 16)
                if live(n, STORE, EX0):
                    sp.wait_ge(d_y_ready, n - STORE + 1)
                    sp.dma_start(y_dram[bass.ds((n - STORE) * CAP, CAP), :],
                                 d_y[:, (u - STORE) % 2, :]).then_inc(y_stored[(u - STORE) % 2], 16)
                    if not isinstance(n, int) or n - STORE + RING < EX0:
                        load_expert(sp, n - STORE + RING, u - STORE)

            sp.wait_ge(rows_sent, 16 * NB * TOP0)
            pipeline(sp, step, RING, RING, RING + STORE, total=EX0 - RING)

        def load_expert(sp, e, u):
            sp.dma_start(wgu[:, u % RING, :, :],
                         A["W_gu"][bass.ds(e, 1)].rearrange("e (t p) i -> p (e t) i", p=128)
                         ).then_inc(ring_in[u % RING], 16)
            sp.dma_start(wdn[:, u % RING, :],
                         A["W_down"][bass.ds(e, 1)].rearrange("e p o -> p (e o)")).then_inc(ring_in[u % RING], 16)

        SHIFTED, KV = (1, 5), (3, 6)

        def shift_tensor(pe, done):
            def step(n, u, uses):
                p1 = (u - 1) % 2
                if live(n, 5):
                    pe.wait_ge(f_state_ready, n - 4)
                    await_count(pe, x_ready, done + n - 5)
                    nc.tensor.matmul(bank[:, 4, 0:D], f_state[:, p1, :], f_wo[:, :],
                                     start=True, stop=True).then_inc(f_out_in_psum, 1)
                if live(n, 3):
                    pe.wait_ge(f_z_ready, n - 2)
                    await_count(pe, f_zT_ready, n - 3)
                    for t in range(KT):
                        mm = nc.tensor.transpose(bank[:, 2, t * T:(t + 1) * T],
                                                 f_z[:, t * 128:(t + 1) * 128], ident)
                    mm.then_inc(f_zT_in_psum, 1)
                if live(n, 1):
                    pe.wait_ge(f_h_ready, n)
                    await_count(pe, f_hT_ready, 2 * (n - 1))
                    for t in range(KT):
                        mm = nc.tensor.transpose(bank[:, 0, t * T:(t + 1) * T],
                                                 f_h[:, p1, t * 128:(t + 1) * 128], ident)
                    mm.then_inc(f_hT_in_psum, 1)
                if live(n, 3):
                    pe.wait_ge(f_zT_ready, n - 2)
                    await_count(pe, f_wkvx_ready, n - 4)
                    for kv in range(2):
                        for t in range(KT):
                            mm = nc.tensor.matmul(bank[0:NS, KV[p1], kv * T:(kv + 1) * T],
                                                  f_wkv[:, 1, t, kv * NS:(kv + 1) * NS], f_zT[:, t, :],
                                                  start=(t == 0), stop=(t == KT - 1))
                    mm.then_inc(f_kv_in_psum, 1)
                if live(n, 1):
                    pe.wait_ge(f_hT_ready, 2 * n)
                    await_count(pe, f_xs_ready, n - 2)
                    for t in range(KT):
                        mm = nc.tensor.matmul(bank[:, SHIFTED[p1], 0:D], f_hT[:, p1, t, :], f_wshift[:, t, :],
                                              start=(t == 0), stop=(t == KT - 1))
                    mm.then_inc(f_shift_in_psum, 1)

            pe.wait_ge(x_ready, done)
            pe.wait_ge(d_y_ready, EX0)
            pe.wait_ge(f_loaded, 16 * 8)
            for kv in range(2):
                for t in range(KT):
                    mm = nc.tensor.matmul(bank[0:NS, 3, kv:kv + 1], f_wkv[:, 0, t, kv * NS:(kv + 1) * NS],
                                          f_affine[:, 1, t:t + 1], start=(t == 0), stop=(t == KT - 1))
            mm.then_inc(f_pe, 1)
            pe.wait_ge(f_setup, 1)
            pipeline(pe, step, 8, 4, 5, between=lambda i: i == 0 and cross_tensor(pe, 1, 4 * NB, 3 * NB, 0))

        def shift_scalar(act, done):
            count = act_chain

            def step(n, u, uses):
                p0, p1 = u % 2, (u - 1) % 2
                if live(n, 4):
                    act.wait_ge(f_kv_in_psum, n - 3)
                    await_count(act, f_wkvx_ready, n - 5)
                    e = f_k[:, p0, :]
                    count.did(nc.scalar.activation(e, bank[0:NS, KV[p0], 0:T], ACT.Exp, bias=f_bias[:, 2:3],
                                                   scale=-1.0))
                    count.sync(act)
                    count.did(nc.scalar.activation(e, e, ACT.Ln, bias=1.0))
                    count.sync(act)
                    count.did(nc.scalar.activation(e, e, ACT.Exp, scale=-1.0))
                    count.sync(act)
                    nc.scalar.activation(e, e, ACT.Exp, scale=f_time[:, 3:4]).then_inc(f_k_ready, 1)
                if live(n, 3):
                    act.wait_ge(f_zT_in_psum, n - 2)
                    await_count(act, f_kv_in_psum, n - 3)
                    nc.scalar.copy(f_zT[:, :, :].rearrange("p t c -> p (t c)"),
                                   bank[:, 2, 0:D]).then_inc(f_zT_ready, 1)
                if live(n, 1):
                    act.wait_ge(f_hT_in_psum, n)
                    await_count(act, f_shift_in_psum, n - 2)
                    src = bank[:, 0, 0:D].rearrange("p (t c) -> p t c", t=KT)
                    half = T // 2
                    nc.scalar.copy(f_hT[:, p1, :, 0:half], src[:, :, half:T]).then_inc(f_hT_ready, 1)
                    nc.scalar.copy(f_hT[:, p1, :, half:T], src[:, :, 0:half]).then_inc(f_hT_ready, 1)

            nc.scalar.preload_act_table_set("natural_log_exp_and_others")
            act.wait_ge(x_ready, done)
            act.wait_ge(f_loaded, 16 * 8)
            gate = f_gate[:, 0, :]
            count.did(nc.scalar.activation(f_time[:, 2:3], f_time[:, 0:1], ACT.Exp))
            count.did(nc.scalar.activation(f_time[:, 3:4], f_time[:, 1:2], ACT.Exp))
            count.did(nc.scalar.activation(gate, gate, ACT.Exp, scale=-1.0))
            count.sync(act)
            count.did(nc.scalar.activation(gate, gate, ACT.Ln, bias=1.0))
            count.sync(act)
            nc.scalar.activation(gate, gate, ACT.Exp, scale=-1.0).then_inc(f_gate_exp, 1)
            act.wait_ge(f_setup, 1)
            pipeline(act, step, 8, 4, 4, count, 3)

        def shift_vector(dve, done, rdone):
            count = dve_chain

            def step(n, u, uses):
                p0, p1 = u % 2, (u - 1) % 2
                if live(n, 3):
                    dve.wait_ge(f_rstd_ready, n - 2)
                    await_count(dve, f_zT_in_psum, n - 3)
                    nc.vector.tensor_scalar(
                        f_z[:, :], f_xs[:, p1, :], f_mom[:, p1, 0:1], f_rstd[:, p1:p1 + 1],
                        ALU.subtract, ALU.mult).then_inc(f_z_ready, 1)
                if live(n, 1):
                    dve.wait_ge(collect_rstd, n)
                    await_count(dve, f_hT_in_psum, n - 2)
                    nc.vector.tensor_scalar(
                        f_h[:, p1, :], x_sb[:, n - 1, :], moments[:, n - 1, 0:1],
                        rstd[:, bass.ds(n - 1, 1)], ALU.subtract, ALU.mult).then_inc(f_h_ready, 1)
                if live(n, 2):
                    dve.wait_ge(f_shift_in_psum, n - 1)
                    await_count(dve, f_z_ready, n - 3)
                    nc.vector.tensor_tensor(f_xs[:, p0, :], bank[:, SHIFTED[p0], 0:D], f_part[:, p0, :],
                                            ALU.add).then_inc(f_xs_ready, 1)
                if live(n, 5):
                    dve.wait_ge(f_out_in_psum, n - 4)
                    nc.vector.tensor_tensor(x_sb[:, n - 5, :], bank[:, 4, 0:D], x_sb[:, n - 5, :],
                                            ALU.add).then_inc(x_ready, 1)
                if live(n, 4):
                    dve.wait_ge(f_k_ready, n - 3)
                    nc.vector.scalar_tensor_tensor(f_wkvx[:, :], bank[0:NS, KV[p0], T:2 * T], f_bias[:, 1:2],
                                                   f_k[:, p0, :], ALU.add, ALU.mult).then_inc(f_wkvx_ready, 1)
                if live(n, 2):
                    dve.wait_ge(f_xs_ready, n - 1)
                    hold(dve)
                    count.did(nc.vector.bn_stats(bn6[:, 2, :], f_xs[:, p0, :]))
                    count.sync(dve)
                    hold(dve)
                    count.did(nc.vector.bn_aggr(f_mom[:, p0, :], bn6[:, 2, :]))
                if live(n, 1):
                    dve.wait_ge(f_h_ready, n)
                    await_count(dve, f_xs_ready, n - 2)
                    count.did(nc.vector.tensor_tensor(f_part[:, p1, :], f_h[:, p1, :], f_gate[:, 1, :],
                                                      ALU.mult))
                if live(n, 4):
                    dve.wait_ge(f_wkvx_ready, n - 3)
                    await_count(dve, f_out_in_psum, n - 5)
                    nc.vector.tensor_tensor_scan(f_state[:, p0, :], f_decay[:, :], f_wkvx[:, :], 0.0,
                                                 ALU.mult, ALU.add).then_inc(f_state_ready, 1)
                if live(n, 2):
                    count.sync(dve)
                    nc.vector.tensor_scalar(f_var[:, p0:p0 + 1], f_mom[:, p0, 1:2], EPS, None,
                                            ALU.add).then_inc(f_var_ready, 1)
                if live(n, 5) and not live(n, 0):
                    dve.wait_ge(x_ready, done + n - 4)
                    stats(dve, count, n - 5)
                if live(n, 0):
                    dve.wait_ge(y_in[u % GB], 16 * TOP0 * uses(0, GB))
                    beside = live(n, 5)
                    for k in range(TOP0):
                        if k:
                            count.sync(dve, but=1 if beside and k <= 2 else 0)
                        ins = nc.vector.scalar_tensor_tensor(x_sb[:, n, :], g_y[:, u % GB, k, :],
                                                             m_w[:, n, k:k + 1], x_sb[:, n, :],
                                                             ALU.mult, ALU.add)
                        if k < TOP0 - 1:
                            count.did(ins)
                        else:
                            ins.then_inc(y_used, 1)
                        if beside and k < 3:
                            if k == 0:
                                dve.wait_ge(x_ready, done + n - 4)
                            else:
                                count.sync(dve, but=1)
                            stats_part(dve, count, n - 5, k)
                    dve.wait_ge(y_used, n + 1)
                    await_count(dve, collect_stats, n)
                    stats(dve, count, n, collect_stats, 1)

            seq = lambda ins: (count.did(ins), count.sync(dve))
            tt, ts = nc.vector.tensor_tensor, nc.vector.tensor_scalar
            dve.wait_ge(f_gate_exp, 1)
            count.did(ts(f_gate[:, 1, :], f_gate[:, 0, :], -1.0, 1.0, ALU.mult, ALU.add))
            for t in range(KT):
                count.did(tt(f_wshift[:, t, :], f_wshift[:, t, :], f_gate[:, 0, :], ALU.mult))
                count.did(ts(f_wkv[:, 1, t, :], f_wkv[:, 0, t, :], f_affine[:, 0, t:t + 1], None, ALU.mult))
            count.did(ts(f_decay[:, :], table("ones", NS), f_time[:, 2:3], None, ALU.mult))
            seq(ts(f_time[:, 3:4], f_time[:, 3:4], -1.0, None, ALU.mult))
            dve.wait_ge(f_pe, 1)
            seq(nc.vector.tensor_copy(f_bias[:, 0:2], bank[0:NS, 3, 0:2]))
            ts(f_bias[:, 2:3], f_bias[:, 0:1], -1.0, None, ALU.mult).then_inc(f_setup, 1)
            pipeline(dve, step, 8, 4, 5, count, 3 + 2 + TOP0 - 1 + 2,
                     between=lambda i: i == 0 and cross_vector(dve, 1, 4 * NB, 3 * NB, 0))

        def shift_gpsimd(pool, done, rdone):
            def gather(n, k):
                if n >= NB:
                    return
                if k == 0:
                    await_count(pool, y_used, n - GB + 1)
                pool.indirect_dma_start(
                    out=g_y[:, n % GB, k, :], out_offset=None, in_=y_dram,
                    in_offset=bass.IndirectOffsetOnAxis(ap=m_slot[:, n, k:k + 1], axis=0),
                    bounds_check=SLOTS, oob_is_err=False).then_inc(y_in[n % GB], 16)

            for p in range(2):
                pool.wait_ge(y_stored[p], 16 * (EX0 // 2))
            pool.wait_ge(slots_zero, 16 * 6)
            for n in range(2):
                for k in range(TOP0):
                    gather(n, k)
            for n in range(NB + 5):
                gather(n + 2, 0)
                if live(n, 2):
                    p0 = n % 2
                    pool.wait_ge(f_var_ready, n - 1)
                    await_count(pool, f_z_ready, n - 3)
                    nc.gpsimd.tensor_tensor(f_rstd[:, p0:p0 + 1], f_var[:, p0:p0 + 1], minus_half[:, 0:1],
                                            ALU.pow).then_inc(f_rstd_ready, 1)
                gather(n + 2, 1)
                if live(n, 5):
                    pool_rstd(pool, n - 5, rdone)
                gather(n + 2, 2)
                gather(n + 2, 3)
                if live(n, 0):
                    pool_rstd(pool, n, 0, collect_stats, collect_rstd)
                if n == NB:
                    cross_gpsimd(pool, 1, 4 * NB, 3 * NB, 0)

        def pair_experts(i):
            return range(2 * i, min(2 * i + 2, EXS))

        def mlp_tensor(pe, done):
            def turned(n, u, i):
                idx, par = PAIRS * n + i, (u + i) % 2
                pe.wait_ge(l_hid_ready, idx + 1)
                await_count(pe, l_hidT_ready, idx - 1)
                for e in pair_experts(i):
                    mm = nc.tensor.transpose(bank[:, 4 + par, (e % 2) * T:(e % 2 + 1) * T],
                                             l_hid[:, par, (e % 2) * I1:(e % 2 + 1) * I1], ident)
                mm.then_inc(l_hidT_in_psum, 1)

            def step(n, u, uses):
                for i in range(PAIRS):
                    if live(n, 2):
                        idx, par = PAIRS * (n - 2) + i, (u + i) % 2
                        await_count(pe, l_hid_ready, idx - 1)
                        w = 2 * I1 * len(pair_experts(i))
                        for t in range(KT):
                            mm = nc.tensor.matmul(
                                bank[:, 2 + par, 0:w], l_hT[:, (u - 2) % HBUF, t, :],
                                wgu[:, 2 * i:2 * i + len(pair_experts(i)), t, :], start=(t == 0),
                                stop=(t == KT - 1))
                        mm.then_inc(l_gu_in_psum, 1)
                    if live(n, 3):
                        pe.wait_ge(l_hidT_ready, PAIRS * (n - 3) + min(i, PAIRS - 2) + 1)
                        if i == 0:
                            await_count(pe, x_ready, done + n - 4)
                        if i == PAIRS - 1:
                            pe.wait_ge(l_hidT_ready, PAIRS * (n - 2))
                        for e in pair_experts(i):
                            mm = nc.tensor.matmul(bank[:, 6 + (u - 3) % 2, 0:D], l_hidT[:, (u - 3) % 2, e, :],
                                                  wdn[:, e, :], start=(e == 0), stop=(e == EXS - 1))
                        if i == PAIRS - 1:
                            mm.then_inc(l_out_in_psum, 1)
                    if i == 0 and live(n, 3):
                        turned(n - 3, u - 3, PAIRS - 1)
                    if i > 0 and live(n, 2):
                        turned(n - 2, u - 2, i - 1)
                    if i == 1 and live(n, 0):
                        pe.wait_ge(l_h_ready, n + 1)
                        await_count(pe, l_hT_ready, n)
                        for t in range(KT):
                            mm = nc.tensor.transpose(bank[:, 0, t * T:(t + 1) * T],
                                                     l_h[:, u % 2, t * 128:(t + 1) * 128], ident)
                        mm.then_inc(l_hT_in_psum, 1)
                    if i == 3 and live(n, 0):
                        pe.wait_ge(l_hT_ready, n + 1)
                        await_count(pe, l_prob_ready, n)
                        for t in range(KT):
                            mm = nc.tensor.matmul(bank[:, 1, 0:EX1], l_hT[:, u % HBUF, t, :], l_wr[:, t, :],
                                                  start=(t == 0), stop=(t == KT - 1))
                        mm.then_inc(l_logit_in_psum, 1)

            pe.wait_ge(x_ready, done)
            pe.wait_ge(l_loaded, 16 * 6)
            pipeline(pe, step, 4, 4, 3)

        def mlp_scalar(act, done):
            def copy_hidden(act, n, u, i):
                act.wait_ge(l_hidT_in_psum, PAIRS * n + i + 1)
                if i == 0:
                    await_count(act, l_out_in_psum, n - 1)
                k = len(pair_experts(i))
                nc.scalar.copy(l_hidT[:, u % 2, 2 * i:2 * i + k, :].rearrange("p e c -> p (e c)"),
                               bank[:, 4 + (u + i) % 2, 0:k * T]).then_inc(l_hidT_ready, 1)

            def step(n, u, uses):
                for i in range(PAIRS):
                    if live(n, 2):
                        idx, par = PAIRS * (n - 2) + i, (u + i) % 2
                        act.wait_ge(l_gu_in_psum, idx + 1)
                        if i == 0:
                            act.wait_ge(l_p_ready, n - 1)
                        await_count(act, l_hid_ready, idx - 1)
                        for e in pair_experts(i):
                            c = (e % 2) * I1
                            nc.scalar.activation(l_sig[:, par, c:c + I1], bank[:, 2 + par, 2 * c:2 * c + I1],
                                                 ACT.Sigmoid, scale=l_p[:, u % 2, e:e + 1]
                                                 ).then_inc(l_sig_ready, 1)
                    if i == 0 and live(n, 3):
                        copy_hidden(act, n - 3, u - 3, PAIRS - 1)
                    if i > 0 and live(n, 2):
                        copy_hidden(act, n - 2, u - 2, i - 1)
                    if i == 1 and live(n, 0):
                        act.wait_ge(l_hT_in_psum, n + 1)
                        await_count(act, l_gu_in_psum, PAIRS * (n - HBUF + 1))
                        nc.scalar.copy(l_hT[:, u % HBUF].rearrange("p t c -> p (t c)"),
                                       bank[:, 0, 0:D]).then_inc(l_hT_ready, 1)
                    if i == PAIRS - 1 and live(n, 0):
                        act.wait_ge(l_logit_in_psum, n + 1)
                        await_count(act, l_index_ready, n)
                        nc.scalar.copy(l_logit[:, :], bank[:, 1, 0:EX1]).then_inc(l_logit_ready, 1)
                        await_count(act, l_top_ready, n)
                        nc.scalar.activation(l_prob[:, :], bank[:, 1, 0:EX1],
                                             ACT.Sigmoid).then_inc(l_prob_ready, 1)

            nc.scalar.preload_act_table(ACT.Sigmoid)
            pipeline(act, step, 4, 4, 3)

        def mlp_vector(dve, done, rdone):
            count = dve_chain

            def step(n, u, uses):
                if live(n, 0):
                    dve.wait_ge(rstd_ready, rdone + n + 1)
                    await_count(dve, l_hT_in_psum, n - 1)
                    nc.vector.tensor_scalar(
                        l_h[:, u % 2, :], x_sb[:, n, :], moments[:, n, 0:1],
                        rstd[:, bass.ds(n, 1)], ALU.subtract, ALU.mult).then_inc(l_h_ready, 1)
                if live(n, 1):
                    dve.wait_ge(l_logit_ready, n)
                    await_count(dve, l_pick_ready, n - 1)
                    hold(dve)
                    count.did(nc.vector.max(l_top[:, :], l_logit[:, :]))
                for i in range(PAIRS):
                    if live(n, 2):
                        idx, par = PAIRS * (n - 2) + i, (u + i) % 2
                        dve.wait_ge(l_sig_ready, EXS * (n - 2) + 2 * i + len(pair_experts(i)))
                        await_count(dve, l_hidT_in_psum, idx - 1)
                        for e in pair_experts(i):
                            c = (e % 2) * I1
                            count.did(nc.vector.scalar_tensor_tensor(
                                l_sig[:, par, c:c + I1], bank[:, 2 + par, 2 * c:2 * c + I1],
                                l_p[:, u % 2, e:e + 1], l_sig[:, par, c:c + I1], ALU.mult, ALU.mult))
                        count.sync(dve)
                        for e in pair_experts(i):
                            c = (e % 2) * I1
                            ins = nc.vector.scalar_tensor_tensor(
                                l_hid[:, par, c:c + I1], bank[:, 2 + par, 2 * c + I1:2 * c + 2 * I1],
                                l_p[:, u % 2, e:e + 1], l_sig[:, par, c:c + I1], ALU.mult, ALU.mult)
                            if e == pair_experts(i)[-1]:
                                ins.then_inc(l_hid_ready, 1)
                            else:
                                count.did(ins)
                    if i == 0 and live(n, 1):
                        if not live(n, 2):
                            count.sync(dve)
                        hold(dve)
                        nc.vector.max_index(l_topi[:, :], l_top[:, :], l_logit[:, :]
                                            ).then_inc(l_index_ready, 1)
                    if i == 1 and live(n, 1):
                        dve.wait_ge(l_index_ready, n)
                        await_count(dve, l_top_ready, n - 1)
                        nc.vector.tensor_copy(l_pick[:, :], l_topi[:, 0:TOP1]).then_inc(l_pick_ready, 1)
                    if i == 2 and live(n, 1):
                        dve.wait_ge(l_pick_ready, n)
                        dve.wait_ge(l_prob_ready, n)
                        await_count(dve, l_p_ready, n - 1)
                        for k in range(TOP1):
                            ins = nc.vector.scalar_tensor_tensor(
                                l_mask[:, k, :], table("iota32")[:, 0:EX1], l_pick[:, k:k + 1], l_prob[:, :],
                                ALU.is_equal, ALU.mult)
                            if k < TOP1 - 1:
                                count.did(ins)
                        ins.then_inc(l_top_ready, 1)
                    if i == 1 and live(n, 4):
                        dve.wait_ge(l_out_in_psum, n - 3)
                        nc.vector.tensor_tensor(x_sb[:, n - 4, :], bank[:, 6 + u % 2, 0:D],
                                                x_sb[:, n - 4, :], ALU.add).then_inc(x_ready, 1)

            count.did(nc.vector.memset(l_p[:, :, EX1:EXS], 1.0))
            count.sync(dve)
            pipeline(dve, step, 4, 4, 4, count, EXS + PAIRS - 1 + 2)

        def mlp_gpsimd(pool):
            def step(n, u, uses):
                if live(n, 1):
                    pool.wait_ge(l_top_ready, n)
                    await_count(pool, l_hid_ready, PAIRS * (n - 2))
                    nc.gpsimd.tensor_tensor(l_p[:, (u - 1) % 2, 0:EX1], l_mask[:, 0, :], l_mask[:, 1, :],
                                            ALU.add).then_inc(l_p_ready, 1)

            pipeline(pool, step, 4, 4, 1)

        def load_x(sp, q):
            sp.dma_start(x_sb[:, 4 * q:4 * q + 4, :],
                         A["x"][4 * q:4 * q + 4].rearrange("b t d -> t b d")).then_inc(x_loaded[q], 16)

        def load_mlp_inputs(pool, n):
            if n == 0:
                pool.wait_ge(x_ready, NB)
                for t, name in ((m_wr, "routerT"), (m_wgu, "shared_guT"), (m_wdn, "shared_downT")):
                    pool.dma_start(t[:, :, :], A[name].rearrange("(t p) o -> p t o", p=128)
                                   ).then_inc(m_w_loaded, 16)
                pool.dma_start(m_bias[:, :], A["e_bias"].to_broadcast([128, EX0])).then_inc(m_w_loaded, 16)
                nc.gpsimd.memset(g_y[:, :, :, :], 0.0).then_inc(y_zero, 1)
            elif n == 1:
                pool.wait_ge(y_zero, 1)
                pool.dma_start(y_dram[SLOTS:SLOTS + 1, :], g_y[0:1, 0, 0, :]).then_inc(slots_zero, 16)
                for i in range(5):
                    pool.dma_start(xp_dram[bass.ds(i * 512, 512), :].rearrange("(p r) d -> p (r d)", p=128),
                                   g_y[:, i % GB].rearrange("p k d -> p (k d)")).then_inc(slots_zero, 16)
            elif n == 2:
                for t, name in ((f_wshift[:, :, :], "shiftT"), (f_wkv[:, 0], "kvT")):
                    pool.dma_start(t, A[name].rearrange("(t p) o -> p t o", p=128)).then_inc(f_loaded, 16)
                pool.dma_start(f_wo[:, :], A["outT"]).then_inc(f_loaded, 16)
                pool.dma_start(f_gate[:, 0, :], A["gate"].to_broadcast([128, D])).then_inc(f_loaded, 16)
            elif n == 3:
                for i, name in enumerate(("ln_gamma", "ln_beta")):
                    pool.dma_start(f_affine[:, i, :], A[name]).then_inc(f_loaded, 16)
                for i, name in enumerate(("time_decay", "time_first")):
                    pool.dma_start(f_time[:, i:i + 1], A[name]).then_inc(f_loaded, 16)

        @block.tensor
        def _(pe):
            attn_tensor(pe)
            cross_tensor(pe, 0, NB, NB)
            shared_tensor(pe, 2 * NB)
            expert_tensor(pe)
            shift_tensor(pe, 3 * NB)
            cross_tensor(pe, 1, 4 * NB, 3 * NB)
            mlp_tensor(pe, 5 * NB)

        @block.scalar
        def _(act):
            attn_scalar(act)
            cross_scalar(act, 0, NB, NB)
            shared_scalar(act, 2 * NB)
            expert_scalar(act)
            shift_scalar(act, 3 * NB)
            cross_scalar(act, 1, 4 * NB, 3 * NB)
            mlp_scalar(act, 5 * NB)

        @block.vector
        def _(dve):
            attn_vector(dve)
            cross_vector(dve, 0, NB, NB)
            shared_vector(dve, 2 * NB)
            expert_vector(dve)
            shift_vector(dve, 3 * NB, 3 * NB)
            cross_vector(dve, 1, 4 * NB, 3 * NB)
            mlp_vector(dve, 5 * NB, 4 * NB)

        @block.gpsimd
        def _(pool):
            nc.gpsimd.memset(minus_half[:, :], -0.5).then_inc(const_ready, 1)
            nc.gpsimd.memset(zero_eps[:, 0:1], 0.0).then_inc(const_ready, 1)
            nc.gpsimd.memset(zero_eps[:, 1:2], EPS).then_inc(const_ready, 1)
            pool.wait_ge(const_ready, 3)
            attn_gpsimd(pool)
            nc.gpsimd.memset(a_vp[:, :, :], 0.0).then_inc(pad_ready, 1)
            nc.gpsimd.memset(c_vT[:, :, :, :, :], 0.0).then_inc(pad_ready, 1)
            pool.wait_ge(pad_ready, 2)
            nc.gpsimd.memset(k_stack[NSTACK:NSTACK + 3, :, :, :], 1.0).then_inc(pad_ready, 1)
            pool.wait_ge(pad_ready, 3)
            for b in range(NB):
                pool_rstd(pool, b, NB)
                if b in EARLY_AFTER:
                    cross_gpsimd(pool, 0, NB, NB, EARLY_AFTER.index(b))
            cross_gpsimd(pool, 0, NB, NB)
            dispatch_gpsimd(pool)
            shift_gpsimd(pool, 3 * NB, 3 * NB)
            cross_gpsimd(pool, 1, 4 * NB, 3 * NB)
            mlp_gpsimd(pool)

        @block.sync
        def _(sp):
            sp.dma_start(const[:, :], A["const"]).then_inc(const_loaded, 16)
            load_x(sp, 0)
            for t, name in ((wqk[:, :, 0:D], "wqT"), (wqk[:, :, D:2 * D], "wkT"), (wv[:, :, :], "wvT"),
                            (wo[:, :, :], "woT")):
                sp.dma_start(t, A[name].rearrange("(t p) o -> p t o", p=128)).then_inc(w_loaded, 16)
            sp.dma_start(bern[:, 0, :], A["bern_u"].to_broadcast([NK0, H0])).then_inc(w_loaded, 16)
            for q in range(1, 4):
                load_x(sp, q)
            cross_sync(sp, 0, NB, NB)
            for e in range(RING):
                load_expert(sp, e, e)
            expert_sync(sp)
            sp.wait_ge(d_y_in_psum, EX0)
            sp.dma_start(l_wr[:, :, :], A["router1"].rearrange("(t p) o -> p t o", p=128)
                         ).then_inc(l_loaded, 16)
            for t in range(KT):
                sp.dma_start(wgu[:, 0:EX1, t, :],
                             A["gate_up"][:, t * 128:(t + 1) * 128, :].rearrange("e p i -> p e i")
                             ).then_inc(l_loaded, 16)
            sp.dma_start(wgu[:, EX1], A["shared1_gu"].rearrange("(t p) i -> p t i", p=128)
                         ).then_inc(l_loaded, 16)
            sp.dma_start(wdn[:, 0:EX1, :], A["down"].rearrange("e p o -> p e o")).then_inc(l_loaded, 16)
            sp.dma_start(wdn[:, EX1, :], A["shared1_down"]).then_inc(l_loaded, 16)
            cross_sync(sp, 1, 4 * NB, 3 * NB)
            for q in range(NB // 2):
                sp.wait_ge(x_ready, 5 * NB + 2 * q + 2)
                sp.dma_start(out[2 * q:2 * q + 2].rearrange("b t d -> t b d"),
                             x_sb[:, 2 * q:2 * q + 2, :]).then_inc(out_stored, 16)
            sp.wait_ge(out_stored, 16 * (NB // 2))


def kernel(**inputs):
    import numpy as np
    import concourse.bacc as bacc
    from concourse import mybir as mb
    from concourse.bass_utils import run_bass_kernel_spmd

    laid = layout(inputs)
    nc = bacc.Bacc("TRN2", target_bir_lowering=False, num_devices=1)
    arrays, A = {}, {}
    for name, a in laid.items():
        a = np.ascontiguousarray(a)
        arrays[f"in_{name}"] = a
        A[name] = nc.dram_tensor(f"in_{name}", a.shape, mb.dt.from_np(a.dtype), kind="ExternalInput").ap()
    out = nc.dram_tensor("out_0", (NB, T, D), F32, kind="ExternalOutput").ap()
    decoder_kernel(nc, A, out)
    r = run_bass_kernel_spmd(nc, [arrays], core_ids=[0])
    return r.results[0]["out_0"]


def layout(inputs):
    import numpy as np

    i = {k: np.asarray(v) for k, v in inputs.items()}
    return {
        "x": i["x"], "context": i["ctx_2048"], "contextT": i["ctx_2048"].transpose(0, 2, 1), "const": constants(),
        "wqT": i["L0_attn_wq"].T, "wkT": i["L0_attn_wk"].T, "wvT": i["L0_attn_wv"].T,
        "routerT": i["L0_ffn_router_w"].T, "e_bias": i["L0_ffn_e_bias"][None],
        "shared_guT": np.concatenate([i["L0_ffn_shared_gate"].T, i["L0_ffn_shared_up"].T], axis=1),
        "shared_downT": i["L0_ffn_shared_down"].T,
        "W_gu": np.concatenate([i["L0_ffn_W_gate"], i["L0_ffn_W_up"]], axis=2),
        "W_down": i["L0_ffn_W_down"],
        "shiftT": i["L1_attn_W_shift"].T,
        "kvT": np.concatenate([i["L1_attn_W_key"].T, i["L1_attn_W_value"].T], axis=1),
        "outT": i["L1_attn_W_output"].T, "gate": i["L1_attn_gate"][None],
        "ln_gamma": i["L1_attn_ln_gamma"].reshape(KT, 128).T,
        "ln_beta": i["L1_attn_ln_beta"].reshape(KT, 128).T,
        "time_decay": i["L1_attn_time_decay"][:, None], "time_first": i["L1_attn_time_first"][:, None],
        "router1": i["L1_ffn_router_w"], "gate_up": i["L1_ffn_gate_up_w"], "down": i["L1_ffn_down_w"],
        "shared1_gu": np.concatenate([i["L1_ffn_shared_gate_w"], i["L1_ffn_shared_up_w"]], axis=1),
        "shared1_down": i["L1_ffn_shared_down_w"],
        "woT": i["L0_attn_wo"].T, "bern_u": i["L0_attn_bern_u"],
    }
```
